# Optimizing a Trainium2 kernel written in Bass

```python
import numpy as np
import jax
import jax.numpy as jnp

def _softmax(x, axis=-1):
    return jax.nn.softmax(x, axis=axis)

def _gelu(x):
    return jax.nn.gelu(x, approximate=True)

def _silu(x):
    return jax.nn.silu(x)

def _sigmoid(x):
    return jax.nn.sigmoid(x)

def _layernorm(x, axis=-1, eps=1e-05):
    m = jnp.mean(x, axis=axis, keepdims=True)
    v = jnp.var(x, axis=axis, keepdims=True)
    return (x - m) / jnp.sqrt(v + eps)

def _scatter_add(tgt, idx, src, axis=0):
    return tgt.at[idx].add(src)

def _segment_sum(src, seg, n):
    return jax.ops.segment_sum(src, seg, n)
kernel_name = 'mk_decoder_postln_d1_seqx_r4_80d229'

def setup_inputs(seed: int=0):
    np.random.seed(seed)
    _w = jnp.asarray

    def _rec_inputs():
        import jax
        import jax.numpy as jnp
        _rk = jax.random.key(seed)
        x = -0.0002928 + 1 * jax.random.normal(jax.random.fold_in(_rk, 1), (8, 512, 256), jnp.float32)
        _lenS = 512 - jax.random.randint(jax.random.fold_in(_rk, 7), (8,), 0, max(1, 512 // 4) + 1, jnp.int32)
        _lenS2 = 1601 - jax.random.randint(jax.random.fold_in(_rk, 8), (8,), 0, max(1, 1601 // 4) + 1, jnp.int32)
        _ctx_1024P = jax.random.normal(jax.random.fold_in(_rk, 11), (8, 16, 256), jnp.float32)
        _ctx_1024c = jax.random.dirichlet(jax.random.fold_in(_rk, 511), 0.3 * jnp.ones((16,), jnp.float32), (8, 1601))
        _ctx_1024t = jnp.einsum('bsk,bkd->bsd', _ctx_1024c, _ctx_1024P)
        _ctx_1024t = _ctx_1024t * jax.lax.rsqrt(jnp.mean(jnp.square(_ctx_1024t)) + 1e-12) * 0.953939
        ctx_1024 = -1.39393e-06 + 0.999914 * (_ctx_1024t + 0.3 * jax.random.normal(jax.random.fold_in(_rk, 611), (8, 1601, 256), jnp.float32))
        return (x, ctx_1024)
    x, ctx_1024 = _rec_inputs()

    def _L0_attn_setup():
        import jax, jax.numpy as jnp
        import numpy as np
        import math
        B, L, D, MAXL = (4, 1024, 256, 4096)

        def _shift1(a):
            return jnp.concatenate([jnp.zeros_like(a[:, :1]), a[:, :-1]], axis=1)
        key = jax.random.key(seed)
        ks = jax.random.split(key, 12)
        s = 0.02

        def w(k, shape):
            return jax.random.normal(k, shape, jnp.float32) * s
        return {'x': jax.random.normal(ks[0], (B, L, D), jnp.float32), 'pos_phases': jax.random.normal(ks[1], (MAXL, D), jnp.float32) * math.pi, 'Wpv': w(ks[2], (D, D)), 'bpv': jnp.zeros((D,), jnp.float32), 'Wk': w(ks[3], (D, D)), 'bk': jnp.zeros((D,), jnp.float32), 'Wkv': w(ks[4], (D, D)), 'bkv': jnp.zeros((D,), jnp.float32), 'Wg1': w(ks[5], (2 * D, D)), 'bg1': jnp.zeros((D,), jnp.float32), 'Wg2': w(ks[6], (D, 1)), 'bg2': jnp.zeros((1,), jnp.float32), 'Wb1': w(ks[7], (D, D // 2)), 'bb1': jnp.zeros((D // 2,), jnp.float32), 'Wb2': w(ks[8], (D // 2, 2)), 'bb2': jnp.zeros((2,), jnp.float32), 'ln_g': jnp.ones((D,), jnp.float32), 'ln_b': jnp.zeros((D,), jnp.float32), 'Wo': w(ks[9], (D, D)), 'bo': jnp.zeros((D,), jnp.float32)}
    _L0_attn_all = _L0_attn_setup()
    _L0_attn_in = {k: v for k, v in _L0_attn_all.items() if k in ('pos_phases', 'Wpv', 'bpv', 'Wk', 'bk', 'Wkv', 'bkv', 'Wg1', 'bg1', 'Wg2', 'bg2', 'Wb1', 'bb1', 'Wb2', 'bb2', 'ln_g', 'ln_b', 'Wo', 'bo')}
    del _L0_attn_all

    def _L0_xattn_setup():
        import jax, jax.numpy as jnp
        import numpy as np
        import math
        D_MODEL = 256
        N_HEADS = 16
        D_HEAD = D_MODEL // N_HEADS
        key = jax.random.key(seed)
        ks = jax.random.split(key, 11)
        N, L, S = (2, 512, 512)
        inp = {'queries': jax.random.normal(ks[0], (N, L, D_MODEL), dtype=jnp.float32), 'keys': jax.random.normal(ks[1], (N, S, D_MODEL), dtype=jnp.float32), 'values': jax.random.normal(ks[2], (N, S, D_MODEL), dtype=jnp.float32), 'Wq': jax.random.normal(ks[3], (D_MODEL, N_HEADS * D_HEAD), dtype=jnp.float32) / math.sqrt(D_MODEL), 'bq': jnp.zeros((N_HEADS * D_HEAD,), dtype=jnp.float32), 'Wk': jax.random.normal(ks[4], (D_MODEL, N_HEADS * D_HEAD), dtype=jnp.float32) / math.sqrt(D_MODEL), 'bk': jnp.zeros((N_HEADS * D_HEAD,), dtype=jnp.float32), 'Wv': jax.random.normal(ks[5], (D_MODEL, N_HEADS * D_HEAD), dtype=jnp.float32) / math.sqrt(D_MODEL), 'bv': jnp.zeros((N_HEADS * D_HEAD,), dtype=jnp.float32), 'Wo': jax.random.normal(ks[6], (N_HEADS * D_HEAD, D_MODEL), dtype=jnp.float32) / math.sqrt(N_HEADS * D_HEAD), 'bo': jnp.zeros((D_MODEL,), dtype=jnp.float32)}
        return inp
    _L0_xattn_all = _L0_xattn_setup()
    _L0_xattn_in = {k: v for k, v in _L0_xattn_all.items() if k in ('Wq', 'bq', 'Wk', 'bk', 'Wv', 'bv', 'Wo', 'bo')}
    del _L0_xattn_all

    def _L0_ffn_setup():
        import jax, jax.numpy as jnp
        import numpy as np
        NEG_INF = jnp.float32(-1000000000.0)

        def _router(x, Wr, br, top_k=2):
            logits = jnp.einsum('bsd,de->bse', x, Wr) + br
            _, top_idx = jax.lax.top_k(logits, top_k)
            num_experts = logits.shape[-1]
            mask = jnp.any(top_idx[..., None] == jnp.arange(num_experts), axis=-2)
            sparse_logits = jnp.where(mask, logits, NEG_INF)
            weights = jax.nn.softmax(sparse_logits, axis=-1)
            return (weights, top_idx, mask)
        key = jax.random.key(seed)
        ks = jax.random.split(key, 8)
        B, S, D, E, H = (4, 512, 256, 8, 1024)
        sd = 1.0 / np.sqrt(D)
        sh = 1.0 / np.sqrt(H)
        x = jax.random.normal(ks[0], (B, S, D), dtype=jnp.float32)
        Wr = jax.random.normal(ks[1], (D, E), dtype=jnp.float32) * sd
        br = jnp.zeros((E,), dtype=jnp.float32)
        W1 = jax.random.normal(ks[2], (E, D, H), dtype=jnp.float32) * sd
        b1 = jnp.zeros((E, H), dtype=jnp.float32)
        W2 = jax.random.normal(ks[3], (E, H, D), dtype=jnp.float32) * sh
        b2 = jnp.zeros((E, D), dtype=jnp.float32)
        return {'x': x, 'Wr': Wr, 'br': br, 'W1': W1, 'b1': b1, 'W2': W2, 'b2': b2}
    _L0_ffn_all = _L0_ffn_setup()
    _L0_ffn_in = {k: v for k, v in _L0_ffn_all.items() if k in ('Wr', 'br', 'W1', 'b1', 'W2', 'b2')}
    del _L0_ffn_all
    return {'x': x, 'ctx_1024': ctx_1024, 'L0_attn_pos_phases': _L0_attn_in['pos_phases'], 'L0_attn_Wpv': _L0_attn_in['Wpv'], 'L0_attn_bpv': _L0_attn_in['bpv'], 'L0_attn_Wk': _L0_attn_in['Wk'], 'L0_attn_bk': _L0_attn_in['bk'], 'L0_attn_Wkv': _L0_attn_in['Wkv'], 'L0_attn_bkv': _L0_attn_in['bkv'], 'L0_attn_Wg1': _L0_attn_in['Wg1'], 'L0_attn_bg1': _L0_attn_in['bg1'], 'L0_attn_Wg2': _L0_attn_in['Wg2'], 'L0_attn_bg2': _L0_attn_in['bg2'], 'L0_attn_Wb1': _L0_attn_in['Wb1'], 'L0_attn_bb1': _L0_attn_in['bb1'], 'L0_attn_Wb2': _L0_attn_in['Wb2'], 'L0_attn_bb2': _L0_attn_in['bb2'], 'L0_attn_ln_g': _L0_attn_in['ln_g'], 'L0_attn_ln_b': _L0_attn_in['ln_b'], 'L0_attn_Wo': _L0_attn_in['Wo'], 'L0_attn_bo': _L0_attn_in['bo'], 'L0_xattn_Wq': _L0_xattn_in['Wq'], 'L0_xattn_bq': _L0_xattn_in['bq'], 'L0_xattn_Wk': _L0_xattn_in['Wk'], 'L0_xattn_bk': _L0_xattn_in['bk'], 'L0_xattn_Wv': _L0_xattn_in['Wv'], 'L0_xattn_bv': _L0_xattn_in['bv'], 'L0_xattn_Wo': _L0_xattn_in['Wo'], 'L0_xattn_bo': _L0_xattn_in['bo'], 'L0_ffn_Wr': _L0_ffn_in['Wr'], 'L0_ffn_br': _L0_ffn_in['br'], 'L0_ffn_W1': _L0_ffn_in['W1'], 'L0_ffn_b1': _L0_ffn_in['b1'], 'L0_ffn_W2': _L0_ffn_in['W2'], 'L0_ffn_b2': _L0_ffn_in['b2']}

def reference(x, ctx_1024, L0_attn_pos_phases, L0_attn_Wpv, L0_attn_bpv, L0_attn_Wk, L0_attn_bk, L0_attn_Wkv, L0_attn_bkv, L0_attn_Wg1, L0_attn_bg1, L0_attn_Wg2, L0_attn_bg2, L0_attn_Wb1, L0_attn_bb1, L0_attn_Wb2, L0_attn_bb2, L0_attn_ln_g, L0_attn_ln_b, L0_attn_Wo, L0_attn_bo, L0_xattn_Wq, L0_xattn_bq, L0_xattn_Wk, L0_xattn_bk, L0_xattn_Wv, L0_xattn_bv, L0_xattn_Wo, L0_xattn_bo, L0_ffn_Wr, L0_ffn_br, L0_ffn_W1, L0_ffn_b1, L0_ffn_W2, L0_ffn_b2):
    import jax
    import jax.numpy as jnp

    def _L0_attn_ref(x, pos_phases, Wpv, bpv, Wk, bk, Wkv, bkv, Wg1, bg1, Wg2, bg2, Wb1, bb1, Wb2, bb2, ln_g, ln_b, Wo, bo):
        import jax, jax.numpy as jnp
        import numpy as np
        import math
        B, L, D, MAXL = (4, 1024, 256, 4096)

        def _shift1(a):
            return jnp.concatenate([jnp.zeros_like(a[:, :1]), a[:, :-1]], axis=1)
        Bq, Lq, Dq = x.shape
        sqrtD = jnp.sqrt(jnp.float32(Dq))
        pp = pos_phases[:Lq]
        pos_cos, pos_sin = (jnp.cos(pp), jnp.sin(pp))
        pos_values = x @ Wpv + bpv
        pos_mem_cos = jnp.cumsum(pos_cos * pos_values, axis=1)
        pos_mem_sin = jnp.cumsum(pos_sin * pos_values, axis=1)
        pos_ret = (pos_cos * pos_mem_cos + pos_sin * pos_mem_sin) / sqrtD
        key_ph = jnp.tanh(x @ Wk + bk) * jnp.pi
        key_cos, key_sin = (jnp.cos(key_ph), jnp.sin(key_ph))
        kv_values = x @ Wkv + bkv
        x_shifted = _shift1(x)
        gate_in = jnp.concatenate([x, x_shifted], axis=-1)
        gh = jax.nn.gelu(gate_in @ Wg1 + bg1, approximate=False)
        value_gates = jax.nn.sigmoid(gh @ Wg2 + bg2)
        kc_s = _shift1(key_cos)
        ks_s = _shift1(key_sin)
        kv_mem_cos = jnp.cumsum(kc_s * kv_values * value_gates, axis=1)
        kv_mem_sin = jnp.cumsum(ks_s * kv_values * value_gates, axis=1)
        gate_cumsum = jnp.maximum(jnp.cumsum(value_gates, axis=1), 1.0)
        kv_ret = (key_cos * kv_mem_cos + key_sin * kv_mem_sin) / (jnp.sqrt(gate_cumsum) * sqrtD)
        bh = jax.nn.gelu(x @ Wb1 + bb1, approximate=False)
        bw = jax.nn.softmax(bh @ Wb2 + bb2, axis=-1)
        blended = bw[..., 0:1] * pos_ret + bw[..., 1:2] * kv_ret
        mu = jnp.mean(blended, axis=-1, keepdims=True)
        var = jnp.var(blended, axis=-1, keepdims=True)
        ln = (blended - mu) / jnp.sqrt(var + 1e-05) * ln_g + ln_b
        return x + ln @ Wo + bo

    def _L0_xattn_ref(queries, keys, values, Wq, bq, Wk, bk, Wv, bv, Wo, bo):
        import jax, jax.numpy as jnp
        import numpy as np
        import math
        D_MODEL = 256
        N_HEADS = 16
        D_HEAD = D_MODEL // N_HEADS
        N, L, _ = queries.shape
        S = keys.shape[1]
        H, D = (N_HEADS, D_HEAD)
        q = (queries @ Wq + bq).reshape(N, L, H, D)
        k = (keys @ Wk + bk).reshape(N, S, H, D)
        v = (values @ Wv + bv).reshape(N, S, H, D)
        sm = jnp.einsum('nlhd,nshd->nlhs', q, k) / math.sqrt(D)
        sm = jax.nn.softmax(sm, axis=1)
        attn = jnp.einsum('nlhs,nshd->nlhd', sm, v).reshape(N, L, H * D)
        return attn @ Wo + bo

    def _L0_ffn_ref(x, Wr, br, W1, b1, W2, b2):
        import jax, jax.numpy as jnp
        import numpy as np
        NEG_INF = jnp.float32(-1000000000.0)

        def _router(x, Wr, br, top_k=2):
            logits = jnp.einsum('bsd,de->bse', x, Wr) + br
            _, top_idx = jax.lax.top_k(logits, top_k)
            num_experts = logits.shape[-1]
            mask = jnp.any(top_idx[..., None] == jnp.arange(num_experts), axis=-2)
            sparse_logits = jnp.where(mask, logits, NEG_INF)
            weights = jax.nn.softmax(sparse_logits, axis=-1)
            return (weights, top_idx, mask)
        weights, top_idx, mask = _router(x, Wr, br, top_k=2)
        num_experts = W1.shape[0]
        out = jnp.zeros_like(x)
        for e in range(num_experts):
            h = jax.nn.relu(jnp.einsum('bsd,dh->bsh', x, W1[e]) + b1[e])
            y = jnp.einsum('bsh,hd->bsd', h, W2[e]) + b2[e]
            w = weights[:, :, e] * mask[:, :, e].astype(x.dtype)
            out = out + y * w[:, :, None]
        return out
    x = _layernorm(x + _L0_attn_ref(x, L0_attn_pos_phases, L0_attn_Wpv, L0_attn_bpv, L0_attn_Wk, L0_attn_bk, L0_attn_Wkv, L0_attn_bkv, L0_attn_Wg1, L0_attn_bg1, L0_attn_Wg2, L0_attn_bg2, L0_attn_Wb1, L0_attn_bb1, L0_attn_Wb2, L0_attn_bb2, L0_attn_ln_g, L0_attn_ln_b, L0_attn_Wo, L0_attn_bo), axis=-1)
    x = _layernorm(x + _L0_xattn_ref(x, ctx_1024, ctx_1024, L0_xattn_Wq, L0_xattn_bq, L0_xattn_Wk, L0_xattn_bk, L0_xattn_Wv, L0_xattn_bv, L0_xattn_Wo, L0_xattn_bo), axis=-1)
    x = _layernorm(x + _L0_ffn_ref(x, L0_ffn_Wr, L0_ffn_br, L0_ffn_W1, L0_ffn_b1, L0_ffn_W2, L0_ffn_b2), axis=-1)
    return x

_drawn_inputs = setup_inputs


def setup_inputs(seed=0):
    import zlib

    import numpy as np

    out = dict(_drawn_inputs(seed))
    spreads = {'L0_attn_bpv': (0.0, 0.1),
     'L0_attn_bk': (0.0, 0.625),
     'L0_attn_bkv': (0.0, 0.1),
     'L0_attn_bg1': (0.0, 0.8),
     'L0_attn_bb1': (0.0, 0.8),
     'L0_attn_bb2': (0.0, 0.473),
     'L0_attn_ln_g': (1.0, 0.2),
     'L0_attn_ln_b': (0.0, 0.1),
     'L0_attn_bo': (0.0, 0.1),
     'L0_xattn_bq': (0.0, 0.8),
     'L0_xattn_bk': (0.0, 0.1),
     'L0_xattn_bv': (0.0, 0.1),
     'L0_xattn_bo': (0.0, 0.1),
     'L0_ffn_br': (0.0, 0.1),
     'L0_ffn_b1': (0.0, 0.1),
     'L0_ffn_b2': (0.0, 0.1)}
    factors = {'L0_attn_Wg1': 8.0, 'L0_attn_Wg2': 8.0, 'L0_attn_Wb1': 8.0, 'L0_attn_Wb2': 5.955}
    for name, (base, spread) in spreads.items():
        noise = np.random.default_rng([zlib.crc32(name.encode()), seed]).standard_normal(out[name].shape)
        drawn = base * np.exp(spread * noise) if base else spread * noise
        out[name] = jnp.asarray(drawn.astype(out[name].dtype))
    for name, factor in factors.items():
        out[name] = (out[name] * factor).astype(out[name].dtype)
    return out
```

```python
import math
from contextlib import ExitStack

import concourse.bass as bass
from concourse import mybir

P = 128
F32 = mybir.dt.float32
BF16 = mybir.dt.bfloat16
U32 = mybir.dt.uint32
ALU = mybir.AluOpType
ACT = mybir.ActivationFunctionType
AX_X = mybir.AxisListType.X


class Steps:

    def __init__(self, before):
        self.before, self.n = before, 0

    def next(self):
        self.n += 1
        return self.before + self.n


def last_user(k, buffers, per_round):
    if k >= buffers:
        return 0, k - buffers
    return -1, max(p for p in range(per_round) if p % buffers == k)


def decoder_layer(nc, a, out):
    B, L, D = a["x"].shape
    S = a["ctxT"].shape[-1]
    S_REAL = a["S_REAL"]
    H = 16
    DH = D // H
    C = D // P
    TT = L // P
    E = a["W1"].shape[0]
    HID = a["W1"].shape[-1]
    HC = HID // P
    GH = 4
    G = H // GH
    NG = B * G
    ST = S // P
    TAIL = S_REAL - (ST - 1) * P
    KC = S // 4
    PARTS = 3
    Q_SLOTS = (0, 0, 1, 1, 0, 2)
    K_SLOTS = (0, 1, 0, 1, 2, 0)
    STACK = DH * len(Q_SLOTS)
    PAD = 32
    TWO_PI = 2 * math.pi
    TWO_PI_HI = 6.28125
    ROUND = 1.5 * 2.0 ** 23
    PI_DOWN = 3.1415925
    EPS = 1e-5
    SCALE = 1.0 / math.sqrt(DH)
    ROOT_D = math.sqrt(D)
    assert C == 2 and TT == 4 and B % 2 == 0 and G == 4 and E == 8

    q_parts = nc.dram_tensor("q_parts", [PARTS, B, D, L], BF16, kind="Internal").ap()
    k_parts = nc.dram_tensor("k_parts", [PARTS, B, D, S], BF16, kind="Internal").ap()
    v_all = nc.dram_tensor("v_all", [B, G, P, ST * GH * DH], F32, kind="Internal").ap()
    attn_all = nc.dram_tensor("attn_all", [NG, P, L], F32, kind="Internal").ap()
    x1_all = nc.dram_tensor("x1_all", [B, L, D], F32, kind="Internal").ap()

    with ExitStack() as top:
        def sem(name):
            return top.enter_context(nc.semaphore(name))

        def tensors(ctx):
            def sb(name, shape, dt=F32):
                return ctx.enter_context(nc.sbuf_tensor(name, shape, dt))
            return sb

        psum = top.enter_context(nc.psum_tensor("psum", [P, 8, 512], F32))

        sb = tensors(top)
        ident = sb("ident", [P, P])
        mean_w = sb("mean_w", [P, P])
        eps_col = sb("eps_col", [P, 1])
        half_pi = sb("half_pi", [P, 1])
        cols = sb("cols", [P, a["cols"].shape[-1]])
        rows = sb("rows", [P, 4, D])
        iota8 = sb("iota8", [P, E])
        router_w = sb("router_w", [P, C, E])
        router_b = sb("router_b", [P, E])
        b1_cols = sb("b1_cols", [P, E, HC])
        b2_rows = sb("b2_rows", [E, D])

        def col(i):
            return cols[:, i:i + 1]

        BPV, BK, BKV, BG1, LNG, LNB, BQ, XBK = (2 * i for i in range(8))
        BB1, BG2, BW_A, BW_B, WG2, WB2 = 16, 17, 18, 19, 20, 22
        BO, XBO, XBV, _ = range(4)

        consts_loaded = sem("consts_loaded")
        N_CONSTS = 0
        consts_made = sem("consts_made")
        ident_zeroed = sem("ident_zeroed")
        derived_ready = sem("derived_ready")

        def wait_alone(eng, *waits):
            for _, n in waits:
                eng.to_reg(n)
            eng.wait_ge(consts_made, 1)
            for s, n in waits:
                eng.wait_ge(s, n)

        with ExitStack() as ctx:
            sb = tensors(ctx)
            wpv, wk, wkv, wo, wq = (sb(n, [P, C, D]) for n in ("wpv", "wk", "wkv", "wo", "wq"))
            wg1 = sb("wg1", [P, 2 * C, D])
            wb1 = sb("wb1", [P, C, P])
            wg2_wide = sb("wg2_wide", [P, C, P])
            wb2_wide = sb("wb2_wide", [P, P])
            mcols = sb("mcols", [P, 4])
            pos = sb("pos", [P, C, L])
            turns = sb("turns", [P, C, L])
            pos_cos = sb("pos_cos", [P, C, L])
            pos_sin = sb("pos_sin", [P, C, L])
            xt = sb("xt", [P, 2, C, L + 1])
            xin = sb("xin", [P, 2, TT, D])
            x2bo = sb("x2bo", [P, TT, D])
            phase = sb("phase", [P, C, L])
            phase_abs = sb("phase_abs", [P, C, L])
            key_cos = sb("key_cos", [P, C, L + 1])
            key_sin = sb("key_sin", [P, C, L + 1])
            gate_h = sb("gate_h", [P, C, L])
            blend_h = sb("blend_h", [P, L])
            gate_t = sb("gate_t", [P, L])
            gate = sb("gate", [P, L])
            gate_sum = sb("gate_sum", [P, L])
            gate_ln = sb("gate_ln", [P, L])
            gate_rs = sb("gate_rs", [P, L])
            below_max = sb("below_max", [P, 2, L])
            bexp = sb("bexp", [P, 2, L])
            bsum = sb("bsum", [P, L])
            bsum_ln = sb("bsum_ln", [P, L])
            bsum_r = sb("bsum_r", [P, L])
            bw = sb("bw", [P, 2, L])
            kv_w = sb("kv_w", [P, L])
            mem_c = sb("mem_c", [P, C, L])
            mem_s = sb("mem_s", [P, C, L])
            pos_ret = sb("pos_ret", [P, C, L])
            kvg = sb("kvg", [P, C, L])
            blended = sb("blended", [P, C, L])
            centred = sb("centred", [P, C, L])
            squares = sb("squares", [P, C, L])
            var_ln = sb("var_ln", [P, L])
            rstd_b = sb("rstd_b", [P, L])
            normed = sb("normed", [P, C, L])
            ln_t = sb("ln_t", [P, C, L])
            y = sb("y", [P, TT, D])
            stats = sb("stats", [P, TT, 6])
            moments = sb("moments", [P, TT, 2])
            rstd_ln = sb("rstd_ln", [P, TT])
            rstd = sb("rstd", [P, TT])
            x1 = sb("x1", [P, TT, D])
            x1t = sb("x1t", [P, C, L])
            q_f = sb("q_f", [P, C, L])
            q_rest = sb("q_rest", [P, C, L])
            q_out = sb("q_out", [P, PARTS, C, L], BF16)

            (xt_loaded0, xt_loaded1, pos_ready, trig_ready, pv_ready, kz_ready, gh_ready, bh_ready,
             gate_z_ready, kv_ready, bw_z_ready, mean_ready, var_ready, mix_out_ready, x1t_ready,
             q_ready) = (sem(n) for n in (
                 "xt_loaded0", "xt_loaded1", "pos_ready", "trig_ready", "pv_ready", "kz_ready",
                 "gh_ready", "bh_ready", "gate_z_ready", "kv_ready", "bw_z_ready", "mean_ready",
                 "var_ready", "mix_out_ready", "x1t_ready", "q_ready"))
            xt_loaded = (xt_loaded0, xt_loaded1)
            (phase_ready, gate_h_ready, blend_h_ready, gate_t_ready, key_trig_ready, act_abs, bexp_ready,
             bsum_r_ready, gate_rs_ready, act_ln, squares_ready, rstd_b_ready, ln_ready, rstd_ready,
             x1t_copied, q_copied) = (sem(n) for n in (
                 "phase_ready", "gate_h_ready", "blend_h_ready", "gate_t_ready", "key_trig_ready",
                 "act_abs", "bexp_ready", "bsum_r_ready", "gate_rs_ready", "act_ln",
                 "squares_ready", "rstd_b_ready", "ln_ready", "rstd_ready", "x1t_copied", "q_copied"))
            (dve_pos, dve_mix, pv_used, below_max_ready, gate_sum_ready, bsum_ready, kv_used,
             blended_ready, centred_ready, normed_ready, moments_ready, x1_ready) = (
                 sem(n) for n in ("dve_pos", "dve_mix", "pv_used", "below_max_ready",
                                  "gate_sum_ready", "bsum_ready", "kv_used", "blended_ready",
                                  "centred_ready", "normed_ready", "moments_ready", "x1_ready"))
            x_bo_ready = sem("x_bo_ready")
            x2bo_ready, pool_split, q_split, q_stored, x1_stored, y_ready = (
                sem(n) for n in ("x2bo_ready", "pool_split", "q_split", "q_stored", "x1_stored", "y_ready"))

            consts = [
                (cols[:], a["cols"]),
                (rows[:], a["rows"].rearrange("(o n) d -> o n d", o=1).to_broadcast([P, 4, D])),
                (router_w[:], a["Wr"].rearrange("(c p) e -> p c e", p=P)),
                (router_b[:], a["br"].rearrange("(o e) -> o e", o=1).to_broadcast([P, E])),
                (b1_cols[:], a["b1T"]),
                (b2_rows[:], a["b2"]),
                (wg1[:], a["Wg1"].rearrange("(c p) d -> p c d", p=P)),
                (wb1[:], a["Wb1"].rearrange("(c p) d -> p c d", p=P)),
                (pos[:], a["posT"].rearrange("(c p) l -> p c l", p=P)),
            ] + [(t[:], a[n].rearrange("(c p) d -> p c d", p=P)) for t, n in (
                (wpv, "Wpv"), (wk, "Wk"), (wkv, "Wkv"), (wo, "Wo"), (wq, "xWq"))]
            N_CONSTS = 16 * len(consts)

            DVE_MIX_STEPS = 34
            with nc.Block() as block:
                @block.sync
                def _(sp):
                    for tile, src in consts:
                        sp.dma_start(tile, src).then_inc(consts_loaded, 16)
                    with sp.Fori(0, B // 2) as it:
                        for h in range(2):
                            b = 2 * it + h
                            sp.wait_ge(y_ready, b)
                            for c in range(C):
                                sp.dma_start(xt[:, h, c, 1:L + 1], a["xT"][b, c]).then_inc(xt_loaded[h], 16)
                            sp.dma_start(xin[:, h], a["x"][b].rearrange("(t p) d -> p t d", p=P)) \
                                .then_inc(xt_loaded[h], 16)

                @block.gpsimd
                def _(pool):
                    pool.memset(ident[:], 0.0).then_inc(ident_zeroed, 1)
                    pool.memset(mean_w[:], 1.0 / D)
                    pool.memset(eps_col[:], EPS)
                    pool.memset(half_pi[:], math.pi / 2)
                    pool.memset(xt[:, :, :, 0:1], 0.0)
                    pool.memset(key_cos[:, :, 0:1], 0.0)
                    pool.memset(key_sin[:, :, 0:1], 0.0)
                    for e in range(E):
                        pool.memset(iota8[:, e:e + 1], float(e))
                    pool.wait_ge(ident_zeroed, 1)
                    pool.affine_select(out=ident[:], in_=ident[:], compare_op=ALU.not_equal, fill=1.0, base=0,
                                       pattern=[[-1, P]], channel_multiplier=1).then_inc(consts_made, 1)
                    pool.wait_ge(consts_loaded, N_CONSTS)
                    with pool.Fori(0, B // 2) as it:
                        for h in range(2):
                            b = 2 * it + h
                            wait_alone(pool, (y_ready, b + 1), (xt_loaded[h], 48 * (it + 1)))
                            pool.tensor_tensor(x2bo[:], xin[:, h], rows[:, BO:BO + 1, :].to_broadcast([P, TT, D]),
                                               ALU.add).then_inc(x_bo_ready, 1)
                            pool.wait_ge(x_bo_ready, b + 1)
                            pool.tensor_tensor(x2bo[:], x2bo[:], xin[:, h], ALU.add).then_inc(x2bo_ready, 1)
                            wait_alone(pool, (x1_ready, b + 1))
                            pool.dma_start(x1_all[b].rearrange("(t p) d -> p t d", p=P), x1[:]) \
                                .then_inc(x1_stored, 16)
                            wait_alone(pool, (q_stored, 16 * PARTS * b), (q_copied, b + 1))
                            pool.tensor_scalar(q_out[:, 0], q_f[:], 1.0, None, ALU.mult).then_inc(pool_split, 1)
                            pool.wait_ge(pool_split, 3 * b + 1)
                            pool.tensor_tensor(q_rest[:], q_f[:], q_out[:, 0], ALU.subtract).then_inc(pool_split, 1)
                            wait_alone(pool, (pool_split, 3 * b + 2))
                            pool.tensor_scalar(q_out[:, 1], q_rest[:], 1.0, None, ALU.mult).then_inc(pool_split, 1)
                            pool.wait_ge(pool_split, 3 * b + 3)
                            pool.tensor_tensor(q_out[:, 2], q_rest[:], q_out[:, 1], ALU.subtract).then_inc(q_split, 1)
                            wait_alone(pool, (q_split, b + 1))
                            for part in range(PARTS):
                                pool.dma_start(q_parts[part, b].rearrange("(c p) l -> p c l", p=P),
                                               q_out[:, part]).then_inc(q_stored, 16)
                    pool.wait_ge(q_stored, 16 * PARTS * B)
                    pool.wait_ge(x1_stored, 16 * B)

                @block.tensor
                def _(pe):
                    def project(bank, weights, rhs, chunks):
                        for co in range(C):
                            for k in range(chunks):
                                last = pe.matmul(psum[:, bank + co, :], weights[:, k, co * P:(co + 1) * P],
                                                 rhs(k), start=k == 0, stop=k == chunks - 1)
                        return last

                    pe.wait_ge(consts_loaded, N_CONSTS)
                    pe.wait_ge(consts_made, 1)
                    pe.wait_ge(derived_ready, 1)
                    with pe.Fori(0, B // 2) as it:
                        for h in range(2):
                            b = 2 * it + h
                            now = lambda k: xt[:, h, k % C, 1 - k // C:L + 1 - k // C]
                            pe.wait_ge(xt_loaded[h], 48 * (it + 1))
                            pe.wait_ge(rstd_b_ready, b)
                            project(2, wk, now, C).then_inc(kz_ready, 1)
                            pe.wait_ge(q_copied, b)
                            project(4, wg1, now, 2 * C).then_inc(gh_ready, 1)
                            pe.wait_ge(x1t_copied, b)
                            for k in range(C):
                                last = pe.matmul(psum[:, 6, :], wb1[:, k, :], now(k), start=k == 0, stop=k == C - 1)
                            last.then_inc(bh_ready, 1)
                            pe.wait_ge(y_ready, b + 1)
                            project(0, wpv, now, C).then_inc(pv_ready, 1)
                            pe.wait_ge(gate_h_ready, b + 1)
                            for k in range(C):
                                last = pe.matmul(psum[:, 7, :], wg2_wide[:, k, :], gate_h[:, k, :],
                                                 start=k == 0, stop=k == C - 1)
                            last.then_inc(gate_z_ready, 1)
                            project(4, wkv, now, C).then_inc(kv_ready, 1)
                            pe.wait_ge(blend_h_ready, b + 1)
                            pe.matmul(psum[:, 6, :], wb2_wide[:], blend_h[:], start=True, stop=True) \
                                .then_inc(bw_z_ready, 1)
                            pe.wait_ge(phase_ready, b + 1)
                            pe.wait_ge(blended_ready, b + 1)
                            for k in range(C):
                                last = pe.matmul(psum[:, 2, :], mean_w[:], blended[:, k, :], start=k == 0, stop=k == C - 1)
                            last.then_inc(mean_ready, 1)
                            pe.wait_ge(squares_ready, b + 1)
                            for k in range(C):
                                last = pe.matmul(psum[:, 3, :], mean_w[:], squares[:, k, :], start=k == 0, stop=k == C - 1)
                            last.then_inc(var_ready, 1)
                            pe.wait_ge(pv_used, b + 1)
                            pe.wait_ge(ln_ready, b + 1)
                            for t in range(TT):
                                for k in range(C):
                                    last = pe.matmul(psum[:, t // 2, (t % 2) * D:(t % 2 + 1) * D],
                                                     ln_t[:, k, t * P:(t + 1) * P], wo[:, k, :],
                                                     start=k == 0, stop=k == C - 1)
                            last.then_inc(mix_out_ready, 1)
                            pe.wait_ge(gate_t_ready, b + 1)
                            pe.wait_ge(below_max_ready, b + 1)
                            pe.wait_ge(x1_ready, b + 1)
                            for k in range(C):
                                for t in range(TT):
                                    last = pe.transpose(psum[:, 6 + k, t * P:(t + 1) * P],
                                                        x1[:, t, k * P:(k + 1) * P], ident[:])
                            last.then_inc(x1t_ready, 1)
                            pe.wait_ge(kv_used, b + 1)
                            pe.wait_ge(x1t_copied, b + 1)
                            project(4, wq, lambda k: x1t[:, k, :], C).then_inc(q_ready, 1)

                @block.scalar
                def _(act):
                    act.wait_ge(consts_loaded, N_CONSTS)
                    act.wait_ge(consts_made, 1)
                    act.wait_ge(pos_ready, 1)
                    act.activation(pos_sin[:], pos[:], ACT.Sin)
                    act.activation(pos_cos[:], turns[:], ACT.Sin, bias=half_pi[:], scale=-1.0).then_inc(trig_ready, 1)
                    with act.Fori(0, B // 2) as it:
                        for h in range(2):
                            b = 2 * it + h
                            for c in range(C):
                                act.wait_ge(kz_ready, b + 1)
                                last = act.activation(phase[:, c], psum[:, 2 + c], ACT.Tanh, bias=col(BK + c))
                            last.then_inc(phase_ready, 1)
                            for c in range(C):
                                act.wait_ge(gh_ready, b + 1)
                                act.wait_ge(gate_z_ready, b)
                                last = act.activation(gate_h[:, c], psum[:, 4 + c], ACT.Gelu, bias=col(BG1 + c))
                            last.then_inc(gate_h_ready, 1)
                            act.wait_ge(bw_z_ready, b)
                            act.wait_ge(bh_ready, b + 1)
                            act.activation(blend_h[:], psum[:, 6], ACT.Gelu, bias=col(BB1)).then_inc(blend_h_ready, 1)
                            act.wait_ge(gate_z_ready, b + 1)
                            act.activation(gate_t[:], psum[:, 7], ACT.Tanh, bias=mcols[:, 0:1], scale=0.5) \
                                .then_inc(gate_t_ready, 1)
                            act.wait_ge(phase_ready, b + 1)
                            act.activation(phase_abs[:], phase[:], ACT.Abs).then_inc(act_abs, 1)
                            act.wait_ge(blended_ready, b)
                            act.activation(key_sin[:, :, 1:L + 1], phase[:], ACT.Sin, scale=PI_DOWN)
                            act.wait_ge(act_abs, b + 1)
                            act.activation(key_cos[:, :, 1:L + 1], phase_abs[:], ACT.Sin, bias=half_pi[:],
                                           scale=-PI_DOWN).then_inc(key_trig_ready, 1)
                            act.wait_ge(below_max_ready, b + 1)
                            act.activation(bexp[:, 0], below_max[:, 0], ACT.Exp)
                            act.activation(bexp[:, 1], below_max[:, 1], ACT.Exp, scale=-1.0).then_inc(bexp_ready, 1)
                            act.wait_ge(gate_sum_ready, b + 1)
                            act.activation(gate_ln[:], gate_sum[:], ACT.Ln).then_inc(act_ln, 1)
                            act.wait_ge(act_ln, 4 * b + 1)
                            act.activation(gate_rs[:], gate_ln[:], ACT.Exp, scale=-0.5).then_inc(gate_rs_ready, 1)
                            act.wait_ge(bsum_ready, b + 1)
                            act.activation(bsum_ln[:], bsum[:], ACT.Ln).then_inc(act_ln, 1)
                            act.wait_ge(act_ln, 4 * b + 2)
                            act.activation(bsum_r[:], bsum_ln[:], ACT.Exp, scale=-1.0).then_inc(bsum_r_ready, 1)
                            act.wait_ge(centred_ready, b + 1)
                            act.activation(squares[:], centred[:], ACT.Square).then_inc(squares_ready, 1)
                            act.wait_ge(var_ready, b + 1)
                            act.activation(var_ln[:], psum[:, 3], ACT.Ln, bias=eps_col[:]).then_inc(act_ln, 1)
                            act.wait_ge(act_ln, 4 * b + 3)
                            act.activation(rstd_b[:], var_ln[:], ACT.Exp, scale=-0.5).then_inc(rstd_b_ready, 1)
                            act.wait_ge(normed_ready, b + 1)
                            act.wait_ge(mix_out_ready, b)
                            for c in range(C):
                                last = act.activation(ln_t[:, c], normed[:, c], ACT.Identity, bias=col(LNB + c),
                                                      scale=col(LNG + c))
                            last.then_inc(ln_ready, 1)
                            act.wait_ge(moments_ready, b + 1)
                            act.activation(rstd_ln[:], moments[:, :, 1], ACT.Ln, bias=eps_col[:]).then_inc(act_ln, 1)
                            act.wait_ge(act_ln, 4 * b + 4)
                            act.activation(rstd[:], rstd_ln[:], ACT.Exp, scale=-0.5).then_inc(rstd_ready, 1)
                            act.wait_ge(q_ready, b)
                            act.wait_ge(x1t_ready, b + 1)
                            act.activation(x1t[:], psum[:, 6:8], ACT.Copy).then_inc(x1t_copied, 1)
                            act.wait_ge(q_split, b)
                            act.wait_ge(q_ready, b + 1)
                            for c in range(C):
                                last = act.activation(q_f[:, c], psum[:, 4 + c], ACT.Identity, bias=col(BQ + c))
                            last.then_inc(q_copied, 1)

                @block.vector
                def _(v):
                    v.wait_ge(consts_loaded, N_CONSTS)
                    v.tensor_tensor(mcols[:, 1:2], col(WB2), col(WB2 + 1), ALU.subtract).then_inc(dve_pos, 1)
                    v.tensor_tensor(mcols[:, 2:3], col(BW_A), col(BW_B), ALU.subtract)
                    v.tensor_scalar(mcols[:, 0:1], col(BG2), 0.5, None, ALU.mult)
                    for k in range(C):
                        v.tensor_copy(wg2_wide[:, k, :], col(WG2 + k).to_broadcast([P, P]))
                    v.wait_ge(dve_pos, 1)
                    v.tensor_copy(wb2_wide[:], mcols[:, 1:2].to_broadcast([P, P])).then_inc(derived_ready, 1)
                    v.tensor_scalar(turns[:], pos[:], 1.0 / TWO_PI, ROUND, ALU.mult, ALU.add).then_inc(dve_pos, 1)
                    v.wait_ge(dve_pos, 2)
                    v.tensor_scalar(turns[:], turns[:], -ROUND, None, ALU.add).then_inc(dve_pos, 1)
                    v.wait_ge(dve_pos, 3)
                    v.scalar_tensor_tensor(pos[:], turns[:], -TWO_PI_HI, pos[:], ALU.mult, ALU.add).then_inc(dve_pos, 1)
                    v.wait_ge(dve_pos, 4)
                    v.scalar_tensor_tensor(pos[:], turns[:], TWO_PI_HI - TWO_PI, pos[:], ALU.mult, ALU.add) \
                        .then_inc(dve_pos, 1)
                    v.wait_ge(dve_pos, 5)
                    v.tensor_scalar(pos[:], pos[:], -PI_DOWN, PI_DOWN, ALU.max, ALU.min).then_inc(dve_pos, 1)
                    v.wait_ge(dve_pos, 6)
                    v.scalar_tensor_tensor(turns[:], pos[:], -1.0, pos[:], ALU.mult, ALU.max).then_inc(pos_ready, 1)
                    v.wait_ge(trig_ready, 1)
                    v.sem_inc(y_ready, 1)
                    with v.Fori(0, B // 2) as it:
                        for h in range(2):
                            b = 2 * it + h
                            step = Steps(DVE_MIX_STEPS * b)
                            v.wait_ge(pv_ready, b + 1)
                            for c in range(C):
                                v.scalar_tensor_tensor(mem_c[:, c], psum[:, c], col(BPV + c), pos_cos[:, c], ALU.add,
                                                       ALU.mult).then_inc(dve_mix, 1)
                                step.next()
                            for c in range(C):
                                last = v.scalar_tensor_tensor(mem_s[:, c], psum[:, c], col(BPV + c), pos_sin[:, c],
                                                              ALU.add, ALU.mult)
                                last.then_inc(pv_used if c else dve_mix, 1)
                            s0 = step.next()
                            v.wait_ge(dve_mix, s0)
                            v.wait_ge(pv_used, b + 1)

                            def scan(mem):
                                for c in range(C):
                                    v.tensor_tensor_scan(mem[:, c], mem[:, c], mem[:, c], 0.0, ALU.add, ALU.bypass) \
                                        .then_inc(dve_mix, 1)
                                    s = step.next()
                                return s

                            def times(out_t, in0, in1, op=ALU.mult):
                                v.tensor_tensor(out_t, in0, in1, op).then_inc(dve_mix, 1)
                                return step.next()

                            scan(mem_c)
                            s = scan(mem_s)
                            v.wait_ge(dve_mix, s - 2)
                            times(mem_c[:], mem_c[:], pos_cos[:])
                            v.wait_ge(dve_mix, s)
                            s = times(mem_s[:], mem_s[:], pos_sin[:])
                            v.wait_ge(dve_mix, s)
                            times(pos_ret[:], mem_c[:], mem_s[:], ALU.add)
                            v.wait_ge(gate_t_ready, b + 1)
                            v.tensor_scalar(gate[:], gate_t[:], 0.5, 0.5, ALU.mult, ALU.add).then_inc(dve_mix, 1)
                            s = step.next()
                            v.wait_ge(dve_mix, s)
                            v.tensor_tensor_scan(gate_sum[:], gate[:], gate[:], 0.0, ALU.add, ALU.bypass).then_inc(dve_mix, 1)
                            s = step.next()
                            v.wait_ge(dve_mix, s)
                            v.wait_ge(gate_rs_ready, b)
                            v.tensor_scalar(gate_sum[:], gate_sum[:], 1.0, None, ALU.max).then_inc(gate_sum_ready, 1)
                            v.wait_ge(bexp_ready, b)
                            v.wait_ge(bw_z_ready, b + 1)
                            v.tensor_scalar(below_max[:, 0], psum[:, 6], mcols[:, 2:3], 0.0, ALU.add, ALU.min)
                            v.tensor_scalar(below_max[:, 1], psum[:, 6], mcols[:, 2:3], 0.0, ALU.add, ALU.max) \
                                .then_inc(below_max_ready, 1)
                            v.wait_ge(kv_ready, b + 1)
                            for c in range(C):
                                v.scalar_tensor_tensor(kvg[:, c], psum[:, 4 + c], col(BKV + c), gate[:], ALU.add,
                                                       ALU.mult).then_inc(kv_used if c else dve_mix, 1)
                            s = step.next()
                            v.wait_ge(dve_mix, s)
                            v.wait_ge(kv_used, b + 1)
                            v.wait_ge(key_trig_ready, b + 1)
                            times(mem_c[:], kvg[:], key_cos[:, :, 0:L])
                            s = times(mem_s[:], kvg[:], key_sin[:, :, 0:L])
                            v.wait_ge(dve_mix, s - 1)
                            scan(mem_c)
                            v.wait_ge(dve_mix, s)
                            s = scan(mem_s)
                            v.wait_ge(dve_mix, s - 2)
                            times(mem_c[:], mem_c[:], key_cos[:, :, 1:L + 1])
                            v.wait_ge(dve_mix, s)
                            s = times(mem_s[:], mem_s[:], key_sin[:, :, 1:L + 1])
                            v.wait_ge(dve_mix, s)
                            s_kv = times(mem_c[:], mem_c[:], mem_s[:], ALU.add)
                            v.wait_ge(bexp_ready, b + 1)
                            v.wait_ge(bsum_r_ready, b)
                            v.tensor_tensor(bsum[:], bexp[:, 0], bexp[:, 1], ALU.add).then_inc(bsum_ready, 1)
                            v.wait_ge(bsum_r_ready, b + 1)
                            v.wait_ge(gate_rs_ready, b + 1)
                            for i in range(2):
                                v.scalar_tensor_tensor(bw[:, i], bexp[:, i], 1.0 / ROOT_D, bsum_r[:], ALU.mult, ALU.mult) \
                                    .then_inc(dve_mix, 1)
                                s = step.next()
                            v.wait_ge(dve_mix, s)
                            s = times(kv_w[:], bw[:, 1], gate_rs[:])
                            for c in range(C):
                                times(pos_ret[:, c], pos_ret[:, c], bw[:, 0])
                            v.wait_ge(dve_mix, s)
                            for c in range(C):
                                s = times(mem_c[:, c], mem_c[:, c], kv_w[:])
                            v.wait_ge(dve_mix, s)
                            v.wait_ge(mean_ready, b)
                            v.tensor_tensor(blended[:], pos_ret[:], mem_c[:], ALU.add).then_inc(blended_ready, 1)
                            v.wait_ge(blended_ready, b + 1)
                            v.wait_ge(squares_ready, b)
                            for c in range(C):
                                v.wait_ge(mean_ready, b + 1)
                                last = v.tensor_tensor(centred[:, c], blended[:, c], psum[:, 2], ALU.subtract)
                                last.then_inc(centred_ready if c else dve_mix, 1)
                            s = step.next()
                            v.wait_ge(dve_mix, s)
                            v.wait_ge(centred_ready, b + 1)
                            v.wait_ge(ln_ready, b)
                            v.wait_ge(rstd_b_ready, b + 1)
                            for c in range(C):
                                last = v.tensor_tensor(normed[:, c], centred[:, c], rstd_b[:], ALU.mult)
                            last.then_inc(normed_ready, 1)
                            v.wait_ge(x2bo_ready, b + 1)
                            v.wait_ge(mix_out_ready, b + 1)
                            v.tensor_tensor(y[:].rearrange("p t d -> p (t d)").rearrange("p (n f) -> p n f", n=2),
                                            psum[:, 0:2],
                                            x2bo[:].rearrange("p t d -> p (t d)").rearrange("p (n f) -> p n f", n=2),
                                            ALU.add).then_inc(y_ready, 1)
                            v.wait_ge(y_ready, b + 2)
                            for t in range(TT):
                                last = v.bn_stats(stats[:, t], y[:, t])
                                last.then_inc(dve_mix, 1)
                                s = step.next()
                            wait_alone(v, (dve_mix, s))
                            for t in range(TT):
                                last = v.bn_aggr(moments[:, t], stats[:, t])
                            last.then_inc(moments_ready, 1)
                            v.wait_ge(x1_stored, 16 * b)
                            v.wait_ge(x1t_ready, b)
                            v.wait_ge(moments_ready, b + 1)
                            v.wait_ge(rstd_ready, b + 1)
                            for t in range(TT):
                                last = v.tensor_scalar(x1[:, t], y[:, t], moments[:, t, 0:1], rstd[:, t:t + 1],
                                                       ALU.subtract, ALU.mult)
                            last.then_inc(x1_ready, 1)
                            assert step.n == DVE_MIX_STEPS, step.n

        with ExitStack() as ctx:
            sb = tensors(ctx)
            xwk, xwv = sb("xwk", [P, C, D]), sb("xwv", [P, C, D])
            ct = sb("ct", [P, 2, C, S])
            neg_bk = sb("neg_bk", [P, C])
            k_f = sb("k_f", [P, 2, KC])
            k_rest = sb("k_rest", [P, 2, KC])
            k_out = sb("k_out", [P, 2, PARTS, KC], BF16)
            v_out = sb("v_out", [P, 2, G, ST, GH * DH])
            xw_loaded, neg_bk_ready, kp_ready, k_copied, k_hi, k_mid, k_rest_ready, k_split = (
                sem(n) for n in ("xw_loaded", "neg_bk_ready", "kp_ready", "k_copied", "k_hi", "k_mid",
                                 "k_rest_ready", "k_split"))
            ct_loaded = (sem("ct_loaded0"), sem("ct_loaded1"))
            k_stored = (sem("k_stored0"), sem("k_stored1"))
            v_stored = (sem("v_stored0"), sem("v_stored1"))
            vp_ready, v_copied = sem("vp_ready"), sem("v_copied")
            KJ = 4 * C
            VJ = (ST + 1) // 2

            with nc.Block() as block:
                @block.sync
                def _(sp):
                    sp.dma_start(xwk[:], a["xWk"].rearrange("(c p) d -> p c d", p=P)).then_inc(xw_loaded, 16)
                    sp.dma_start(xwv[:], a["xWv"].rearrange("(c p) d -> p c d", p=P)).then_inc(xw_loaded, 16)
                    with sp.Fori(0, B // 2) as it:
                        for h in range(2):
                            sp.wait_ge(v_copied, VJ * (2 * it + h))
                            sp.dma_start(ct[:, h], a["ctxT"][2 * it + h].rearrange("c p s -> p c s")) \
                                .then_inc(ct_loaded[h], 16)

                @block.tensor
                def _(pe):
                    pe.wait_ge(xw_loaded, 32)
                    with pe.Fori(0, B // 2) as it:
                        for h in range(2):
                            b = 2 * it + h
                            pe.wait_ge(ct_loaded[h], 16 * (it + 1))
                            for j in range(KJ):
                                co, s0 = j // 4, (j % 4) * KC
                                if j >= 4:
                                    pe.wait_ge(k_copied, KJ * b + j - 3)
                                for k in range(C):
                                    last = pe.matmul(psum[:, j % 4, 0:KC], xwk[:, k, co * P:(co + 1) * P],
                                                     ct[:, h, k, s0:s0 + KC], start=k == 0, stop=k == C - 1)
                                last.then_inc(kp_ready, 1)
                            for j in range(VJ):
                                if j >= 4:
                                    pe.wait_ge(v_copied, VJ * (b + 1) + j - 3)
                                for t in range(2 * j, min(2 * j + 2, ST)):
                                    for k in range(C):
                                        last = pe.matmul(psum[:, 4 + j % 4, (t % 2) * D:(t % 2 + 1) * D],
                                                         ct[:, h, k, t * P:(t + 1) * P], xwv[:, k, :],
                                                         start=k == 0, stop=k == C - 1)
                                last.then_inc(vp_ready, 1)
                            pe.wait_ge(k_copied, KJ * (b + 1))
                            pe.wait_ge(v_copied, VJ * (b + 2))

                @block.scalar
                def _(act):
                    act.wait_ge(neg_bk_ready, 1)
                    with act.Fori(0, B // 2) as it:
                        for h in range(2):
                            b = 2 * it + h
                            for j in range(KJ):
                                if j >= 2:
                                    act.wait_ge(k_split, KJ * b + j - 1)
                                else:
                                    act.wait_ge(k_split, KJ * b)
                                act.wait_ge(kp_ready, KJ * b + j + 1)
                                act.activation(k_f[:, j % 2], psum[:, j % 4, 0:KC], ACT.Identity,
                                               bias=neg_bk[:, j // 4:j // 4 + 1], scale=-SCALE).then_inc(k_copied, 1)
                                act.wait_ge(k_stored[j % 2], 16 * (KJ // 2 * b + j // 2))
                                act.wait_ge(k_copied, KJ * b + j + 1)
                                act.activation(k_out[:, j % 2, 0], k_f[:, j % 2], ACT.Copy).then_inc(k_hi, 1)
                                act.wait_ge(k_rest_ready, KJ * b + j + 1)
                                act.activation(k_out[:, j % 2, 1], k_rest[:, j % 2], ACT.Copy).then_inc(k_mid, 1)

                @block.gpsimd
                def _(pool):
                    with pool.Fori(0, B // 2) as it:
                        for h in range(2):
                            b = 2 * it + h
                            for j in range(KJ):
                                pool.wait_ge(k_mid, KJ * b + j + 1)
                                pool.tensor_tensor(k_out[:, j % 2, 2], k_rest[:, j % 2], k_out[:, j % 2, 1],
                                                   ALU.subtract).then_inc(k_split, 1)
                                wait_alone(pool, (k_split, KJ * b + j + 1))
                                co, s0 = j // 4, (j % 4) * KC
                                pool.dma_start(
                                    k_parts[:, b, co * P:(co + 1) * P, s0:s0 + KC].rearrange("n p s -> p n s"),
                                    k_out[:, j % 2]).then_inc(k_stored[j % 2], 16)
                            wait_alone(pool, (v_copied, VJ * (b + 2)))
                            pool.dma_start(v_all[b].rearrange("g p f -> p g f"),
                                           v_out[:, h].rearrange("p g t f -> p g (t f)")).then_inc(v_stored[h], 16)
                    for h in range(2):
                        pool.wait_ge(k_stored[h], 16 * B * KJ // 2)
                        pool.wait_ge(v_stored[h], 16 * B // 2)

                @block.vector
                def _(v):
                    v.tensor_scalar(neg_bk[:], cols[:, XBK:XBK + C], -SCALE, None, ALU.mult).then_inc(neg_bk_ready, 1)
                    v.sem_inc(v_copied, VJ)
                    with v.Fori(0, B // 2) as it:
                        for h in range(2):
                            b = 2 * it + h
                            v.wait_ge(v_stored[h], 16 * it)
                            for j in range(KJ):
                                v.wait_ge(k_hi, KJ * b + j + 1)
                                v.tensor_tensor(k_rest[:, j % 2], k_f[:, j % 2], k_out[:, j % 2, 0], ALU.subtract) \
                                    .then_inc(k_rest_ready, 1)
                            for j in range(VJ):
                                v.wait_ge(vp_ready, VJ * b + j + 1)
                                n = min(2, ST - 2 * j)
                                for i in range(n):
                                    last = v.tensor_tensor(
                                        v_out[:, h, :, 2 * j + i, :],
                                        psum[:, 4 + j % 4, i * D:(i + 1) * D].rearrange("p (g f) -> p g f", g=G),
                                        rows[:, XBV, :].rearrange("p (g f) -> p g f", g=G), ALU.add)
                                last.then_inc(v_copied, 1)

        with ExitStack() as ctx:
            sb = tensors(ctx)
            SUBS = 2 * ST
            SCORE_BUFS, P_BUFS = 3, 4
            N_SUB, N_TILE = 2 * SUBS, 2 * ST
            LAG = 2
            qst = sb("qst", [STACK, 2, GH, L], BF16)
            kst = sb("kst", [STACK, 2, GH, S], BF16)
            vst = sb("vst", [P, 2, ST, GH * DH])
            neg_max = sb("neg_max", [P, SCORE_BUFS, 2])
            probs = sb("probs", [P, P_BUFS, GH, L])
            sums = sb("sums", [P, P_BUFS, GH])
            inv = sb("inv", [P, P_BUFS, GH])
            v_scaled = sb("v_scaled", [P, P_BUFS, GH, PAD])
            attn = sb("attn", [P, 2, L])
            heads_loaded = (sem("heads_loaded0"), sem("heads_loaded1"))
            (pads_zeroed, scores_ready, max_ready, exp_done, inv_ready, v_scaled_ready, pv_done,
             attn_copied) = (sem(n) for n in (
                 "pads_zeroed", "scores_ready", "max_ready", "exp_done", "inv_ready", "v_scaled_ready", "pv_done",
                 "attn_copied"))
            attn_stored = (sem("attn_stored0"), sem("attn_stored1"))
            CREDIT = P_BUFS

            def free(k, bufs, per_round, it):
                round_, p = last_user(k, bufs, per_round)
                return per_round * it + per_round * round_ + p + 1 + CREDIT

            with nc.Block() as block:
                @block.sync
                def _(sp):
                    with sp.Fori(0, NG // 2) as it:
                        for h in range(2):
                            n = 2 * it + h
                            sp.wait_ge(attn_copied, n)
                            for slot in range(len(Q_SLOTS)):
                                at = slice(slot * DH, (slot + 1) * DH)
                                qd = q_parts[Q_SLOTS[slot]].rearrange("b (g j d) l -> (b g) d j l", g=G, j=GH)[n]
                                kd = k_parts[K_SLOTS[slot]].rearrange("b (g j d) s -> (b g) d j s", g=G, j=GH)[n]
                                sp.dma_start(qst[at, h], qd).then_inc(heads_loaded[h], 16)
                                sp.dma_start(kst[at, h], kd).then_inc(heads_loaded[h], 16)
                            sp.dma_start(vst[:, h].rearrange("p t f -> p (t f)"),
                                         v_all.rearrange("b g p f -> (b g) p f")[n]).then_inc(heads_loaded[h], 16)

                LOADS = 16 * (2 * len(Q_SLOTS) + 1)

                def rows_of(t):
                    return P if t < ST - 1 else TAIL

                def copy_group(v, it, h):
                    v.wait_ge(pv_done, N_TILE * it + ST * (h + 1))
                    v.wait_ge(attn_stored[h], 16 * it)
                    v.tensor_copy(attn[:, h], psum[:, 6]).then_inc(attn_copied, 1)

                def store_group(pool, it, h):
                    wait_alone(pool, (attn_copied, 2 * it + h + 2))
                    pool.dma_start(attn_all[2 * it + h], attn[:, h]).then_inc(attn_stored[h], 16)

                @block.tensor
                def _(pe):
                    pe.wait_ge(pads_zeroed, 1)
                    with pe.Fori(0, NG // 2) as it:
                        def pv(tile):
                            h, t = divmod(tile, ST)
                            if t == 0:
                                pe.wait_ge(attn_copied, 2 * it + h + 1)
                            pe.wait_ge(v_scaled_ready, N_TILE * it + tile + 1)
                            r, pb = rows_of(t), tile % P_BUFS
                            for j in range(GH):
                                last = pe.matmul(psum[j * PAD:(j + 1) * PAD, 6, :], v_scaled[0:r, pb, j, :],
                                                 probs[0:r, pb, j, :], start=t == 0, stop=t == ST - 1)
                            last.then_inc(pv_done, 1)

                        for tile in range(N_TILE):
                            h, t = divmod(tile, ST)
                            if t == 0:
                                pe.wait_ge(heads_loaded[h], LOADS * (it + 1))
                            r = rows_of(t)
                            for sub in range(2):
                                k = 2 * tile + sub
                                sbuf = k % SCORE_BUFS
                                pe.wait_ge(exp_done, free(k, SCORE_BUFS, N_SUB, it))
                                for i in range(2):
                                    j = 2 * sub + i
                                    last = pe.matmul(psum[0:r, 2 * sbuf + i, :], kst[:, h, j, t * P:t * P + r],
                                                     qst[:, h, j, :], start=True, stop=True)
                                last.then_inc(scores_ready, 1)
                            if tile >= LAG:
                                pv(tile - LAG)
                        for tile in range(N_TILE - LAG, N_TILE):
                            pv(tile)

                @block.vector
                def _(v):
                    v.memset(v_scaled[:], 0.0).then_inc(pads_zeroed, 1)
                    v.sem_inc(attn_copied, 1)
                    with v.Fori(0, NG // 2) as it:
                        def inverse(tile):
                            v.wait_ge(exp_done, N_SUB * it + 2 * tile + 2 + CREDIT)
                            r = rows_of(tile % ST)
                            v.reciprocal(inv[0:r, tile % P_BUFS], sums[0:r, tile % P_BUFS]).then_inc(inv_ready, 1)

                        for tile in range(N_TILE):
                            h, t = divmod(tile, ST)
                            r = rows_of(t)
                            for sub in range(2):
                                k = 2 * tile + sub
                                sbuf = k % SCORE_BUFS
                                v.wait_ge(scores_ready, N_SUB * it + k + 1)
                                v.tensor_reduce(neg_max[0:r, sbuf], psum[0:r, 2 * sbuf:2 * sbuf + 2], AX_X, ALU.min) \
                                    .then_inc(max_ready, 1)
                            if tile >= 1:
                                inverse(tile - 1)
                            if t == LAG and h == 1:
                                copy_group(v, it, 0)
                        inverse(N_TILE - 1)
                        copy_group(v, it, 1)

                @block.gpsimd
                def _(pool):
                    pool.wait_ge(pads_zeroed, 1)
                    with pool.Fori(0, NG // 2) as it:
                        for tile in range(N_TILE):
                            h, t = divmod(tile, ST)
                            r, pb = rows_of(t), tile % P_BUFS
                            if tile >= P_BUFS:
                                pool.wait_ge(pv_done, N_TILE * it + tile - P_BUFS + 1)
                            pool.wait_ge(inv_ready, N_TILE * it + tile + 1)
                            last = pool.tensor_tensor(
                                v_scaled[0:r, pb, :, 0:DH], vst[0:r, h, t, :].rearrange("p (j d) -> p j d", j=GH),
                                inv[0:r, pb].rearrange("p (j o) -> p j o", o=1).to_broadcast([r, GH, DH]), ALU.mult)
                            last.then_inc(v_scaled_ready, 1)
                            if tile == ST + LAG + 1:
                                store_group(pool, it, 0)
                        store_group(pool, it, 1)
                    for h in range(2):
                        pool.wait_ge(attn_stored[h], 16 * NG // 2)

                @block.scalar
                def _(act):
                    act.wait_ge(pads_zeroed, 1)
                    act.sem_inc(exp_done, CREDIT)
                    with act.Fori(0, NG // 2) as it:
                        for tile in range(N_TILE):
                            h, t = divmod(tile, ST)
                            r, pb = rows_of(t), tile % P_BUFS
                            if tile >= P_BUFS:
                                act.wait_ge(pv_done, N_TILE * it + tile - P_BUFS + 1)
                            elif tile == 0:
                                act.wait_ge(pv_done, N_TILE * it)
                            for sub in range(2):
                                k = 2 * tile + sub
                                sbuf = k % SCORE_BUFS
                                act.wait_ge(max_ready, N_SUB * it + k + 1)
                                for i in range(2):
                                    j = 2 * sub + i
                                    last = act.activation(probs[0:r, pb, j, :], psum[0:r, 2 * sbuf + i, :], ACT.Exp,
                                                          bias=neg_max[0:r, sbuf, i:i + 1], scale=-1.0,
                                                          accum_out=sums[0:r, pb, j:j + 1])
                                last.then_inc(exp_done, 1)

        sb = tensors(top)
        wts_all = sb("wts_all", [P, B * TT, E])
        x2t_all = sb("x2t_all", [P, C, B * L])
        acc_all = sb("acc_all", [P, B * TT, D])

        with ExitStack() as ctx:
            sb = tensors(ctx)
            xwo = sb("xwo", [P, G, D])
            at_in = sb("at_in", [P, 2, G, L])
            x1_in = sb("x1_in", [P, 2, TT, D])
            y2 = sb("y2", [P, TT, D])
            stats2 = sb("stats2", [P, TT, 6])
            moments2 = sb("moments2", [P, TT, 2])
            rstd2_ln = sb("rstd2_ln", [P, TT])
            rstd2 = sb("rstd2", [P, TT])
            x2 = sb("x2", [P, TT, D])
            x2t = sb("x2t", [P, C, L])
            logits = sb("logits", [P, TT, E])
            top8 = sb("top8", [P, TT, E])
            top8_at = sb("top8_at", [P, TT, E], U32)
            chosen = sb("chosen", [P, TT, 2])
            onehot = sb("onehot", [P, 2, TT, E])
            gap = sb("gap", [P, TT])
            egap = sb("egap", [P, TT])
            den = sb("den", [P, TT])
            w01 = sb("w01", [P, 2, TT])
            wts = sb("wts", [P, TT, E])
            wts_t = sb("wts_t", [E, L])
            xwo_loaded = sem("xwo_loaded")
            route_loaded = (sem("route_loaded0"), sem("route_loaded1"))
            (x1bo_ready, proj_ready, y2_ready, dve_route, moments2_ready, act_ln2, rstd2_ready, x2_ready, x2t_ready,
             x2t_copied, x2t_kept, logits_z_ready, logits_ready, gap_ready, egap_ready, wts_ready, wts_t_ready,
             wts_t_copied, b2_ready, acc_ready) = (sem(n) for n in (
                 "x1bo_ready", "proj_ready", "y2_ready", "dve_route", "moments2_ready", "act_ln2", "rstd2_ready",
                 "x2_ready", "x2t_ready", "x2t_copied", "x2t_kept", "logits_z_ready", "logits_ready", "gap_ready",
                 "egap_ready", "wts_ready", "wts_t_ready", "wts_t_copied", "b2_ready", "acc_ready"))
            ROUTE_STEPS = 20

            with nc.Block() as block:
                @block.sync
                def _(sp):
                    sp.dma_start(xwo[:], a["xWo"].rearrange("g p d -> p g d")).then_inc(xwo_loaded, 16)
                    with sp.Fori(0, B // 2) as it:
                        for h in range(2):
                            b = 2 * it + h
                            sp.wait_ge(y2_ready, 2 * it)
                            sp.dma_start(at_in[:, h], attn_all.rearrange("(b g) p l -> b p g l", g=G)[b]) \
                                .then_inc(route_loaded[h], 16)
                            sp.dma_start(x1_in[:, h], x1_all[b].rearrange("(t p) d -> p t d", p=P)) \
                                .then_inc(route_loaded[h], 16)

                @block.gpsimd
                def _(pool):
                    with pool.Fori(0, B // 2) as it:
                        for h in range(2):
                            b = 2 * it + h
                            pool.wait_ge(route_loaded[h], 32 * (it + 1))
                            pool.tensor_tensor(x1_in[:, h], x1_in[:, h],
                                               rows[:, XBO:XBO + 1, :].to_broadcast([P, TT, D]), ALU.add) \
                                .then_inc(x1bo_ready, 1)
                            wait_alone(pool, (x2t_copied, b + 1))
                            pool.tensor_copy(x2t_all[:, :, bass.ds(b * L, L)], x2t[:]).then_inc(x2t_kept, 1)

                @block.tensor
                def _(pe):
                    pe.wait_ge(xwo_loaded, 16)
                    with pe.Fori(0, B // 2) as it:
                        for h in range(2):
                            b = 2 * it + h
                            pe.wait_ge(y2_ready, b)
                            pe.wait_ge(route_loaded[h], 32 * (it + 1))
                            for t in range(TT):
                                for g in range(G):
                                    last = pe.matmul(psum[:, t // 2, (t % 2) * D:(t % 2 + 1) * D],
                                                     at_in[:, h, g, t * P:(t + 1) * P], xwo[:, g, :],
                                                     start=g == 0, stop=g == G - 1)
                            last.then_inc(proj_ready, 1)
                            pe.wait_ge(x2t_copied, b)
                            pe.wait_ge(x2_ready, b + 1)
                            for k in range(C):
                                for t in range(TT):
                                    last = pe.transpose(psum[:, 2 + k, t * P:(t + 1) * P],
                                                        x2[:, t, k * P:(k + 1) * P], ident[:])
                            last.then_inc(x2t_ready, 1)
                            pe.wait_ge(logits_ready, b)
                            pe.wait_ge(x2t_copied, b + 1)
                            for t in range(TT):
                                for k in range(C):
                                    last = pe.matmul(psum[:, 4, t * E:(t + 1) * E], x2t[:, k, t * P:(t + 1) * P],
                                                     router_w[:, k, :], start=k == 0, stop=k == C - 1)
                            last.then_inc(logits_z_ready, 1)
                            pe.wait_ge(wts_t_copied, b)
                            pe.wait_ge(wts_ready, b + 1)
                            for t in range(TT):
                                last = pe.transpose(psum[0:E, 5, t * P:(t + 1) * P], wts[:, t, :], ident[:])
                            last.then_inc(wts_t_ready, 1)
                            pe.wait_ge(acc_ready, b)
                            pe.wait_ge(wts_t_copied, b + 1)
                            for t in range(TT):
                                last = pe.matmul(psum[:, 6 + t // 2, (t % 2) * D:(t % 2 + 1) * D],
                                                 wts_t[:, t * P:(t + 1) * P], b2_rows[:], start=True, stop=True)
                            last.then_inc(b2_ready, 1)

                @block.scalar
                def _(act):
                    with act.Fori(0, B // 2) as it:
                        for h in range(2):
                            b = 2 * it + h
                            act.wait_ge(moments2_ready, b + 1)
                            act.activation(rstd2_ln[:], moments2[:, :, 1], ACT.Ln, bias=eps_col[:]).then_inc(act_ln2, 1)
                            act.wait_ge(act_ln2, b + 1)
                            act.activation(rstd2[:], rstd2_ln[:], ACT.Exp, scale=-0.5).then_inc(rstd2_ready, 1)
                            act.wait_ge(logits_z_ready, b)
                            act.wait_ge(x2t_kept, b)
                            act.wait_ge(x2t_ready, b + 1)
                            act.activation(x2t[:], psum[:, 2:4], ACT.Copy).then_inc(x2t_copied, 1)
                            act.wait_ge(gap_ready, b + 1)
                            act.activation(egap[:], gap[:], ACT.Exp).then_inc(egap_ready, 1)
                            act.wait_ge(b2_ready, b)
                            act.wait_ge(wts_t_ready, b + 1)
                            act.activation(wts_t[:], psum[0:E, 5], ACT.Copy).then_inc(wts_t_copied, 1)

                @block.vector
                def _(v):
                    with v.Fori(0, B // 2) as it:
                        for h in range(2):
                            b = 2 * it + h
                            step = Steps(ROUTE_STEPS * b)

                            def wide(t):
                                return t.rearrange("p t d -> p (t d)").rearrange("p (n f) -> p n f", n=2)

                            v.wait_ge(x1bo_ready, b + 1)
                            v.wait_ge(proj_ready, b + 1)
                            v.tensor_tensor(wide(y2[:]), psum[:, 0:2], wide(x1_in[:, h]), ALU.add).then_inc(y2_ready, 1)
                            v.wait_ge(y2_ready, b + 1)
                            for t in range(TT):
                                v.bn_stats(stats2[:, t], y2[:, t]).then_inc(dve_route, 1)
                                s = step.next()
                            wait_alone(v, (dve_route, s))
                            for t in range(TT):
                                last = v.bn_aggr(moments2[:, t], stats2[:, t])
                            last.then_inc(moments2_ready, 1)
                            v.wait_ge(x2t_ready, b)
                            v.wait_ge(moments2_ready, b + 1)
                            v.wait_ge(rstd2_ready, b + 1)
                            for t in range(TT):
                                last = v.tensor_scalar(x2[:, t], y2[:, t], moments2[:, t, 0:1], rstd2[:, t:t + 1],
                                                       ALU.subtract, ALU.mult)
                            last.then_inc(x2_ready, 1)
                            v.wait_ge(logits_z_ready, b + 1)
                            v.tensor_tensor(logits[:], psum[:, 4, 0:TT * E].rearrange("p (t e) -> p t e", t=TT),
                                            router_b[:].rearrange("p (o e) -> p o e", o=1).to_broadcast([P, TT, E]),
                                            ALU.add).then_inc(logits_ready, 1)
                            wait_alone(v, (logits_ready, b + 1))
                            for t in range(TT):
                                v.max(top8[:, t], logits[:, t]).then_inc(dve_route, 1)
                                s = step.next()
                            wait_alone(v, (dve_route, s))
                            for t in range(TT):
                                v.max_index(top8_at[:, t], top8[:, t], logits[:, t]).then_inc(dve_route, 1)
                                s = step.next()
                            v.tensor_tensor(gap[:], top8[:, :, 1], top8[:, :, 0], ALU.subtract).then_inc(gap_ready, 1)
                            v.wait_ge(dve_route, s)
                            v.tensor_copy(chosen[:], top8_at[:, :, 0:2]).then_inc(dve_route, 1)
                            s = step.next()
                            v.wait_ge(egap_ready, b + 1)
                            v.tensor_scalar(den[:], egap[:], 1.0, None, ALU.add).then_inc(dve_route, 1)
                            s1 = step.next()
                            v.wait_ge(dve_route, s)
                            for i in range(2):
                                v.tensor_tensor(onehot[:, i],
                                                iota8[:].rearrange("p (o e) -> p o e", o=1).to_broadcast([P, TT, E]),
                                                chosen[:, :, i:i + 1].to_broadcast([P, TT, E]), ALU.is_equal) \
                                    .then_inc(dve_route, 1)
                                s2 = step.next()
                            v.wait_ge(dve_route, s1)
                            v.reciprocal(w01[:, 0], den[:]).then_inc(dve_route, 1)
                            s = step.next()
                            v.wait_ge(dve_route, s)
                            v.tensor_tensor(w01[:, 1], w01[:, 0], egap[:], ALU.mult).then_inc(dve_route, 1)
                            s = step.next()
                            v.wait_ge(dve_route, s)
                            for i in range(2):
                                v.tensor_tensor(onehot[:, i], onehot[:, i],
                                                w01[:, i].rearrange("p (t o) -> p t o", o=1).to_broadcast([P, TT, E]),
                                                ALU.mult).then_inc(dve_route, 1)
                                s = step.next()
                            v.wait_ge(dve_route, s)
                            v.tensor_tensor(wts[:], onehot[:, 0], onehot[:, 1], ALU.add).then_inc(wts_ready, 1)
                            v.wait_ge(wts_ready, b + 1)
                            v.tensor_copy(wts_all[:, bass.ds(b * TT, TT), :], wts[:])
                            v.wait_ge(b2_ready, b + 1)
                            v.tensor_tensor(acc_all[:, bass.ds(b * TT, TT), :].rearrange("p t d -> p (t d)").rearrange("p (n f) -> p n f", n=2), psum[:, 6:8], wide(x2[:]), ALU.add) \
                                .then_inc(acc_ready, 1)
                            assert step.n == ROUTE_STEPS, step.n

        with ExitStack() as ctx:
            sb = tensors(ctx)
            w1 = sb("w1", [P, C, HID])
            w2 = sb("w2", [P, HC, D])
            hid = sb("hid", [P, HC, L])
            wcol = sb("wcol", [P, 2, TT])
            b1c = sb("b1c", [P, HC])
            w_loaded, w1_used, hz_ready, h_ready, y_z_ready, y_added, wcol_ready = (sem(n) for n in (
                "w_loaded", "w1_used", "hz_ready", "h_ready", "y_z_ready", "y_added", "wcol_ready"))
            b1c_ready = sem("b1c_ready")
            with nc.Block() as block:
                @block.sync
                def _(sp):
                    with sp.Fori(0, E) as e:
                        sp.wait_ge(y_z_ready, e * (B * TT // 2))
                        sp.dma_start(w1[:], a["W1"][e].rearrange("(c p) h -> p c h", p=P)).then_inc(w_loaded, 16)
                        sp.dma_start(w2[:], a["W2"][e].rearrange("(c p) d -> p c d", p=P)).then_inc(w_loaded, 16)

                @block.tensor
                def _(pe):
                    with pe.Fori(0, E) as e:
                        wait_alone(pe, (w_loaded, 32 * (e + 1)))
                        with pe.Fori(0, B) as b:
                            n = e * B + b
                            for c in range(HC):
                                if c >= 4:
                                    pe.wait_ge(h_ready, n * HC + c - 3)
                                for k in range(C):
                                    last = pe.matmul(psum[:, c % 4, :], w1[:, k, c * P:(c + 1) * P],
                                                     x2t_all[:, k, bass.ds(b * L, L)], start=k == 0, stop=k == C - 1)
                                last.then_inc(hz_ready, 1)
                            pe.wait_ge(h_ready, n * HC + HC)
                            for j in range(TT // 2):
                                pe.wait_ge(y_added, n * (TT // 2) + j - (TT // 2) + 2)
                                for t in (2 * j, 2 * j + 1):
                                    for c in range(HC):
                                        last = pe.matmul(psum[:, 4 + j, (t % 2) * D:(t % 2 + 1) * D],
                                                         hid[:, c, t * P:(t + 1) * P], w2[:, c, :],
                                                         start=c == 0, stop=c == HC - 1)
                                last.then_inc(y_z_ready, 1)

                @block.scalar
                def _(act):
                    with act.Fori(0, E) as e:
                        act.wait_ge(y_z_ready, e * (B * TT // 2))
                        act.activation(b1c[:], b1_cols[:, bass.ds(e, 1), :].rearrange("p o c -> p (o c)"), ACT.Copy) \
                            .then_inc(b1c_ready, 1)
                        with act.Fori(0, B) as b:
                            n = e * B + b
                            act.wait_ge(b1c_ready, e + 1)
                            act.wait_ge(y_z_ready, n * (TT // 2))
                            for c in range(HC):
                                act.wait_ge(hz_ready, n * HC + c + 1)
                                act.activation(hid[:, c], psum[:, c % 4], ACT.Relu, bias=b1c[:, c:c + 1]) \
                                    .then_inc(h_ready, 1)

                @block.gpsimd
                def _(pool):
                    pass

                @block.vector
                def _(v):
                    v.sem_inc(y_added, 1)
                    with v.Fori(0, E) as e:
                        with v.Fori(0, B) as b:
                            n = e * B + b
                            v.wait_ge(y_added, n * (TT // 2) + 1)
                            v.tensor_copy(wcol[:, 0], wts_all[:, bass.ds(b * TT, TT), bass.ds(e, 1)]
                                          .rearrange("p t o -> p (t o)")).then_inc(wcol_ready, 1)
                            v.wait_ge(wcol_ready, n + 1)
                            for j in range(TT // 2):
                                v.wait_ge(y_z_ready, n * (TT // 2) + j + 1)
                                for t in (2 * j, 2 * j + 1):
                                    at = acc_all[:, bass.ds(b * TT + t, 1), :].rearrange("p o d -> p (o d)")
                                    last = v.scalar_tensor_tensor(
                                        at, psum[:, 4 + j, (t % 2) * D:(t % 2 + 1) * D],
                                        wcol[:, 0, t:t + 1], at, ALU.mult, ALU.add)
                                last.then_inc(y_added, 1)

        with ExitStack() as ctx:
            sb = tensors(ctx)
            NT = B * TT
            stats3 = sb("stats3", [P, NT, 6])
            moments3 = sb("moments3", [P, NT, 2])
            rstd3_ln = sb("rstd3_ln", [P, NT])
            rstd3 = sb("rstd3", [P, NT])
            stats3_ready, moments3_ready, act_ln3, rstd3_ready, out_ready, out_stored = (sem(n) for n in (
                "stats3_ready", "moments3_ready", "act_ln3", "rstd3_ready", "out_ready", "out_stored"))
            with nc.Block() as block:
                @block.vector
                def _(v):
                    with v.Fori(0, NT) as t:
                        v.bn_stats(stats3[:, bass.ds(t, 1), :].rearrange("p o s -> p (o s)"),
                                   acc_all[:, bass.ds(t, 1), :].rearrange("p o d -> p (o d)")).then_inc(stats3_ready, 1)
                    v.wait_ge(stats3_ready, NT)
                    for t in range(NT):
                        last = v.bn_aggr(moments3[:, t], stats3[:, t])
                    last.then_inc(moments3_ready, 1)
                    v.wait_ge(moments3_ready, 1)
                    v.wait_ge(rstd3_ready, 1)
                    with v.Fori(0, NT) as t:
                        at = acc_all[:, bass.ds(t, 1), :].rearrange("p o d -> p (o d)")
                        v.tensor_scalar(at, at, moments3[:, bass.ds(t, 1), 0:1].rearrange("p o s -> p (o s)"),
                                        rstd3[:, bass.ds(t, 1)], ALU.subtract, ALU.mult).then_inc(out_ready, 1)

                @block.scalar
                def _(act):
                    act.wait_ge(moments3_ready, 1)
                    act.activation(rstd3_ln[:], moments3[:, :, 1], ACT.Ln, bias=eps_col[:]).then_inc(act_ln3, 1)
                    act.wait_ge(act_ln3, 1)
                    act.activation(rstd3[:], rstd3_ln[:], ACT.Exp, scale=-0.5).then_inc(rstd3_ready, 1)

                @block.sync
                def _(sp):
                    with sp.Fori(0, B) as b:
                        sp.wait_ge(out_ready, TT * (b + 1))
                        sp.dma_start(out[b].rearrange("(t p) d -> p t d", p=P),
                                     acc_all[:, bass.ds(b * TT, TT), :]).then_inc(out_stored, 16)
                    sp.wait_ge(out_stored, 16 * B)


def _columns(*vectors):
    import numpy as np
    return np.ascontiguousarray(np.concatenate([v.reshape(-1, P).T for v in vectors], axis=1))


def kernel(**inputs):
    import numpy as np
    import concourse.bacc as bacc
    from concourse.bass_utils import run_bass_kernel_spmd

    w = {k: np.asarray(v) for k, v in inputs.items()}
    x, ctx = w["x"], w["ctx_1024"]
    B, L, D = x.shape
    S = ctx.shape[1]
    padded = -(-S // P) * P
    m, t, f = "L0_attn_", "L0_xattn_", "L0_ffn_"
    one = lambda v, i=0: np.repeat(v[i:i + 1], P)
    ctx_p = np.zeros((B, padded, D), ctx.dtype)
    ctx_p[:, :S] = ctx
    wo = w[t + "Wo"].reshape(4, 4, D // 16, D)
    wo_p = np.zeros((4, 4, 32, D), wo.dtype)
    wo_p[:, :, :D // 16] = wo
    arrays = {
        "x": x,
        "xT": x.transpose(0, 2, 1).reshape(B, D // P, P, L),
        "ctxT": ctx_p.transpose(0, 2, 1).reshape(B, D // P, P, padded),
        "posT": w[m + "pos_phases"][:L].T,
        "cols": _columns(w[m + "bpv"], w[m + "bk"], w[m + "bkv"], w[m + "bg1"], w[m + "ln_g"], w[m + "ln_b"],
                         w[t + "bq"], w[t + "bk"], w[m + "bb1"], one(w[m + "bg2"]), one(w[m + "bb2"], 0),
                         one(w[m + "bb2"], 1), w[m + "Wg2"], w[m + "Wb2"].T),
        "rows": np.stack([w[m + "bo"], w[t + "bo"], w[t + "bv"], w[t + "bv"]]),
        "Wpv": w[m + "Wpv"], "Wk": w[m + "Wk"], "Wkv": w[m + "Wkv"], "Wg1": w[m + "Wg1"],
        "Wb1": w[m + "Wb1"], "Wo": w[m + "Wo"],
        "xWq": w[t + "Wq"], "xWk": w[t + "Wk"], "xWv": w[t + "Wv"], "xWo": wo_p.reshape(4, P, D),
        "Wr": w[f + "Wr"], "br": w[f + "br"], "W1": w[f + "W1"], "W2": w[f + "W2"],
        "b1T": w[f + "b1"].reshape(w[f + "b1"].shape[0], -1, P).transpose(2, 0, 1), "b2": w[f + "b2"],
    }
    arrays = {f"in_{n}": np.ascontiguousarray(v) for n, v in arrays.items()}
    nc = bacc.Bacc("TRN2", target_bir_lowering=False, num_devices=1)
    a = {n[3:]: nc.dram_tensor(n, v.shape, mybir.dt.from_np(v.dtype), kind="ExternalInput").ap()
         for n, v in arrays.items()}
    a["S_REAL"] = S
    out = nc.dram_tensor("out", [B, L, D], F32, kind="ExternalOutput").ap()
    decoder_layer(nc, a, out)
    r = run_bass_kernel_spmd(nc, [arrays], core_ids=[0])
    return r.results[0]["out"]
```

```python
import math
from contextlib import ExitStack

import concourse.bass as bass
from concourse import mybir

P = 128
F32 = mybir.dt.float32
BF16 = mybir.dt.bfloat16
U32 = mybir.dt.uint32
I32 = mybir.dt.int32
ALU = mybir.AluOpType
ACT = mybir.ActivationFunctionType
AX_X = mybir.AxisListType.X


class Steps:

    def __init__(self, before):
        self.before, self.n = before, 0

    def next(self):
        self.n += 1
        return self.before + self.n


def last_user(k, buffers, per_round):
    if k >= buffers:
        return 0, k - buffers
    return -1, max(p for p in range(per_round) if p % buffers == k)


def decoder_layer(nc, a, out):
    B, L, D = a["x"].shape
    S = a["ctxT"].shape[-1]
    S_REAL = a["S_REAL"]
    H = 16
    DH = D // H
    C = D // P
    TT = L // P
    E = a["W1"].shape[0]
    HID = a["W1"].shape[-1]
    HC = HID // P
    GH = 4
    G = H // GH
    NG = B * G
    ST = S // P
    TAIL = S_REAL - (ST - 1) * P
    KC = S // 4
    PARTS = 3
    Q_SLOTS = (0, 0, 1, 1, 0, 2)
    K_SLOTS = (0, 1, 0, 1, 2, 0)
    STACK = DH * len(Q_SLOTS)
    PAD = 32
    TWO_PI = 2 * math.pi
    TWO_PI_HI = 6.28125
    ROUND = 1.5 * 2.0 ** 23
    PI_DOWN = 3.1415925
    EPS = 1e-5
    SCALE = 1.0 / math.sqrt(DH)
    ROOT_D = math.sqrt(D)
    assert C == 2 and TT == 4 and B % 2 == 0 and G == 4 and E == 8

    q_parts = nc.dram_tensor("q_parts", [PARTS, B, D, L], BF16, kind="Internal").ap()
    k_parts = nc.dram_tensor("k_parts", [PARTS, B, D, S], BF16, kind="Internal").ap()
    v_all = nc.dram_tensor("v_all", [B, G, P, ST * GH * DH], F32, kind="Internal").ap()
    attn_all = nc.dram_tensor("attn_all", [NG, P, L], F32, kind="Internal").ap()
    ROW = D + 2
    AT_DEST, AT_WEIGHT = D, D + 1
    TOKENS = B * L
    REGION = TOKENS + P
    NO_DEST = 4 * TOKENS
    NO_TILE = E * REGION
    TILES = 2 * TOKENS // P + E
    xs = nc.dram_tensor("xs", [E * REGION + P, ROW], F32, kind="Internal").ap()
    y_all = nc.dram_tensor("y_all", [2 * TOKENS, D], F32, kind="Internal").ap()
    x2_all = nc.dram_tensor("x2_all", [B, L, D], F32, kind="Internal").ap()
    x1_all = nc.dram_tensor("x1_all", [B, L, D], F32, kind="Internal").ap()

    with ExitStack() as top:
        def sem(name):
            return top.enter_context(nc.semaphore(name))

        def tensors(ctx):
            def sb(name, shape, dt=F32):
                return ctx.enter_context(nc.sbuf_tensor(name, shape, dt))
            return sb

        psum = top.enter_context(nc.psum_tensor("psum", [P, 8, 512], F32))

        sb = tensors(top)
        ident = sb("ident", [P, P])
        mean_w = sb("mean_w", [P, P])
        eps_col = sb("eps_col", [P, 1])
        half_pi = sb("half_pi", [P, 1])
        cols = sb("cols", [P, a["cols"].shape[-1]])
        rows = sb("rows", [P, 4, D])
        iota8 = sb("iota8", [P, E])
        router_w = sb("router_w", [P, C, E])
        router_b = sb("router_b", [P, E])
        b1_cols = sb("b1_cols", [P, E, HC])
        b2_rows = sb("b2_rows", [E, D])
        before = sb("before", [P, P])
        ones = sb("ones", [P, P])
        dest_ids = sb("dest_ids", [P, 2, B * TT])
        region_at = sb("region_at", [P, E])
        own_row = sb("own_row", [P, 1])
        tile_no = sb("tile_no", [1, TILES + 1])

        def col(i):
            return cols[:, i:i + 1]

        BPV, BK, BKV, BG1, LNG, LNB, BQ, XBK = (2 * i for i in range(8))
        BB1, BG2, BW_A, BW_B, WG2, WB2 = 16, 17, 18, 19, 20, 22
        BO, XBO, XBV, _ = range(4)

        consts_loaded = sem("consts_loaded")
        N_CONSTS = 0
        consts_made = sem("consts_made")
        ident_zeroed = sem("ident_zeroed")
        derived_ready = sem("derived_ready")

        def wait_alone(eng, *waits):
            for _, n in waits:
                eng.to_reg(n)
            eng.wait_ge(consts_made, 1)
            for s, n in waits:
                eng.wait_ge(s, n)

        with ExitStack() as ctx:
            sb = tensors(ctx)
            wpv, wk, wkv, wo, wq = (sb(n, [P, C, D]) for n in ("wpv", "wk", "wkv", "wo", "wq"))
            wg1 = sb("wg1", [P, 2 * C, D])
            wb1 = sb("wb1", [P, C, P])
            wg2_wide = sb("wg2_wide", [P, C, P])
            wb2_wide = sb("wb2_wide", [P, P])
            mcols = sb("mcols", [P, 4])
            pos = sb("pos", [P, C, L])
            turns = sb("turns", [P, C, L])
            pos_cos = sb("pos_cos", [P, C, L])
            pos_sin = sb("pos_sin", [P, C, L])
            xt = sb("xt", [P, 2, C, L + 1])
            xin = sb("xin", [P, 2, TT, D])
            x2bo = sb("x2bo", [P, TT, D])
            phase = sb("phase", [P, C, L])
            phase_abs = sb("phase_abs", [P, C, L])
            key_cos = sb("key_cos", [P, C, L + 1])
            key_sin = sb("key_sin", [P, C, L + 1])
            gate_h = sb("gate_h", [P, C, L])
            blend_h = sb("blend_h", [P, L])
            gate_t = sb("gate_t", [P, L])
            gate = sb("gate", [P, L])
            gate_sum = sb("gate_sum", [P, L])
            gate_ln = sb("gate_ln", [P, L])
            gate_rs = sb("gate_rs", [P, L])
            below_max = sb("below_max", [P, 2, L])
            bexp = sb("bexp", [P, 2, L])
            bsum = sb("bsum", [P, L])
            bsum_ln = sb("bsum_ln", [P, L])
            bsum_r = sb("bsum_r", [P, L])
            bw = sb("bw", [P, 2, L])
            kv_w = sb("kv_w", [P, L])
            mem_c = sb("mem_c", [P, C, L])
            mem_s = sb("mem_s", [P, C, L])
            pos_ret = sb("pos_ret", [P, C, L])
            kvg = sb("kvg", [P, C, L])
            blended = sb("blended", [P, C, L])
            centred = sb("centred", [P, C, L])
            squares = sb("squares", [P, C, L])
            var_ln = sb("var_ln", [P, L])
            rstd_b = sb("rstd_b", [P, L])
            normed = sb("normed", [P, C, L])
            ln_t = sb("ln_t", [P, C, L])
            y = sb("y", [P, TT, D])
            stats = sb("stats", [P, TT, 6])
            moments = sb("moments", [P, TT, 2])
            rstd_ln = sb("rstd_ln", [P, TT])
            rstd = sb("rstd", [P, TT])
            x1 = sb("x1", [P, TT, D])
            x1t = sb("x1t", [P, C, L])
            q_f = sb("q_f", [P, C, L])
            q_rest = sb("q_rest", [P, C, L])
            q_out = sb("q_out", [P, PARTS, C, L], BF16)

            (xt_loaded0, xt_loaded1, pos_ready, trig_ready, pv_ready, kz_ready, gh_ready, bh_ready,
             gate_z_ready, kv_ready, bw_z_ready, mean_ready, var_ready, mix_out_ready, x1t_ready,
             q_ready) = (sem(n) for n in (
                 "xt_loaded0", "xt_loaded1", "pos_ready", "trig_ready", "pv_ready", "kz_ready",
                 "gh_ready", "bh_ready", "gate_z_ready", "kv_ready", "bw_z_ready", "mean_ready",
                 "var_ready", "mix_out_ready", "x1t_ready", "q_ready"))
            xt_loaded = (xt_loaded0, xt_loaded1)
            (phase_ready, gate_h_ready, blend_h_ready, gate_t_ready, key_trig_ready, act_abs, bexp_ready,
             bsum_r_ready, gate_rs_ready, act_ln, squares_ready, rstd_b_ready, ln_ready, rstd_ready,
             x1t_copied, q_copied) = (sem(n) for n in (
                 "phase_ready", "gate_h_ready", "blend_h_ready", "gate_t_ready", "key_trig_ready",
                 "act_abs", "bexp_ready", "bsum_r_ready", "gate_rs_ready", "act_ln",
                 "squares_ready", "rstd_b_ready", "ln_ready", "rstd_ready", "x1t_copied", "q_copied"))
            (dve_pos, dve_mix, pv_used, below_max_ready, gate_sum_ready, bsum_ready, kv_used,
             blended_ready, centred_ready, normed_ready, moments_ready, x1_ready) = (
                 sem(n) for n in ("dve_pos", "dve_mix", "pv_used", "below_max_ready",
                                  "gate_sum_ready", "bsum_ready", "kv_used", "blended_ready",
                                  "centred_ready", "normed_ready", "moments_ready", "x1_ready"))
            x_bo_ready = sem("x_bo_ready")
            x2bo_ready, pool_split, q_split, q_stored, x1_stored, y_ready = (
                sem(n) for n in ("x2bo_ready", "pool_split", "q_split", "q_stored", "x1_stored", "y_ready"))

            consts = [
                (cols[:], a["cols"]),
                (rows[:], a["rows"].rearrange("(o n) d -> o n d", o=1).to_broadcast([P, 4, D])),
                (router_w[:], a["Wr"].rearrange("(c p) e -> p c e", p=P)),
                (router_b[:], a["br"].rearrange("(o e) -> o e", o=1).to_broadcast([P, E])),
                (b1_cols[:], a["b1T"]),
                (b2_rows[:], a["b2"]),
                (before[:], a["before"]),
                (dest_ids[:], a["dest_ids"]),
                (region_at[:], a["region_at"]),
                (own_row[:], a["own_row"]),
                (tile_no[:], a["tile_no"]),
                (wg1[:], a["Wg1"].rearrange("(c p) d -> p c d", p=P)),
                (wb1[:], a["Wb1"].rearrange("(c p) d -> p c d", p=P)),
                (pos[:], a["posT"].rearrange("(c p) l -> p c l", p=P)),
            ] + [(t[:], a[n].rearrange("(c p) d -> p c d", p=P)) for t, n in (
                (wpv, "Wpv"), (wk, "Wk"), (wkv, "Wkv"), (wo, "Wo"), (wq, "xWq"))]
            N_CONSTS = 16 * len(consts)

            DVE_MIX_STEPS = 34
            with nc.Block() as block:
                @block.sync
                def _(sp):
                    for tile, src in consts:
                        sp.dma_start(tile, src).then_inc(consts_loaded, 16)
                    with sp.Fori(0, B // 2) as it:
                        for h in range(2):
                            b = 2 * it + h
                            sp.wait_ge(y_ready, b)
                            for c in range(C):
                                sp.dma_start(xt[:, h, c, 1:L + 1], a["xT"][b, c]).then_inc(xt_loaded[h], 16)
                            sp.dma_start(xin[:, h], a["x"][b].rearrange("(t p) d -> p t d", p=P)) \
                                .then_inc(xt_loaded[h], 16)

                @block.gpsimd
                def _(pool):
                    pool.memset(ident[:], 0.0).then_inc(ident_zeroed, 1)
                    pool.memset(mean_w[:], 1.0 / D)
                    pool.memset(ones[:], 1.0)
                    pool.memset(eps_col[:], EPS)
                    pool.memset(half_pi[:], math.pi / 2)
                    pool.memset(xt[:, :, :, 0:1], 0.0)
                    pool.memset(key_cos[:, :, 0:1], 0.0)
                    pool.memset(key_sin[:, :, 0:1], 0.0)
                    for e in range(E):
                        pool.memset(iota8[:, e:e + 1], float(e))
                    pool.wait_ge(ident_zeroed, 1)
                    pool.affine_select(out=ident[:], in_=ident[:], compare_op=ALU.not_equal, fill=1.0, base=0,
                                       pattern=[[-1, P]], channel_multiplier=1).then_inc(consts_made, 1)
                    pool.wait_ge(consts_loaded, N_CONSTS)
                    with pool.Fori(0, B // 2) as it:
                        for h in range(2):
                            b = 2 * it + h
                            wait_alone(pool, (y_ready, b + 1), (xt_loaded[h], 48 * (it + 1)))
                            pool.tensor_tensor(x2bo[:], xin[:, h], rows[:, BO:BO + 1, :].to_broadcast([P, TT, D]),
                                               ALU.add).then_inc(x_bo_ready, 1)
                            pool.wait_ge(x_bo_ready, b + 1)
                            pool.tensor_tensor(x2bo[:], x2bo[:], xin[:, h], ALU.add).then_inc(x2bo_ready, 1)
                            wait_alone(pool, (x1_ready, b + 1))
                            pool.dma_start(x1_all[b].rearrange("(t p) d -> p t d", p=P), x1[:]) \
                                .then_inc(x1_stored, 16)
                            wait_alone(pool, (q_stored, 16 * PARTS * b), (q_copied, b + 1))
                            pool.tensor_scalar(q_out[:, 0], q_f[:], 1.0, None, ALU.mult).then_inc(pool_split, 1)
                            pool.wait_ge(pool_split, 3 * b + 1)
                            pool.tensor_tensor(q_rest[:], q_f[:], q_out[:, 0], ALU.subtract).then_inc(pool_split, 1)
                            wait_alone(pool, (pool_split, 3 * b + 2))
                            pool.tensor_scalar(q_out[:, 1], q_rest[:], 1.0, None, ALU.mult).then_inc(pool_split, 1)
                            pool.wait_ge(pool_split, 3 * b + 3)
                            pool.tensor_tensor(q_out[:, 2], q_rest[:], q_out[:, 1], ALU.subtract).then_inc(q_split, 1)
                            wait_alone(pool, (q_split, b + 1))
                            for part in range(PARTS):
                                pool.dma_start(q_parts[part, b].rearrange("(c p) l -> p c l", p=P),
                                               q_out[:, part]).then_inc(q_stored, 16)
                    pool.wait_ge(q_stored, 16 * PARTS * B)
                    pool.wait_ge(x1_stored, 16 * B)

                @block.tensor
                def _(pe):
                    def project(bank, weights, rhs, chunks):
                        for co in range(C):
                            for k in range(chunks):
                                last = pe.matmul(psum[:, bank + co, :], weights[:, k, co * P:(co + 1) * P],
                                                 rhs(k), start=k == 0, stop=k == chunks - 1)
                        return last

                    pe.wait_ge(consts_loaded, N_CONSTS)
                    pe.wait_ge(consts_made, 1)
                    pe.wait_ge(derived_ready, 1)
                    with pe.Fori(0, B // 2) as it:
                        for h in range(2):
                            b = 2 * it + h
                            now = lambda k: xt[:, h, k % C, 1 - k // C:L + 1 - k // C]
                            pe.wait_ge(xt_loaded[h], 48 * (it + 1))
                            pe.wait_ge(rstd_b_ready, b)
                            project(2, wk, now, C).then_inc(kz_ready, 1)
                            pe.wait_ge(q_copied, b)
                            project(4, wg1, now, 2 * C).then_inc(gh_ready, 1)
                            pe.wait_ge(x1t_copied, b)
                            for k in range(C):
                                last = pe.matmul(psum[:, 6, :], wb1[:, k, :], now(k), start=k == 0, stop=k == C - 1)
                            last.then_inc(bh_ready, 1)
                            pe.wait_ge(y_ready, b + 1)
                            project(0, wpv, now, C).then_inc(pv_ready, 1)
                            pe.wait_ge(gate_h_ready, b + 1)
                            for k in range(C):
                                last = pe.matmul(psum[:, 7, :], wg2_wide[:, k, :], gate_h[:, k, :],
                                                 start=k == 0, stop=k == C - 1)
                            last.then_inc(gate_z_ready, 1)
                            project(4, wkv, now, C).then_inc(kv_ready, 1)
                            pe.wait_ge(blend_h_ready, b + 1)
                            pe.matmul(psum[:, 6, :], wb2_wide[:], blend_h[:], start=True, stop=True) \
                                .then_inc(bw_z_ready, 1)
                            pe.wait_ge(phase_ready, b + 1)
                            pe.wait_ge(blended_ready, b + 1)
                            for k in range(C):
                                last = pe.matmul(psum[:, 2, :], mean_w[:], blended[:, k, :], start=k == 0, stop=k == C - 1)
                            last.then_inc(mean_ready, 1)
                            pe.wait_ge(squares_ready, b + 1)
                            for k in range(C):
                                last = pe.matmul(psum[:, 3, :], mean_w[:], squares[:, k, :], start=k == 0, stop=k == C - 1)
                            last.then_inc(var_ready, 1)
                            pe.wait_ge(pv_used, b + 1)
                            pe.wait_ge(ln_ready, b + 1)
                            for t in range(TT):
                                for k in range(C):
                                    last = pe.matmul(psum[:, t // 2, (t % 2) * D:(t % 2 + 1) * D],
                                                     ln_t[:, k, t * P:(t + 1) * P], wo[:, k, :],
                                                     start=k == 0, stop=k == C - 1)
                            last.then_inc(mix_out_ready, 1)
                            pe.wait_ge(gate_t_ready, b + 1)
                            pe.wait_ge(below_max_ready, b + 1)
                            pe.wait_ge(x1_ready, b + 1)
                            for k in range(C):
                                for t in range(TT):
                                    last = pe.transpose(psum[:, 6 + k, t * P:(t + 1) * P],
                                                        x1[:, t, k * P:(k + 1) * P], ident[:])
                            last.then_inc(x1t_ready, 1)
                            pe.wait_ge(kv_used, b + 1)
                            pe.wait_ge(x1t_copied, b + 1)
                            project(4, wq, lambda k: x1t[:, k, :], C).then_inc(q_ready, 1)

                @block.scalar
                def _(act):
                    act.wait_ge(consts_loaded, N_CONSTS)
                    act.wait_ge(consts_made, 1)
                    act.wait_ge(pos_ready, 1)
                    act.activation(pos_sin[:], pos[:], ACT.Sin)
                    act.activation(pos_cos[:], turns[:], ACT.Sin, bias=half_pi[:], scale=-1.0).then_inc(trig_ready, 1)
                    with act.Fori(0, B // 2) as it:
                        for h in range(2):
                            b = 2 * it + h
                            for c in range(C):
                                act.wait_ge(kz_ready, b + 1)
                                last = act.activation(phase[:, c], psum[:, 2 + c], ACT.Tanh, bias=col(BK + c))
                            last.then_inc(phase_ready, 1)
                            for c in range(C):
                                act.wait_ge(gh_ready, b + 1)
                                act.wait_ge(gate_z_ready, b)
                                last = act.activation(gate_h[:, c], psum[:, 4 + c], ACT.Gelu, bias=col(BG1 + c))
                            last.then_inc(gate_h_ready, 1)
                            act.wait_ge(bw_z_ready, b)
                            act.wait_ge(bh_ready, b + 1)
                            act.activation(blend_h[:], psum[:, 6], ACT.Gelu, bias=col(BB1)).then_inc(blend_h_ready, 1)
                            act.wait_ge(gate_z_ready, b + 1)
                            act.activation(gate_t[:], psum[:, 7], ACT.Tanh, bias=mcols[:, 0:1], scale=0.5) \
                                .then_inc(gate_t_ready, 1)
                            act.wait_ge(phase_ready, b + 1)
                            act.activation(phase_abs[:], phase[:], ACT.Abs).then_inc(act_abs, 1)
                            act.wait_ge(blended_ready, b)
                            act.activation(key_sin[:, :, 1:L + 1], phase[:], ACT.Sin, scale=PI_DOWN)
                            act.wait_ge(act_abs, b + 1)
                            act.activation(key_cos[:, :, 1:L + 1], phase_abs[:], ACT.Sin, bias=half_pi[:],
                                           scale=-PI_DOWN).then_inc(key_trig_ready, 1)
                            act.wait_ge(below_max_ready, b + 1)
                            act.activation(bexp[:, 0], below_max[:, 0], ACT.Exp)
                            act.activation(bexp[:, 1], below_max[:, 1], ACT.Exp, scale=-1.0).then_inc(bexp_ready, 1)
                            act.wait_ge(gate_sum_ready, b + 1)
                            act.activation(gate_ln[:], gate_sum[:], ACT.Ln).then_inc(act_ln, 1)
                            act.wait_ge(act_ln, 4 * b + 1)
                            act.activation(gate_rs[:], gate_ln[:], ACT.Exp, scale=-0.5).then_inc(gate_rs_ready, 1)
                            act.wait_ge(bsum_ready, b + 1)
                            act.activation(bsum_ln[:], bsum[:], ACT.Ln).then_inc(act_ln, 1)
                            act.wait_ge(act_ln, 4 * b + 2)
                            act.activation(bsum_r[:], bsum_ln[:], ACT.Exp, scale=-1.0).then_inc(bsum_r_ready, 1)
                            act.wait_ge(centred_ready, b + 1)
                            act.activation(squares[:], centred[:], ACT.Square).then_inc(squares_ready, 1)
                            act.wait_ge(var_ready, b + 1)
                            act.activation(var_ln[:], psum[:, 3], ACT.Ln, bias=eps_col[:]).then_inc(act_ln, 1)
                            act.wait_ge(act_ln, 4 * b + 3)
                            act.activation(rstd_b[:], var_ln[:], ACT.Exp, scale=-0.5).then_inc(rstd_b_ready, 1)
                            act.wait_ge(normed_ready, b + 1)
                            act.wait_ge(mix_out_ready, b)
                            for c in range(C):
                                last = act.activation(ln_t[:, c], normed[:, c], ACT.Identity, bias=col(LNB + c),
                                                      scale=col(LNG + c))
                            last.then_inc(ln_ready, 1)
                            act.wait_ge(moments_ready, b + 1)
                            act.activation(rstd_ln[:], moments[:, :, 1], ACT.Ln, bias=eps_col[:]).then_inc(act_ln, 1)
                            act.wait_ge(act_ln, 4 * b + 4)
                            act.activation(rstd[:], rstd_ln[:], ACT.Exp, scale=-0.5).then_inc(rstd_ready, 1)
                            act.wait_ge(q_ready, b)
                            act.wait_ge(x1t_ready, b + 1)
                            act.activation(x1t[:], psum[:, 6:8], ACT.Copy).then_inc(x1t_copied, 1)
                            act.wait_ge(q_split, b)
                            act.wait_ge(q_ready, b + 1)
                            for c in range(C):
                                last = act.activation(q_f[:, c], psum[:, 4 + c], ACT.Identity, bias=col(BQ + c))
                            last.then_inc(q_copied, 1)

                @block.vector
                def _(v):
                    v.wait_ge(consts_loaded, N_CONSTS)
                    v.tensor_tensor(mcols[:, 1:2], col(WB2), col(WB2 + 1), ALU.subtract).then_inc(dve_pos, 1)
                    v.tensor_tensor(mcols[:, 2:3], col(BW_A), col(BW_B), ALU.subtract)
                    v.tensor_scalar(mcols[:, 0:1], col(BG2), 0.5, None, ALU.mult)
                    for k in range(C):
                        v.tensor_copy(wg2_wide[:, k, :], col(WG2 + k).to_broadcast([P, P]))
                    v.wait_ge(dve_pos, 1)
                    v.tensor_copy(wb2_wide[:], mcols[:, 1:2].to_broadcast([P, P])).then_inc(derived_ready, 1)
                    v.tensor_scalar(turns[:], pos[:], 1.0 / TWO_PI, ROUND, ALU.mult, ALU.add).then_inc(dve_pos, 1)
                    v.wait_ge(dve_pos, 2)
                    v.tensor_scalar(turns[:], turns[:], -ROUND, None, ALU.add).then_inc(dve_pos, 1)
                    v.wait_ge(dve_pos, 3)
                    v.scalar_tensor_tensor(pos[:], turns[:], -TWO_PI_HI, pos[:], ALU.mult, ALU.add).then_inc(dve_pos, 1)
                    v.wait_ge(dve_pos, 4)
                    v.scalar_tensor_tensor(pos[:], turns[:], TWO_PI_HI - TWO_PI, pos[:], ALU.mult, ALU.add) \
                        .then_inc(dve_pos, 1)
                    v.wait_ge(dve_pos, 5)
                    v.tensor_scalar(pos[:], pos[:], -PI_DOWN, PI_DOWN, ALU.max, ALU.min).then_inc(dve_pos, 1)
                    v.wait_ge(dve_pos, 6)
                    v.scalar_tensor_tensor(turns[:], pos[:], -1.0, pos[:], ALU.mult, ALU.max).then_inc(pos_ready, 1)
                    v.wait_ge(trig_ready, 1)
                    v.sem_inc(y_ready, 1)
                    with v.Fori(0, B // 2) as it:
                        for h in range(2):
                            b = 2 * it + h
                            step = Steps(DVE_MIX_STEPS * b)
                            v.wait_ge(pv_ready, b + 1)
                            for c in range(C):
                                v.scalar_tensor_tensor(mem_c[:, c], psum[:, c], col(BPV + c), pos_cos[:, c], ALU.add,
                                                       ALU.mult).then_inc(dve_mix, 1)
                                step.next()
                            for c in range(C):
                                last = v.scalar_tensor_tensor(mem_s[:, c], psum[:, c], col(BPV + c), pos_sin[:, c],
                                                              ALU.add, ALU.mult)
                                last.then_inc(pv_used if c else dve_mix, 1)
                            s0 = step.next()
                            v.wait_ge(dve_mix, s0)
                            v.wait_ge(pv_used, b + 1)

                            def scan(mem):
                                for c in range(C):
                                    v.tensor_tensor_scan(mem[:, c], mem[:, c], mem[:, c], 0.0, ALU.add, ALU.bypass) \
                                        .then_inc(dve_mix, 1)
                                    s = step.next()
                                return s

                            def times(out_t, in0, in1, op=ALU.mult):
                                v.tensor_tensor(out_t, in0, in1, op).then_inc(dve_mix, 1)
                                return step.next()

                            scan(mem_c)
                            s = scan(mem_s)
                            v.wait_ge(dve_mix, s - 2)
                            times(mem_c[:], mem_c[:], pos_cos[:])
                            v.wait_ge(dve_mix, s)
                            s = times(mem_s[:], mem_s[:], pos_sin[:])
                            v.wait_ge(dve_mix, s)
                            times(pos_ret[:], mem_c[:], mem_s[:], ALU.add)
                            v.wait_ge(gate_t_ready, b + 1)
                            v.tensor_scalar(gate[:], gate_t[:], 0.5, 0.5, ALU.mult, ALU.add).then_inc(dve_mix, 1)
                            s = step.next()
                            v.wait_ge(dve_mix, s)
                            v.tensor_tensor_scan(gate_sum[:], gate[:], gate[:], 0.0, ALU.add, ALU.bypass).then_inc(dve_mix, 1)
                            s = step.next()
                            v.wait_ge(dve_mix, s)
                            v.wait_ge(gate_rs_ready, b)
                            v.tensor_scalar(gate_sum[:], gate_sum[:], 1.0, None, ALU.max).then_inc(gate_sum_ready, 1)
                            v.wait_ge(bexp_ready, b)
                            v.wait_ge(bw_z_ready, b + 1)
                            v.tensor_scalar(below_max[:, 0], psum[:, 6], mcols[:, 2:3], 0.0, ALU.add, ALU.min)
                            v.tensor_scalar(below_max[:, 1], psum[:, 6], mcols[:, 2:3], 0.0, ALU.add, ALU.max) \
                                .then_inc(below_max_ready, 1)
                            v.wait_ge(kv_ready, b + 1)
                            for c in range(C):
                                v.scalar_tensor_tensor(kvg[:, c], psum[:, 4 + c], col(BKV + c), gate[:], ALU.add,
                                                       ALU.mult).then_inc(kv_used if c else dve_mix, 1)
                            s = step.next()
                            v.wait_ge(dve_mix, s)
                            v.wait_ge(kv_used, b + 1)
                            v.wait_ge(key_trig_ready, b + 1)
                            times(mem_c[:], kvg[:], key_cos[:, :, 0:L])
                            s = times(mem_s[:], kvg[:], key_sin[:, :, 0:L])
                            v.wait_ge(dve_mix, s - 1)
                            scan(mem_c)
                            v.wait_ge(dve_mix, s)
                            s = scan(mem_s)
                            v.wait_ge(dve_mix, s - 2)
                            times(mem_c[:], mem_c[:], key_cos[:, :, 1:L + 1])
                            v.wait_ge(dve_mix, s)
                            s = times(mem_s[:], mem_s[:], key_sin[:, :, 1:L + 1])
                            v.wait_ge(dve_mix, s)
                            s_kv = times(mem_c[:], mem_c[:], mem_s[:], ALU.add)
                            v.wait_ge(bexp_ready, b + 1)
                            v.wait_ge(bsum_r_ready, b)
                            v.tensor_tensor(bsum[:], bexp[:, 0], bexp[:, 1], ALU.add).then_inc(bsum_ready, 1)
                            v.wait_ge(bsum_r_ready, b + 1)
                            v.wait_ge(gate_rs_ready, b + 1)
                            for i in range(2):
                                v.scalar_tensor_tensor(bw[:, i], bexp[:, i], 1.0 / ROOT_D, bsum_r[:], ALU.mult, ALU.mult) \
                                    .then_inc(dve_mix, 1)
                                s = step.next()
                            v.wait_ge(dve_mix, s)
                            s = times(kv_w[:], bw[:, 1], gate_rs[:])
                            for c in range(C):
                                times(pos_ret[:, c], pos_ret[:, c], bw[:, 0])
                            v.wait_ge(dve_mix, s)
                            for c in range(C):
                                s = times(mem_c[:, c], mem_c[:, c], kv_w[:])
                            v.wait_ge(dve_mix, s)
                            v.wait_ge(mean_ready, b)
                            v.tensor_tensor(blended[:], pos_ret[:], mem_c[:], ALU.add).then_inc(blended_ready, 1)
                            v.wait_ge(blended_ready, b + 1)
                            v.wait_ge(squares_ready, b)
                            for c in range(C):
                                v.wait_ge(mean_ready, b + 1)
                                last = v.tensor_tensor(centred[:, c], blended[:, c], psum[:, 2], ALU.subtract)
                                last.then_inc(centred_ready if c else dve_mix, 1)
                            s = step.next()
                            v.wait_ge(dve_mix, s)
                            v.wait_ge(centred_ready, b + 1)
                            v.wait_ge(ln_ready, b)
                            v.wait_ge(rstd_b_ready, b + 1)
                            for c in range(C):
                                last = v.tensor_tensor(normed[:, c], centred[:, c], rstd_b[:], ALU.mult)
                            last.then_inc(normed_ready, 1)
                            v.wait_ge(x2bo_ready, b + 1)
                            v.wait_ge(mix_out_ready, b + 1)
                            v.tensor_tensor(y[:].rearrange("p t d -> p (t d)").rearrange("p (n f) -> p n f", n=2),
                                            psum[:, 0:2],
                                            x2bo[:].rearrange("p t d -> p (t d)").rearrange("p (n f) -> p n f", n=2),
                                            ALU.add).then_inc(y_ready, 1)
                            v.wait_ge(y_ready, b + 2)
                            for t in range(TT):
                                last = v.bn_stats(stats[:, t], y[:, t])
                                last.then_inc(dve_mix, 1)
                                s = step.next()
                            wait_alone(v, (dve_mix, s))
                            for t in range(TT):
                                last = v.bn_aggr(moments[:, t], stats[:, t])
                            last.then_inc(moments_ready, 1)
                            v.wait_ge(x1_stored, 16 * b)
                            v.wait_ge(x1t_ready, b)
                            v.wait_ge(moments_ready, b + 1)
                            v.wait_ge(rstd_ready, b + 1)
                            for t in range(TT):
                                last = v.tensor_scalar(x1[:, t], y[:, t], moments[:, t, 0:1], rstd[:, t:t + 1],
                                                       ALU.subtract, ALU.mult)
                            last.then_inc(x1_ready, 1)
                            assert step.n == DVE_MIX_STEPS, step.n

        with ExitStack() as ctx:
            sb = tensors(ctx)
            xwk, xwv = sb("xwk", [P, C, D]), sb("xwv", [P, C, D])
            ct = sb("ct", [P, 2, C, S])
            neg_bk = sb("neg_bk", [P, C])
            k_f = sb("k_f", [P, 2, KC])
            k_rest = sb("k_rest", [P, 2, KC])
            k_out = sb("k_out", [P, 2, PARTS, KC], BF16)
            v_out = sb("v_out", [P, 2, G, ST, GH * DH])
            xw_loaded, neg_bk_ready, kp_ready, k_copied, k_hi, k_mid, k_rest_ready, k_split = (
                sem(n) for n in ("xw_loaded", "neg_bk_ready", "kp_ready", "k_copied", "k_hi", "k_mid",
                                 "k_rest_ready", "k_split"))
            ct_loaded = (sem("ct_loaded0"), sem("ct_loaded1"))
            k_stored = (sem("k_stored0"), sem("k_stored1"))
            v_stored = (sem("v_stored0"), sem("v_stored1"))
            vp_ready, v_copied = sem("vp_ready"), sem("v_copied")
            KJ = 4 * C
            VJ = (ST + 1) // 2

            with nc.Block() as block:
                @block.sync
                def _(sp):
                    sp.dma_start(xwk[:], a["xWk"].rearrange("(c p) d -> p c d", p=P)).then_inc(xw_loaded, 16)
                    sp.dma_start(xwv[:], a["xWv"].rearrange("(c p) d -> p c d", p=P)).then_inc(xw_loaded, 16)
                    with sp.Fori(0, B // 2) as it:
                        for h in range(2):
                            sp.wait_ge(v_copied, VJ * (2 * it + h))
                            sp.dma_start(ct[:, h], a["ctxT"][2 * it + h].rearrange("c p s -> p c s")) \
                                .then_inc(ct_loaded[h], 16)

                @block.tensor
                def _(pe):
                    pe.wait_ge(xw_loaded, 32)
                    with pe.Fori(0, B // 2) as it:
                        for h in range(2):
                            b = 2 * it + h
                            pe.wait_ge(ct_loaded[h], 16 * (it + 1))
                            for j in range(KJ):
                                co, s0 = j // 4, (j % 4) * KC
                                if j >= 4:
                                    pe.wait_ge(k_copied, KJ * b + j - 3)
                                for k in range(C):
                                    last = pe.matmul(psum[:, j % 4, 0:KC], xwk[:, k, co * P:(co + 1) * P],
                                                     ct[:, h, k, s0:s0 + KC], start=k == 0, stop=k == C - 1)
                                last.then_inc(kp_ready, 1)
                            for j in range(VJ):
                                if j >= 4:
                                    pe.wait_ge(v_copied, VJ * (b + 1) + j - 3)
                                for t in range(2 * j, min(2 * j + 2, ST)):
                                    for k in range(C):
                                        last = pe.matmul(psum[:, 4 + j % 4, (t % 2) * D:(t % 2 + 1) * D],
                                                         ct[:, h, k, t * P:(t + 1) * P], xwv[:, k, :],
                                                         start=k == 0, stop=k == C - 1)
                                last.then_inc(vp_ready, 1)
                            pe.wait_ge(k_copied, KJ * (b + 1))
                            pe.wait_ge(v_copied, VJ * (b + 2))

                @block.scalar
                def _(act):
                    act.wait_ge(neg_bk_ready, 1)
                    with act.Fori(0, B // 2) as it:
                        for h in range(2):
                            b = 2 * it + h
                            for j in range(KJ):
                                if j >= 2:
                                    act.wait_ge(k_split, KJ * b + j - 1)
                                else:
                                    act.wait_ge(k_split, KJ * b)
                                act.wait_ge(kp_ready, KJ * b + j + 1)
                                act.activation(k_f[:, j % 2], psum[:, j % 4, 0:KC], ACT.Identity,
                                               bias=neg_bk[:, j // 4:j // 4 + 1], scale=-SCALE).then_inc(k_copied, 1)
                                act.wait_ge(k_stored[j % 2], 16 * (KJ // 2 * b + j // 2))
                                act.wait_ge(k_copied, KJ * b + j + 1)
                                act.activation(k_out[:, j % 2, 0], k_f[:, j % 2], ACT.Copy).then_inc(k_hi, 1)
                                act.wait_ge(k_rest_ready, KJ * b + j + 1)
                                act.activation(k_out[:, j % 2, 1], k_rest[:, j % 2], ACT.Copy).then_inc(k_mid, 1)

                @block.gpsimd
                def _(pool):
                    with pool.Fori(0, B // 2) as it:
                        for h in range(2):
                            b = 2 * it + h
                            for j in range(KJ):
                                pool.wait_ge(k_mid, KJ * b + j + 1)
                                pool.tensor_tensor(k_out[:, j % 2, 2], k_rest[:, j % 2], k_out[:, j % 2, 1],
                                                   ALU.subtract).then_inc(k_split, 1)
                                wait_alone(pool, (k_split, KJ * b + j + 1))
                                co, s0 = j // 4, (j % 4) * KC
                                pool.dma_start(
                                    k_parts[:, b, co * P:(co + 1) * P, s0:s0 + KC].rearrange("n p s -> p n s"),
                                    k_out[:, j % 2]).then_inc(k_stored[j % 2], 16)
                            wait_alone(pool, (v_copied, VJ * (b + 2)))
                            pool.dma_start(v_all[b].rearrange("g p f -> p g f"),
                                           v_out[:, h].rearrange("p g t f -> p g (t f)")).then_inc(v_stored[h], 16)
                    for h in range(2):
                        pool.wait_ge(k_stored[h], 16 * B * KJ // 2)
                        pool.wait_ge(v_stored[h], 16 * B // 2)

                @block.vector
                def _(v):
                    v.tensor_scalar(neg_bk[:], cols[:, XBK:XBK + C], -SCALE, None, ALU.mult).then_inc(neg_bk_ready, 1)
                    v.sem_inc(v_copied, VJ)
                    with v.Fori(0, B // 2) as it:
                        for h in range(2):
                            b = 2 * it + h
                            v.wait_ge(v_stored[h], 16 * it)
                            for j in range(KJ):
                                v.wait_ge(k_hi, KJ * b + j + 1)
                                v.tensor_tensor(k_rest[:, j % 2], k_f[:, j % 2], k_out[:, j % 2, 0], ALU.subtract) \
                                    .then_inc(k_rest_ready, 1)
                            for j in range(VJ):
                                v.wait_ge(vp_ready, VJ * b + j + 1)
                                n = min(2, ST - 2 * j)
                                for i in range(n):
                                    last = v.tensor_tensor(
                                        v_out[:, h, :, 2 * j + i, :],
                                        psum[:, 4 + j % 4, i * D:(i + 1) * D].rearrange("p (g f) -> p g f", g=G),
                                        rows[:, XBV, :].rearrange("p (g f) -> p g f", g=G), ALU.add)
                                last.then_inc(v_copied, 1)

        sb = tensors(top)
        w1_all = sb("w1_all", [P, E, C, HID])
        w2_all = sb("w2_all", [P, E, HC, D])
        ffn_loaded = sem("ffn_loaded")

        with ExitStack() as ctx:
            sb = tensors(ctx)
            SUBS = 2 * ST
            SCORE_BUFS, P_BUFS = 3, 3
            N_SUB, N_TILE = 2 * SUBS, 2 * ST
            LAG = 2
            qst = sb("qst", [STACK, 2, GH, L], BF16)
            kst = sb("kst", [STACK, 2, GH, S], BF16)
            vst = sb("vst", [P, 2, ST, GH * DH])
            neg_max = sb("neg_max", [P, SCORE_BUFS, 2])
            probs = sb("probs", [P, P_BUFS, GH, L])
            sums = sb("sums", [P, P_BUFS, GH])
            inv = sb("inv", [P, P_BUFS, GH])
            v_scaled = sb("v_scaled", [P, P_BUFS, GH, PAD])
            attn = sb("attn", [P, 2, L])
            heads_loaded = (sem("heads_loaded0"), sem("heads_loaded1"))
            (pads_zeroed, scores_ready, max_ready, exp_done, inv_ready, v_scaled_ready, pv_done,
             attn_copied) = (sem(n) for n in (
                 "pads_zeroed", "scores_ready", "max_ready", "exp_done", "inv_ready", "v_scaled_ready", "pv_done",
                 "attn_copied"))
            attn_stored = (sem("attn_stored0"), sem("attn_stored1"))
            CREDIT = P_BUFS

            def free(k, bufs, per_round, it):
                round_, p = last_user(k, bufs, per_round)
                return per_round * it + per_round * round_ + p + 1 + CREDIT

            with nc.Block() as block:
                @block.sync
                def _(sp):
                    with sp.Fori(0, NG // 2) as it:
                        for h in range(2):
                            n = 2 * it + h
                            sp.wait_ge(attn_copied, n)
                            for slot in range(len(Q_SLOTS)):
                                at = slice(slot * DH, (slot + 1) * DH)
                                qd = q_parts[Q_SLOTS[slot]].rearrange("b (g j d) l -> (b g) d j l", g=G, j=GH)[n]
                                kd = k_parts[K_SLOTS[slot]].rearrange("b (g j d) s -> (b g) d j s", g=G, j=GH)[n]
                                sp.dma_start(qst[at, h], qd).then_inc(heads_loaded[h], 16)
                                sp.dma_start(kst[at, h], kd).then_inc(heads_loaded[h], 16)
                            sp.dma_start(vst[:, h].rearrange("p t f -> p (t f)"),
                                         v_all.rearrange("b g p f -> (b g) p f")[n]).then_inc(heads_loaded[h], 16)
                    with sp.Fori(0, E) as e:
                        sp.dma_start(w1_all[:, bass.ds(e, 1)].rearrange("p o c h -> p (o c) h"),
                                     a["W1"][e].rearrange("(c p) h -> p c h", p=P)).then_inc(ffn_loaded, 16)
                        sp.dma_start(w2_all[:, bass.ds(e, 1)].rearrange("p o c d -> p (o c) d"),
                                     a["W2"][e].rearrange("(c p) d -> p c d", p=P)).then_inc(ffn_loaded, 16)

                LOADS = 16 * (2 * len(Q_SLOTS) + 1)

                def rows_of(t):
                    return P if t < ST - 1 else TAIL

                def copy_group(v, it, h):
                    v.wait_ge(pv_done, N_TILE * it + ST * (h + 1))
                    v.wait_ge(attn_stored[h], 16 * it)
                    v.tensor_copy(attn[:, h], psum[:, 6]).then_inc(attn_copied, 1)

                def store_group(pool, it, h):
                    wait_alone(pool, (attn_copied, 2 * it + h + 2))
                    pool.dma_start(attn_all[2 * it + h], attn[:, h]).then_inc(attn_stored[h], 16)

                @block.tensor
                def _(pe):
                    pe.wait_ge(pads_zeroed, 1)
                    with pe.Fori(0, NG // 2) as it:
                        def pv(tile):
                            h, t = divmod(tile, ST)
                            if t == 0:
                                pe.wait_ge(attn_copied, 2 * it + h + 1)
                            pe.wait_ge(v_scaled_ready, N_TILE * it + tile + 1)
                            r, pb = rows_of(t), tile % P_BUFS
                            for j in range(GH):
                                last = pe.matmul(psum[j * PAD:(j + 1) * PAD, 6, :], v_scaled[0:r, pb, j, :],
                                                 probs[0:r, pb, j, :], start=t == 0, stop=t == ST - 1)
                            last.then_inc(pv_done, 1)

                        for tile in range(N_TILE):
                            h, t = divmod(tile, ST)
                            if t == 0:
                                pe.wait_ge(heads_loaded[h], LOADS * (it + 1))
                            r = rows_of(t)
                            for sub in range(2):
                                k = 2 * tile + sub
                                sbuf = k % SCORE_BUFS
                                pe.wait_ge(exp_done, free(k, SCORE_BUFS, N_SUB, it))
                                for i in range(2):
                                    j = 2 * sub + i
                                    last = pe.matmul(psum[0:r, 2 * sbuf + i, :], kst[:, h, j, t * P:t * P + r],
                                                     qst[:, h, j, :], start=True, stop=True)
                                last.then_inc(scores_ready, 1)
                            if tile >= LAG:
                                pv(tile - LAG)
                        for tile in range(N_TILE - LAG, N_TILE):
                            pv(tile)

                @block.vector
                def _(v):
                    v.memset(v_scaled[:], 0.0).then_inc(pads_zeroed, 1)
                    v.sem_inc(attn_copied, 1)
                    with v.Fori(0, NG // 2) as it:
                        def inverse(tile):
                            v.wait_ge(exp_done, N_SUB * it + 2 * tile + 2 + CREDIT)
                            r = rows_of(tile % ST)
                            v.reciprocal(inv[0:r, tile % P_BUFS], sums[0:r, tile % P_BUFS]).then_inc(inv_ready, 1)

                        for tile in range(N_TILE):
                            h, t = divmod(tile, ST)
                            r = rows_of(t)
                            for sub in range(2):
                                k = 2 * tile + sub
                                sbuf = k % SCORE_BUFS
                                v.wait_ge(scores_ready, N_SUB * it + k + 1)
                                v.tensor_reduce(neg_max[0:r, sbuf], psum[0:r, 2 * sbuf:2 * sbuf + 2], AX_X, ALU.min) \
                                    .then_inc(max_ready, 1)
                            if tile >= 1:
                                inverse(tile - 1)
                            if t == LAG and h == 1:
                                copy_group(v, it, 0)
                        inverse(N_TILE - 1)
                        copy_group(v, it, 1)

                @block.gpsimd
                def _(pool):
                    pool.wait_ge(pads_zeroed, 1)
                    with pool.Fori(0, NG // 2) as it:
                        for tile in range(N_TILE):
                            h, t = divmod(tile, ST)
                            r, pb = rows_of(t), tile % P_BUFS
                            if tile >= P_BUFS:
                                pool.wait_ge(pv_done, N_TILE * it + tile - P_BUFS + 1)
                            pool.wait_ge(inv_ready, N_TILE * it + tile + 1)
                            last = pool.tensor_tensor(
                                v_scaled[0:r, pb, :, 0:DH], vst[0:r, h, t, :].rearrange("p (j d) -> p j d", j=GH),
                                inv[0:r, pb].rearrange("p (j o) -> p j o", o=1).to_broadcast([r, GH, DH]), ALU.mult)
                            last.then_inc(v_scaled_ready, 1)
                            if tile == ST + LAG + 1:
                                store_group(pool, it, 0)
                        store_group(pool, it, 1)
                    for h in range(2):
                        pool.wait_ge(attn_stored[h], 16 * NG // 2)

                @block.scalar
                def _(act):
                    act.wait_ge(pads_zeroed, 1)
                    act.sem_inc(exp_done, CREDIT)
                    with act.Fori(0, NG // 2) as it:
                        for tile in range(N_TILE):
                            h, t = divmod(tile, ST)
                            r, pb = rows_of(t), tile % P_BUFS
                            if tile >= P_BUFS:
                                act.wait_ge(pv_done, N_TILE * it + tile - P_BUFS + 1)
                            elif tile == 0:
                                act.wait_ge(pv_done, N_TILE * it)
                            for sub in range(2):
                                k = 2 * tile + sub
                                sbuf = k % SCORE_BUFS
                                act.wait_ge(max_ready, N_SUB * it + k + 1)
                                for i in range(2):
                                    j = 2 * sub + i
                                    last = act.activation(probs[0:r, pb, j, :], psum[0:r, 2 * sbuf + i, :], ACT.Exp,
                                                          bias=neg_max[0:r, sbuf, i:i + 1], scale=-1.0,
                                                          accum_out=sums[0:r, pb, j:j + 1])
                                last.then_inc(exp_done, 1)

        sb = tensors(top)
        tile_row = sb("tile_row", [1, TILES + 1], I32)
        tile_expert = sb("tile_expert", [1, TILES + 1], I32)

        with ExitStack() as ctx:
            sb = tensors(ctx)
            xwo = sb("xwo", [P, G, D])
            at_in = sb("at_in", [P, 2, G, L])
            x1_in = sb("x1_in", [P, 2, TT, D])
            y2 = sb("y2", [P, TT, D])
            stats2 = sb("stats2", [P, TT, 6])
            moments2 = sb("moments2", [P, TT, 2])
            rstd2_ln = sb("rstd2_ln", [P, TT])
            rstd2 = sb("rstd2", [P, TT])
            rows_out = sb("rows_out", [P, 2, 2, TT, ROW])
            x2t = sb("x2t", [P, C, L])
            x2b = sb("x2b", [P, TT, D])
            mask = sb("mask", [P, TT, E])
            slot_at = sb("slot_at", [P, TT + 1, E])
            slot_of = sb("slot_of", [P, TT, E])
            slot_own = sb("slot_own", [P, 2, TT, E])
            slot_f = sb("slot_f", [P, 2 * TT])
            slot_u = sb("slot_u", [P, 2, 2 * TT], U32)
            pad_row = sb("pad_row", [P, ROW])
            pad_f = sb("pad_f", [P, E])
            pad_u = sb("pad_u", [P, E], U32)
            n_rows = sb("n_rows", [1, E])
            n_tiles = sb("n_tiles", [1, E])
            ends = sb("ends", [1, E])
            skip = sb("skip", [1, E])
            past = sb("past", [1, TILES + 1, E])
            past_skip = sb("past_skip", [1, TILES + 1, E])
            expert_f = sb("expert_f", [1, TILES + 1])
            row_f = sb("row_f", [1, TILES + 1])
            row_g = sb("row_g", [1, TILES + 1])
            logits = sb("logits", [P, TT, E])
            top8 = sb("top8", [P, TT, E])
            top8_at = sb("top8_at", [P, TT, E], U32)
            chosen = sb("chosen", [P, TT, 2])
            onehot = sb("onehot", [P, 2, TT, E])
            weighted = sb("weighted", [P, 2, TT, E])
            gap = sb("gap", [P, TT])
            egap = sb("egap", [P, TT])
            den = sb("den", [P, TT])
            w01 = sb("w01", [P, 2, TT])
            wts = sb("wts", [P, TT, E])
            wts_t = sb("wts_t", [E, L])
            xwo_loaded = sem("xwo_loaded")
            route_loaded = (sem("route_loaded0"), sem("route_loaded1"))
            (x1bo_ready, proj_ready, y2_ready, dve_route, moments2_ready, act_ln2, rstd2_ready, x2_ready, x2t_ready,
             x2t_copied, twin_ready, logits_z_ready, logits_ready, gap_ready, egap_ready, wts_ready, wts_t_ready,
             wts_t_copied, b2_ready, acc_ready) = (sem(n) for n in (
                 "x1bo_ready", "proj_ready", "y2_ready", "dve_route", "moments2_ready", "act_ln2", "rstd2_ready",
                 "x2_ready", "x2t_ready", "x2t_copied", "twin_ready", "logits_z_ready", "logits_ready", "gap_ready",
                 "egap_ready", "wts_ready", "wts_t_ready", "wts_t_copied", "b2_ready", "acc_ready"))
            ROUTE_STEPS = 28
            mask_ready, ranks_ready, slots_ready, numbered, pads_made, pads_ready, plan = (sem(n) for n in (
                "mask_ready", "ranks_ready", "slots_ready", "numbered", "pads_made", "pads_ready", "plan"))
            scattered = (sem("scattered0"), sem("scattered1"))
            pads_stored = sem("pads_stored")
            x2b_stored = sem("x2b_stored")

            with nc.Block() as block:
                @block.sync
                def _(sp):
                    sp.dma_start(xwo[:], a["xWo"].rearrange("g p d -> p g d")).then_inc(xwo_loaded, 16)
                    with sp.Fori(0, B // 2) as it:
                        for h in range(2):
                            b = 2 * it + h
                            sp.wait_ge(y2_ready, 2 * it)
                            sp.dma_start(at_in[:, h], attn_all.rearrange("(b g) p l -> b p g l", g=G)[b]) \
                                .then_inc(route_loaded[h], 16)
                            sp.dma_start(x1_in[:, h], x1_all[b].rearrange("(t p) d -> p t d", p=P)) \
                                .then_inc(route_loaded[h], 16)

                @block.gpsimd
                def _(pool):
                    with pool.Fori(0, B // 2) as it:
                        for h in range(2):
                            b = 2 * it + h
                            pool.wait_ge(route_loaded[h], 32 * (it + 1))
                            pool.tensor_tensor(x1_in[:, h], x1_in[:, h],
                                               rows[:, XBO:XBO + 1, :].to_broadcast([P, TT, D]), ALU.add) \
                                .then_inc(x1bo_ready, 1)
                            pool.wait_ge(scattered[h], 16 * 2 * TT * it)
                            pool.tensor_copy(rows_out[:, h, :, :, AT_DEST],
                                             dest_ids[:, :, bass.ds(b * TT, TT)]).then_inc(numbered, 1)
                            wait_alone(pool, (numbered, b + 1), (twin_ready, b + 1), (slots_ready, b + 1))
                            for i in range(2):
                                for t in range(TT):
                                    at = i * TT + t
                                    pool.indirect_dma_start(
                                        xs, bass.IndirectOffsetOnAxis(slot_u[:, h, at:at + 1], 0),
                                        rows_out[:, h, i, t, :], None).then_inc(scattered[h], 16)
                    pool.wait_ge(pads_ready, 1)
                    for e in range(E):
                        pool.indirect_dma_start(xs, bass.IndirectOffsetOnAxis(pad_u[:, e:e + 1], 0), pad_row[:], None) \
                            .then_inc(pads_stored, 16)
                    pool.dma_start(xs[NO_TILE:NO_TILE + P], pad_row[:]).then_inc(pads_stored, 16)
                    pool.wait_ge(pads_stored, 16 * (E + 1))
                    for h in range(2):
                        pool.wait_ge(scattered[h], 16 * TT * B)

                @block.tensor
                def _(pe):
                    pe.wait_ge(xwo_loaded, 16)
                    with pe.Fori(0, B // 2) as it:
                        for h in range(2):
                            b = 2 * it + h
                            pe.wait_ge(y2_ready, b)
                            pe.wait_ge(route_loaded[h], 32 * (it + 1))
                            for t in range(TT):
                                for g in range(G):
                                    last = pe.matmul(psum[:, t // 2, (t % 2) * D:(t % 2 + 1) * D],
                                                     at_in[:, h, g, t * P:(t + 1) * P], xwo[:, g, :],
                                                     start=g == 0, stop=g == G - 1)
                            last.then_inc(proj_ready, 1)
                            pe.wait_ge(x2t_copied, b)
                            pe.wait_ge(x2_ready, b + 1)
                            for k in range(C):
                                for t in range(TT):
                                    last = pe.transpose(psum[:, 2 + k, t * P:(t + 1) * P],
                                                        rows_out[:, h, 0, t, k * P:(k + 1) * P], ident[:])
                            last.then_inc(x2t_ready, 1)
                            pe.wait_ge(slots_ready, b)
                            pe.wait_ge(x2t_copied, b + 1)
                            for t in range(TT):
                                for k in range(C):
                                    last = pe.matmul(psum[:, 4, t * E:(t + 1) * E], x2t[:, k, t * P:(t + 1) * P],
                                                     router_w[:, k, :], start=k == 0, stop=k == C - 1)
                            last.then_inc(logits_z_ready, 1)
                            pe.wait_ge(mask_ready, b + 1)
                            pe.matmul(psum[:, 4, 64:64 + TT * E], before[:], mask[:].rearrange("p t e -> p (t e)"),
                                      start=True, stop=True)
                            pe.matmul(psum[:, 4, 128:128 + TT * E], ones[:], mask[:].rearrange("p t e -> p (t e)"),
                                      start=True, stop=True).then_inc(ranks_ready, 1)
                            pe.wait_ge(wts_t_copied, b)
                            pe.wait_ge(wts_ready, b + 1)
                            for t in range(TT):
                                last = pe.transpose(psum[0:E, 5, t * P:(t + 1) * P], wts[:, t, :], ident[:])
                            last.then_inc(wts_t_ready, 1)
                            pe.wait_ge(acc_ready, b)
                            pe.wait_ge(wts_t_copied, b + 1)
                            for t in range(TT):
                                last = pe.matmul(psum[:, 6 + t // 2, (t % 2) * D:(t % 2 + 1) * D],
                                                 wts_t[:, t * P:(t + 1) * P], b2_rows[:], start=True, stop=True)
                            last.then_inc(b2_ready, 1)

                @block.scalar
                def _(act):
                    with act.Fori(0, B // 2) as it:
                        for h in range(2):
                            b = 2 * it + h
                            act.wait_ge(moments2_ready, b + 1)
                            act.activation(rstd2_ln[:], moments2[:, :, 1], ACT.Ln, bias=eps_col[:]).then_inc(act_ln2, 1)
                            act.wait_ge(act_ln2, b + 1)
                            act.activation(rstd2[:], rstd2_ln[:], ACT.Exp, scale=-0.5).then_inc(rstd2_ready, 1)
                            act.wait_ge(logits_z_ready, b)
                            act.wait_ge(x2t_ready, b + 1)
                            act.activation(x2t[:], psum[:, 2:4], ACT.Copy).then_inc(x2t_copied, 1)
                            act.wait_ge(scattered[h], 16 * 2 * TT * it)
                            act.wait_ge(x2_ready, b + 1)
                            act.activation(rows_out[:, h, 1, :, 0:D], rows_out[:, h, 0, :, 0:D], ACT.Copy) \
                                .then_inc(twin_ready, 1)
                            act.wait_ge(gap_ready, b + 1)
                            act.activation(egap[:], gap[:], ACT.Exp).then_inc(egap_ready, 1)
                            act.wait_ge(b2_ready, b)
                            act.wait_ge(wts_t_ready, b + 1)
                            act.activation(wts_t[:], psum[0:E, 5], ACT.Copy).then_inc(wts_t_copied, 1)
                            act.wait_ge(acc_ready, b + 1)
                            act.dma_start(x2_all[b].rearrange("(t p) d -> p t d", p=P), x2b[:]).then_inc(x2b_stored, 16)
                    act.wait_ge(x2b_stored, 16 * B)

                @block.vector
                def _(v):
                    v.memset(pad_row[:], 0.0).then_inc(pads_made, 1)
                    v.tensor_copy(slot_at[:, 0], region_at[:])
                    v.wait_ge(pads_made, 1)
                    v.memset(pad_row[:, AT_DEST:AT_DEST + 1], float(NO_DEST)).then_inc(pads_made, 1)
                    with v.Fori(0, B // 2) as it:
                        for h in range(2):
                            b = 2 * it + h
                            step = Steps(ROUTE_STEPS * b)

                            def wide(t):
                                return t.rearrange("p t d -> p (t d)").rearrange("p (n f) -> p n f", n=2)

                            v.wait_ge(x1bo_ready, b + 1)
                            v.wait_ge(proj_ready, b + 1)
                            v.tensor_tensor(wide(y2[:]), psum[:, 0:2], wide(x1_in[:, h]), ALU.add).then_inc(y2_ready, 1)
                            v.wait_ge(y2_ready, b + 1)
                            for t in range(TT):
                                v.bn_stats(stats2[:, t], y2[:, t]).then_inc(dve_route, 1)
                                s = step.next()
                            wait_alone(v, (dve_route, s))
                            for t in range(TT):
                                last = v.bn_aggr(moments2[:, t], stats2[:, t])
                            last.then_inc(moments2_ready, 1)
                            v.wait_ge(x2t_ready, b)
                            v.wait_ge(scattered[h], 16 * 2 * TT * it)
                            v.wait_ge(moments2_ready, b + 1)
                            v.wait_ge(rstd2_ready, b + 1)
                            for t in range(TT):
                                last = v.tensor_scalar(rows_out[:, h, 0, t, 0:D], y2[:, t], moments2[:, t, 0:1], rstd2[:, t:t + 1],
                                                       ALU.subtract, ALU.mult)
                            last.then_inc(x2_ready, 1)
                            v.wait_ge(logits_z_ready, b + 1)
                            v.tensor_tensor(logits[:], psum[:, 4, 0:TT * E].rearrange("p (t e) -> p t e", t=TT),
                                            router_b[:].rearrange("p (o e) -> p o e", o=1).to_broadcast([P, TT, E]),
                                            ALU.add).then_inc(logits_ready, 1)
                            wait_alone(v, (logits_ready, b + 1))
                            for t in range(TT):
                                v.max(top8[:, t], logits[:, t]).then_inc(dve_route, 1)
                                s = step.next()
                            wait_alone(v, (dve_route, s))
                            for t in range(TT):
                                v.max_index(top8_at[:, t], top8[:, t], logits[:, t]).then_inc(dve_route, 1)
                                s = step.next()
                            v.tensor_tensor(gap[:], top8[:, :, 1], top8[:, :, 0], ALU.subtract).then_inc(gap_ready, 1)
                            v.wait_ge(dve_route, s)
                            v.tensor_copy(chosen[:], top8_at[:, :, 0:2]).then_inc(dve_route, 1)
                            s = step.next()
                            v.wait_ge(egap_ready, b + 1)
                            v.tensor_scalar(den[:], egap[:], 1.0, None, ALU.add).then_inc(dve_route, 1)
                            s1 = step.next()
                            v.wait_ge(dve_route, s)
                            for i in range(2):
                                v.tensor_tensor(onehot[:, i],
                                                iota8[:].rearrange("p (o e) -> p o e", o=1).to_broadcast([P, TT, E]),
                                                chosen[:, :, i:i + 1].to_broadcast([P, TT, E]), ALU.is_equal) \
                                    .then_inc(dve_route, 1)
                                s2 = step.next()
                            v.wait_ge(dve_route, s2)
                            v.tensor_tensor(mask[:], onehot[:, 0], onehot[:, 1], ALU.add).then_inc(mask_ready, 1)
                            v.wait_ge(dve_route, s1)
                            v.reciprocal(w01[:, 0], den[:]).then_inc(dve_route, 1)
                            s = step.next()
                            v.wait_ge(dve_route, s)
                            v.tensor_tensor(w01[:, 1], w01[:, 0], egap[:], ALU.mult).then_inc(dve_route, 1)
                            s = step.next()
                            v.wait_ge(dve_route, s)
                            v.tensor_copy(rows_out[:, h, :, :, AT_WEIGHT], w01[:])
                            for i in range(2):
                                v.tensor_tensor(weighted[:, i], onehot[:, i],
                                                w01[:, i].rearrange("p (t o) -> p t o", o=1).to_broadcast([P, TT, E]),
                                                ALU.mult).then_inc(dve_route, 1)
                                s = step.next()
                            v.wait_ge(dve_route, s)
                            v.tensor_tensor(wts[:], weighted[:, 0], weighted[:, 1], ALU.add).then_inc(wts_ready, 1)
                            v.wait_ge(ranks_ready, b + 1)
                            for t in range(TT):
                                v.tensor_tensor(slot_at[:, t + 1], slot_at[:, t],
                                                psum[:, 4, 128 + t * E:128 + (t + 1) * E], ALU.add).then_inc(dve_route, 1)
                                s = step.next()
                                v.wait_ge(dve_route, s)
                            v.tensor_tensor(slot_of[:], slot_at[:, 0:TT],
                                            psum[:, 4, 64:64 + TT * E].rearrange("p (t e) -> p t e", t=TT), ALU.add) \
                                .then_inc(dve_route, 1)
                            s = step.next()
                            v.wait_ge(dve_route, s)
                            v.tensor_copy(slot_at[:, 0], slot_at[:, TT]).then_inc(dve_route, 1)
                            step.next()
                            for i in range(2):
                                last = v.tensor_tensor(slot_own[:, i], onehot[:, i], slot_of[:], ALU.mult)
                            last.then_inc(dve_route, 1)
                            s = step.next()
                            v.wait_ge(dve_route, s)
                            v.tensor_reduce(slot_f[:], slot_own[:].rearrange("p i t e -> p (i t) e"), AX_X, ALU.add) \
                                .then_inc(dve_route, 1)
                            s = step.next()
                            v.wait_ge(dve_route, s)
                            v.tensor_copy(slot_u[:, h], slot_f[:]).then_inc(slots_ready, 1)
                            v.wait_ge(b2_ready, b + 1)
                            v.wait_ge(x2b_stored, 16 * b)
                            v.tensor_tensor(x2b[:],
                                            psum[:, 6:8].rearrange("p n (t d) -> p (n t) d", t=2),
                                            rows_out[:, h, 0, :, 0:D], ALU.add).then_inc(acc_ready, 1)
                            assert step.n == ROUTE_STEPS, step.n

                    plans = Steps(0)

                    def planned(last):
                        last.then_inc(plan, 1)
                        v.wait_ge(plan, plans.next())

                    planned(v.tensor_tensor(pad_f[:], slot_at[:, 0], own_row[:].to_broadcast([P, E]), ALU.add))
                    v.tensor_copy(pad_u[:], pad_f[:]).then_inc(pads_ready, 1)
                    planned(v.tensor_tensor(n_rows[:], slot_at[0:1, 0], region_at[0:1], ALU.subtract))
                    planned(v.tensor_scalar(n_rows[:], n_rows[:], (P - 1) / 2, 1.0 / P, ALU.add, ALU.mult))
                    planned(v.tensor_scalar(n_rows[:], n_rows[:], ROUND, None, ALU.add))
                    planned(v.tensor_scalar(n_tiles[:], n_rows[:], -ROUND, None, ALU.add))
                    planned(v.tensor_tensor_scan(ends[:], n_tiles[:], n_tiles[:], 0.0, ALU.add, ALU.bypass))
                    planned(v.tensor_scalar(skip[:], n_tiles[:], -float(P), float(REGION), ALU.mult, ALU.add))
                    each = [1, TILES + 1, E]
                    planned(v.tensor_tensor(past[:], ends[:].rearrange("p (o e) -> p o e", o=1).to_broadcast(each),
                                            tile_no[:].rearrange("p (j o) -> p j o", o=1).to_broadcast(each), ALU.is_le))
                    planned(v.tensor_tensor(past_skip[:], past[:],
                                            skip[:].rearrange("p (o e) -> p o e", o=1).to_broadcast(each), ALU.mult))
                    v.tensor_reduce(expert_f[:], past[:], AX_X, ALU.add)
                    planned(v.tensor_reduce(row_f[:], past_skip[:], AX_X, ALU.add))
                    planned(v.scalar_tensor_tensor(row_g[:], tile_no[:], float(P), row_f[:], ALU.mult, ALU.add))
                    v.tensor_scalar(tile_row[:], row_g[:], float(NO_TILE), None, ALU.min)
                    v.tensor_scalar(tile_expert[:], expert_f[:], float(E - 1), None, ALU.min)

        with ExitStack() as ctx:
            sb = tensors(ctx)
            rows_in = sb("rows_in", [P, 2, ROW])
            xst = sb("xst", [P, 2, C, P])
            dest = sb("dest", [P, 2, 1], U32)
            weight = sb("weight", [P, 2, 1])
            w1 = sb("w1", [P, 2, C, HID])
            w2 = sb("w2", [P, 2, HC, D])
            b1 = sb("b1", [P, 2, HC])
            hid = sb("hid", [P, 2, HC, P])
            y_out = sb("y_out", [P, 2, D])
            rows_loaded = (sem("rows_loaded0"), sem("rows_loaded1"))
            y_scattered = (sem("y_scattered0"), sem("y_scattered1"))
            xs_t_ready, xst_copied, w1_ready, w2_ready, mm1_done, h_ready, mm2_done, y_scaled = (sem(n) for n in (
                "xs_t_ready", "xst_copied", "w1_ready", "w2_ready", "mm1_done", "h_ready", "mm2_done", "y_scaled"))

            with nc.Block() as block:
                @block.sync
                def _(sp):
                    def load(j, n, h):
                        row = sp.value_load(tile_row[0:1, j], min_val=0, max_val=NO_TILE)
                        sp.dma_start(rows_in[:, h], xs[bass.ds(row, P)]).then_inc(rows_loaded[h], 16)

                    load(slice(0, 1), 0, 0)
                    with sp.Fori(0, TILES // 2) as it:
                        for h in range(2):
                            n = 2 * it + h + 1
                            sp.wait_ge(xst_copied, n)
                            load(bass.ds(n, 1), n, 1 - h)

                @block.tensor
                def _(pe):
                    def turn(half, count):
                        pe.wait_ge(rows_loaded[half], count)
                        for k in range(C):
                            last = pe.transpose(psum[:, half, k * P:(k + 1) * P],
                                                rows_in[:, half, k * P:(k + 1) * P], ident[:])
                        last.then_inc(xs_t_ready, 1)

                    turn(0, 16)
                    with pe.Fori(0, TILES // 2) as it:
                        for h in range(2):
                            n = 2 * it + h
                            pe.wait_ge(xst_copied, n + 2)
                            turn(1 - h, 16 * (it + 1 + h))
                            pe.wait_ge(w1_ready, n + 1)
                            for c in range(HC):
                                for k in range(C):
                                    last = pe.matmul(psum[:, 2 + 2 * h + c // 4, (c % 4) * P:(c % 4 + 1) * P],
                                                     w1[:, h, k, c * P:(c + 1) * P], xst[:, h, k, :],
                                                     start=k == 0, stop=k == C - 1)
                                if c % 4 == 3:
                                    last.then_inc(mm1_done, 1)
                            pe.wait_ge(w2_ready, n + 1)
                            pe.wait_ge(y_scaled, n)
                            for c in range(HC):
                                pe.wait_ge(h_ready, HC * n + c + 1)
                                last = pe.matmul(psum[:, 6 + h, 0:D], hid[:, h, c, :], w2[:, h, c, :],
                                                 start=c == 0, stop=c == HC - 1)
                            last.then_inc(mm2_done, 1)

                @block.scalar
                def _(act):
                    with act.Fori(0, TILES // 2) as it:
                        for h in range(2):
                            n = 2 * it + h
                            if h:
                                act.wait_ge(mm2_done, n - 1)
                            else:
                                act.wait_ge(mm2_done, n)
                            for c in range(HC):
                                act.wait_ge(mm1_done, HC // 4 * n + c // 4 + 1)
                                act.activation(hid[:, h, c], psum[:, 2 + 2 * h + c // 4, (c % 4) * P:(c % 4 + 1) * P],
                                               ACT.Relu, bias=b1[:, h, c:c + 1]).then_inc(h_ready, 1)

                @block.gpsimd
                def _(pool):
                    with pool.Fori(0, TILES // 2) as it:
                        for h in range(2):
                            n = 2 * it + h
                            wait_alone(pool, (y_scaled, n + 2))
                            pool.indirect_dma_start(y_all, bass.IndirectOffsetOnAxis(dest[:, h, :], 0), y_out[:, h], None,
                                                    bounds_check=2 * TOKENS - 1, oob_is_err=False) \
                                .then_inc(y_scattered[h], 16)
                    for h in range(2):
                        pool.wait_ge(y_scattered[h], 16 * TILES // 2)

                @block.vector
                def _(v):
                    def weights(j, half):
                        e = v.value_load(tile_expert[0:1, j], min_val=0, max_val=E - 1)
                        at = bass.ds(e, 1)
                        v.tensor_copy(b1[:, half], b1_cols[:, at, :].rearrange("p o c -> p (o c)"))
                        v.tensor_copy(w1[:, half], w1_all[:, at].rearrange("p o c h -> p (o c) h")).then_inc(w1_ready, 1)
                        v.tensor_copy(w2[:, half], w2_all[:, at].rearrange("p o c d -> p (o c) d")).then_inc(w2_ready, 1)

                    def take_rows(half):
                        v.tensor_copy(dest[:, half], rows_in[:, half, AT_DEST:AT_DEST + 1])
                        v.tensor_copy(weight[:, half], rows_in[:, half, AT_WEIGHT:AT_WEIGHT + 1])
                        v.tensor_copy(xst[:, half].rearrange("p c t -> p (c t)"), psum[:, half, 0:C * P]) \
                            .then_inc(xst_copied, 1)

                    v.wait_ge(ffn_loaded, 32 * E)
                    v.sem_inc(y_scaled, 1)
                    v.sem_inc(xst_copied, 1)
                    v.wait_ge(xs_t_ready, 1)
                    take_rows(0)
                    weights(slice(0, 1), 0)
                    with v.Fori(0, TILES // 2) as it:
                        for h in range(2):
                            n = 2 * it + h
                            v.wait_ge(y_scattered[1 - h], 16 * (it + h))
                            v.wait_ge(mm1_done, HC // 4 * n)
                            v.wait_ge(xs_t_ready, n + 2)
                            take_rows(1 - h)
                            v.wait_ge(mm2_done, n)
                            weights(bass.ds(n + 1, 1), 1 - h)
                            v.wait_ge(y_scattered[h], 16 * it)
                            v.wait_ge(mm2_done, n + 1)
                            v.tensor_scalar(y_out[:, h], psum[:, 6 + h, 0:D], weight[:, h], None, ALU.mult) \
                                .then_inc(y_scaled, 1)

        with ExitStack() as ctx:
            sb = tensors(ctx)
            y_in = sb("y_in", [P, 2, 2, TT, D])
            x2_in = sb("x2_in", [P, 2, TT, D])
            y_pair = sb("y_pair", [P, TT, D])
            y3 = sb("y3", [P, 2, TT, D])
            stats3 = sb("stats3", [P, TT, 6])
            moments3 = sb("moments3", [P, 2, TT, 2])
            rstd3_ln = sb("rstd3_ln", [P, TT])
            rstd3 = sb("rstd3", [P, 2, TT])
            y_loaded = (sem("y_loaded0"), sem("y_loaded1"))
            out_stored = (sem("out_stored0"), sem("out_stored1"))
            pair_ready, y3_ready, stats3_ready, moments3_ready, act_ln3, rstd3_ready, out_ready = (sem(n) for n in (
                "pair_ready", "y3_ready", "stats3_ready", "moments3_ready", "act_ln3", "rstd3_ready", "out_ready"))
            with nc.Block() as block:
                @block.sync
                def _(sp):
                    with sp.Fori(0, B // 2) as it:
                        for h in range(2):
                            b = 2 * it + h
                            if h:
                                sp.wait_ge(pair_ready, b - 1)
                            else:
                                sp.wait_ge(pair_ready, b)
                            for i in range(2):
                                sp.dma_start(y_in[:, h, i],
                                             y_all.rearrange("(i b t p) d -> i b p t d", i=2, b=B, p=P)[i, b]) \
                                    .then_inc(y_loaded[h], 16)
                            sp.wait_ge(y3_ready, b)
                            sp.dma_start(x2_in[:, h], x2_all[b].rearrange("(t p) d -> p t d", p=P)) \
                                .then_inc(y_loaded[h], 16)

                @block.gpsimd
                def _(pool):
                    with pool.Fori(0, B // 2) as it:
                        for h in range(2):
                            b = 2 * it + h
                            pool.wait_ge(y3_ready, b + 1)
                            pool.wait_ge(y_loaded[h], 48 * (it + 1))
                            pool.tensor_tensor(y_pair[:], y_in[:, h, 0], y_in[:, h, 1], ALU.add).then_inc(pair_ready, 1)

                @block.vector
                def _(v):
                    v.sem_inc(y3_ready, 1)
                    with v.Fori(0, B // 2) as it:
                        for h in range(2):
                            b = 2 * it + h
                            v.wait_ge(out_stored[h], 16 * it)
                            v.wait_ge(pair_ready, b + 1)
                            v.tensor_tensor(y3[:, h], x2_in[:, h], y_pair[:], ALU.add) \
                                .then_inc(y3_ready, 1)
                            wait_alone(v, (y3_ready, b + 2))
                            for t in range(TT):
                                last = v.bn_stats(stats3[:, t], y3[:, h, t])
                            last.then_inc(stats3_ready, 1)
                            wait_alone(v, (stats3_ready, b + 1))
                            for t in range(TT):
                                last = v.bn_aggr(moments3[:, h, t], stats3[:, t])
                            last.then_inc(moments3_ready, 1)
                            v.wait_ge(moments3_ready, b + 1)
                            v.wait_ge(rstd3_ready, b + 1)
                            for t in range(TT):
                                last = v.tensor_scalar(y3[:, h, t], y3[:, h, t], moments3[:, h, t, 0:1],
                                                       rstd3[:, h, t:t + 1], ALU.subtract, ALU.mult)
                            last.then_inc(out_ready, 1)

                @block.scalar
                def _(act):
                    with act.Fori(0, B // 2) as it:
                        for h in range(2):
                            b = 2 * it + h
                            act.wait_ge(moments3_ready, b + 1)
                            act.activation(rstd3_ln[:], moments3[:, h, :, 1], ACT.Ln, bias=eps_col[:]).then_inc(act_ln3, 1)
                            act.wait_ge(act_ln3, b + 1)
                            act.activation(rstd3[:, h], rstd3_ln[:], ACT.Exp, scale=-0.5).then_inc(rstd3_ready, 1)
                            act.wait_ge(out_ready, b + 1)
                            act.dma_start(out[b].rearrange("(t p) d -> p t d", p=P), y3[:, h]) \
                                .then_inc(out_stored[h], 16)
                    for h in range(2):
                        act.wait_ge(out_stored[h], 16 * B // 2)


def _columns(*vectors):
    import numpy as np
    return np.ascontiguousarray(np.concatenate([v.reshape(-1, P).T for v in vectors], axis=1))


def kernel(**inputs):
    import numpy as np
    import concourse.bacc as bacc
    from concourse.bass_utils import run_bass_kernel_spmd

    w = {k: np.asarray(v) for k, v in inputs.items()}
    x, ctx = w["x"], w["ctx_1024"]
    B, L, D = x.shape
    S = ctx.shape[1]
    padded = -(-S // P) * P
    m, t, f = "L0_attn_", "L0_xattn_", "L0_ffn_"
    one = lambda v, i=0: np.repeat(v[i:i + 1], P)
    ctx_p = np.zeros((B, padded, D), ctx.dtype)
    ctx_p[:, :S] = ctx
    wo = w[t + "Wo"].reshape(4, 4, D // 16, D)
    wo_p = np.zeros((4, 4, 32, D), wo.dtype)
    wo_p[:, :, :D // 16] = wo
    E, TT = w[f + "W1"].shape[0], L // P
    tokens = np.arange(B * L, dtype=np.float32).reshape(B * TT, P).T
    arrays = {
        "before": np.triu(np.ones((P, P), np.float32), 1),
        "dest_ids": np.stack([tokens, tokens + B * L], axis=1),
        "region_at": np.tile(np.arange(E, dtype=np.float32) * (B * L + P), (P, 1)),
        "own_row": np.arange(P, dtype=np.float32)[:, None],
        "tile_no": np.arange(2 * B * TT + E + 1, dtype=np.float32)[None],
        "x": x,
        "xT": x.transpose(0, 2, 1).reshape(B, D // P, P, L),
        "ctxT": ctx_p.transpose(0, 2, 1).reshape(B, D // P, P, padded),
        "posT": w[m + "pos_phases"][:L].T,
        "cols": _columns(w[m + "bpv"], w[m + "bk"], w[m + "bkv"], w[m + "bg1"], w[m + "ln_g"], w[m + "ln_b"],
                         w[t + "bq"], w[t + "bk"], w[m + "bb1"], one(w[m + "bg2"]), one(w[m + "bb2"], 0),
                         one(w[m + "bb2"], 1), w[m + "Wg2"], w[m + "Wb2"].T),
        "rows": np.stack([w[m + "bo"], w[t + "bo"], w[t + "bv"], w[t + "bv"]]),
        "Wpv": w[m + "Wpv"], "Wk": w[m + "Wk"], "Wkv": w[m + "Wkv"], "Wg1": w[m + "Wg1"],
        "Wb1": w[m + "Wb1"], "Wo": w[m + "Wo"],
        "xWq": w[t + "Wq"], "xWk": w[t + "Wk"], "xWv": w[t + "Wv"], "xWo": wo_p.reshape(4, P, D),
        "Wr": w[f + "Wr"], "br": w[f + "br"], "W1": w[f + "W1"], "W2": w[f + "W2"],
        "b1T": w[f + "b1"].reshape(w[f + "b1"].shape[0], -1, P).transpose(2, 0, 1), "b2": w[f + "b2"],
    }
    arrays = {f"in_{n}": np.ascontiguousarray(v) for n, v in arrays.items()}
    nc = bacc.Bacc("TRN2", target_bir_lowering=False, num_devices=1)
    a = {n[3:]: nc.dram_tensor(n, v.shape, mybir.dt.from_np(v.dtype), kind="ExternalInput").ap()
         for n, v in arrays.items()}
    a["S_REAL"] = S
    out = nc.dram_tensor("out", [B, L, D], F32, kind="ExternalOutput").ap()
    decoder_layer(nc, a, out)
    r = run_bass_kernel_spmd(nc, [arrays], core_ids=[0])
    return r.results[0]["out"]
```

```python
import math
from contextlib import ExitStack

import concourse.bass as bass
from concourse import mybir

P = 128
F32 = mybir.dt.float32
BF16 = mybir.dt.bfloat16
U32 = mybir.dt.uint32
I32 = mybir.dt.int32
ALU = mybir.AluOpType
ACT = mybir.ActivationFunctionType
AX_X = mybir.AxisListType.X


class Steps:

    def __init__(self, before):
        self.before, self.n = before, 0

    def next(self):
        self.n += 1
        return self.before + self.n


def last_user(k, buffer_of):
    same = [p for p, buf in enumerate(buffer_of) if buf == buffer_of[k]]
    before = [p for p in same if p < k]
    return (0, before[-1]) if before else (-1, same[-1])


def decoder_layer(nc, a, out):
    B, L, D = a["x"].shape
    SU = a["ctxT"].shape[-1]
    S_REAL = a["S_REAL"]
    H = 16
    DH = D // H
    C = D // P
    TT = L // P
    E = a["W1"].shape[0]
    HID = a["W1"].shape[-1]
    HC = HID // P
    GH = 4
    G = H // GH
    NG = B * G
    ST = -(-S_REAL // P)
    TAIL = S_REAL - (ST - 1) * P
    UT = SU // P
    UNITS, FIRST_UNITS = 2 * B, 3
    KC = SU // 2
    PARTS = 3
    Q_SLOTS = (0, 0, 1, 1, 0, 2)
    K_SLOTS = (0, 1, 0, 1, 2, 0)
    STACK = DH * len(Q_SLOTS)
    PAD = 32
    TWO_PI = 2 * math.pi
    TWO_PI_HI = 6.28125
    ROUND = 1.5 * 2.0 ** 23
    PI_DOWN = 3.1415925
    EPS = 1e-5
    SCALE = 1.0 / math.sqrt(DH)
    ROOT_D = math.sqrt(D)
    assert C == 2 and TT == 4 and B % 2 == 0 and G == 4 and E == 8 and B == E

    q_parts = nc.dram_tensor("q_parts", [PARTS, B, D, L], BF16, kind="Internal").ap()
    k_parts = nc.dram_tensor("k_parts", [PARTS, UNITS, D, SU], BF16, kind="Internal").ap()
    v_all = nc.dram_tensor("v_all", [UNITS, G, P, UT * GH * DH], F32, kind="Internal").ap()
    attn_all = nc.dram_tensor("attn_all", [NG, P, L], F32, kind="Internal").ap()
    ROW = D + 2
    AT_DEST, AT_WEIGHT = D, D + 1
    TOKENS = B * L
    REGION = TOKENS + P
    NO_DEST = 4 * TOKENS
    NO_TILE = E * REGION
    TILES = 2 * TOKENS // P + E
    xs = nc.dram_tensor("xs", [E * REGION + P, ROW], F32, kind="Internal").ap()
    y_all = nc.dram_tensor("y_all", [2 * TOKENS, D], F32, kind="Internal").ap()
    x2_all = nc.dram_tensor("x2_all", [B, L, D], F32, kind="Internal").ap()
    x1_all = nc.dram_tensor("x1_all", [B, L, D], F32, kind="Internal").ap()

    with ExitStack() as top:
        def sem(name):
            return top.enter_context(nc.semaphore(name))

        def tensors(ctx):
            def sb(name, shape, dt=F32):
                return ctx.enter_context(nc.sbuf_tensor(name, shape, dt))
            return sb

        psum = top.enter_context(nc.psum_tensor("psum", [P, 8, 512], F32))

        sb = tensors(top)
        ident = sb("ident", [P, P])
        mean_w = sb("mean_w", [P, P])
        eps_col = sb("eps_col", [P, 1])
        half_pi = sb("half_pi", [P, 1])
        cols = sb("cols", [P, a["cols"].shape[-1]])
        rows = sb("rows", [P, 4, D])
        iota8 = sb("iota8", [P, E])
        router_w = sb("router_w", [P, C, E])
        router_b = sb("router_b", [P, E])
        b1_cols = sb("b1_cols", [P, E, HC])
        b2_rows = sb("b2_rows", [E, D])
        before = sb("before", [P, P])
        ones = sb("ones", [P, P])
        dest_ids = sb("dest_ids", [P, 2, B * TT])
        region_at = sb("region_at", [P, E])
        own_row = sb("own_row", [P, 1])
        tile_no = sb("tile_no", [1, TILES + 1])

        def col(i):
            return cols[:, i:i + 1]

        BPV, BK, BKV, BG1, LNG, LNB, BQ, XBK = (2 * i for i in range(8))
        BB1, BG2, BW_A, BW_B, WG2, WB2 = 16, 17, 18, 19, 20, 22
        BO, XBO, XBV, _ = range(4)

        consts_loaded = sem("consts_loaded")
        N_CONSTS = 0
        consts_made = sem("consts_made")
        ident_zeroed = sem("ident_zeroed")
        derived_ready = sem("derived_ready")

        def wait_alone(eng, *waits):
            waits = [(s, n) for s, n in waits if not isinstance(n, int) or n > 0]
            for _, n in waits:
                if not isinstance(n, int):
                    eng.to_reg(n)
            eng.wait_ge(consts_made, 1)
            for s, n in waits:
                eng.wait_ge(s, n)

        def wait(eng, s, n):
            if not isinstance(n, int) or n > 0:
                eng.wait_ge(s, n)

        OPEN = 1

        def opened(eng, *sems):
            for s in sems:
                eng.sem_inc(s, OPEN)

        OPEN = 1

        def opened(eng, *sems):
            for s in sems:
                eng.sem_inc(s, OPEN)

        xwk, xwv = sb("xwk", [P, C, D]), sb("xwv", [P, C, D])
        neg_bk = sb("neg_bk", [P, C])

        with ExitStack() as ctx:
            sb = tensors(ctx)
            wpv, wk, wkv, wo, wq = (sb(n, [P, C, D]) for n in ("wpv", "wk", "wkv", "wo", "wq"))
            wg1 = sb("wg1", [P, 2 * C, D])
            wb1 = sb("wb1", [P, C, P])
            wg2_wide = sb("wg2_wide", [P, C, P])
            wb2_wide = sb("wb2_wide", [P, P])
            mcols = sb("mcols", [P, 4])
            pos = sb("pos", [P, C, L])
            turns = sb("turns", [P, C, L])
            pos_cos = sb("pos_cos", [P, C, L])
            pos_sin = sb("pos_sin", [P, C, L])
            xt = sb("xt", [P, 2, C, L + 1])
            xin = sb("xin", [P, 2, TT, D])
            x2bo = sb("x2bo", [P, TT, D])
            phase = sb("phase", [P, C, L])
            phase_abs = sb("phase_abs", [P, C, L])
            key_cos = sb("key_cos", [P, C, L + 1])
            key_sin = sb("key_sin", [P, C, L + 1])
            gate_h = sb("gate_h", [P, C, L])
            blend_h = sb("blend_h", [P, L])
            gate_t = sb("gate_t", [P, L])
            gate = sb("gate", [P, L])
            gate_sum = sb("gate_sum", [P, L])
            gate_ln = sb("gate_ln", [P, L])
            gate_rs = sb("gate_rs", [P, L])
            below_max = sb("below_max", [P, 2, L])
            bexp = sb("bexp", [P, 2, L])
            bsum = sb("bsum", [P, L])
            bsum_ln = sb("bsum_ln", [P, L])
            bsum_r = sb("bsum_r", [P, L])
            bw = sb("bw", [P, 2, L])
            kv_w = sb("kv_w", [P, L])
            mem_c = sb("mem_c", [P, C, L])
            mem_s = sb("mem_s", [P, C, L])
            pos_ret = sb("pos_ret", [P, C, L])
            kvg = sb("kvg", [P, C, L])
            blended = sb("blended", [P, C, L])
            centred = sb("centred", [P, C, L])
            squares = turns
            var_ln = sb("var_ln", [P, L])
            rstd_b = sb("rstd_b", [P, L])
            normed = centred
            ln_t = sb("ln_t", [P, C, L])
            y = sb("y", [P, TT, D])
            stats = sb("stats", [P, TT, 6])
            moments = sb("moments", [P, TT, 2])
            rstd_ln = sb("rstd_ln", [P, TT])
            rstd = sb("rstd", [P, TT])
            x1 = sb("x1", [P, TT, D])
            x1t = sb("x1t", [P, C, L])
            q_f = sb("q_f", [P, C, L])
            q_rest = sb("q_rest", [P, C, L])
            q_out = sb("q_out", [P, PARTS, C, L], BF16)

            (xt_loaded0, xt_loaded1, pos_ready, trig_ready, pv_ready, kz_ready, gh_ready, bh_ready,
             gate_z_ready, kv_ready, bw_z_ready, mean_ready, var_ready, mix_out_ready, x1t_ready,
             q_ready) = (sem(n) for n in (
                 "xt_loaded0", "xt_loaded1", "pos_ready", "trig_ready", "pv_ready", "kz_ready",
                 "gh_ready", "bh_ready", "gate_z_ready", "kv_ready", "bw_z_ready", "mean_ready",
                 "var_ready", "mix_out_ready", "x1t_ready", "q_ready"))
            xt_loaded = (xt_loaded0, xt_loaded1)
            (phase_ready, gate_h_ready, blend_h_ready, gate_t_ready, key_trig_ready, act_abs, bexp_ready,
             bsum_r_ready, gate_rs_ready, act_ln, squares_ready, rstd_b_ready, ln_ready, rstd_ready,
             x1t_copied, q_copied) = (sem(n) for n in (
                 "phase_ready", "gate_h_ready", "blend_h_ready", "gate_t_ready", "key_trig_ready",
                 "act_abs", "bexp_ready", "bsum_r_ready", "gate_rs_ready", "act_ln",
                 "squares_ready", "rstd_b_ready", "ln_ready", "rstd_ready", "x1t_copied", "q_copied"))
            (dve_pos, dve_mix, pv_used, below_max_ready, gate_sum_ready, bsum_ready, kv_used,
             blended_ready, centred_ready, normed_ready, moments_ready, x1_ready) = (
                 sem(n) for n in ("dve_pos", "dve_mix", "pv_used", "below_max_ready",
                                  "gate_sum_ready", "bsum_ready", "kv_used", "blended_ready",
                                  "centred_ready", "normed_ready", "moments_ready", "x1_ready"))
            x_bo_ready = sem("x_bo_ready")
            dve_front, dve_end, gate_ln_ready, bsum_ln_ready, mid_ln, end_ln = (sem(n) for n in (
                "dve_front", "dve_end", "gate_ln_ready", "bsum_ln_ready", "mid_ln", "end_ln"))
            x2bo_ready, pool_split, q_split, q_stored, x1_stored, y_ready = (
                sem(n) for n in ("x2bo_ready", "pool_split", "q_split", "q_stored", "x1_stored", "y_ready"))

            consts = [
                (cols[:], a["cols"]),
                (rows[:], a["rows"].rearrange("(o n) d -> o n d", o=1).to_broadcast([P, 4, D])),
                (router_w[:], a["Wr"].rearrange("(c p) e -> p c e", p=P)),
                (router_b[:], a["br"].rearrange("(o e) -> o e", o=1).to_broadcast([P, E])),
                (b1_cols[:], a["b1T"]),
                (b2_rows[:], a["b2"]),
                (before[:], a["before"]),
                (dest_ids[:], a["dest_ids"]),
                (region_at[:], a["region_at"]),
                (own_row[:], a["own_row"]),
                (tile_no[:], a["tile_no"]),
                (wg1[:], a["Wg1"].rearrange("(c p) d -> p c d", p=P)),
                (wb1[:], a["Wb1"].rearrange("(c p) d -> p c d", p=P)),
                (pos[:], a["posT"].rearrange("(c p) l -> p c l", p=P)),
            ] + [(t[:], a[n].rearrange("(c p) d -> p c d", p=P)) for t, n in (
                (wpv, "Wpv"), (wk, "Wk"), (wkv, "Wkv"), (wo, "Wo"), (wq, "xWq"))]
            N_CONSTS = 16 * len(consts)

            ct = sb("ct", [P, 2, C, SU])
            K_BUFS = 2 * C
            k_f = [t[:, i, 0:KC] for t in (mem_c, mem_s) for i in range(C)]
            k_rest = [t[:, i, 0:KC] for t in (pos_ret, kvg) for i in range(C)]
            k_out = sb("k_out", [P, K_BUFS, PARTS, KC], BF16)
            v_out = sb("v_out", [P, G, UT, GH * DH])
            xw_loaded, neg_bk_ready, kp_ready, k_copied, k_hi, k_mid, k_rest_ready, k_split = (
                sem(n) for n in ("xw_loaded", "neg_bk_ready", "kp_ready", "k_copied", "k_hi", "k_mid",
                                 "k_rest_ready", "k_split"))
            ct_loaded = (sem("ct_loaded0"), sem("ct_loaded1"))
            k_stored = [sem(f"k_stored{i}") for i in range(K_BUFS)]
            v_stored = sem("v_stored")
            vp_ready, v_copied = sem("vp_ready"), sem("v_copied")
            KJ = 2 * C
            VJ = (UT + 1) // 2

            def first_units_sp(sp):
                sp.dma_start(xwk[:], a["xWk"].rearrange("(c p) d -> p c d", p=P)).then_inc(xw_loaded, 16)
                sp.dma_start(xwv[:], a["xWv"].rearrange("(c p) d -> p c d", p=P)).then_inc(xw_loaded, 16)
                for u in range(FIRST_UNITS):
                    it, h = divmod(u, 2)
                    wait(sp, v_copied, VJ * u)
                    sp.dma_start(ct[:, h], a["ctxT"][u].rearrange("c p s -> p c s")) \
                        .then_inc(ct_loaded[h], 16)

            def first_units_pe(pe):
                pe.wait_ge(xw_loaded, 32)
                for u in range(FIRST_UNITS):
                    it, h = divmod(u, 2)
                    pe.wait_ge(ct_loaded[h], 16 * (it + 1))
                    for j in range(KJ):
                        co, s0 = j // 2, (j % 2) * KC
                        for k in range(C):
                            last = pe.matmul(psum[:, j % 4, 0:KC], xwk[:, k, co * P:(co + 1) * P],
                                             ct[:, h, k, s0:s0 + KC], start=k == 0, stop=k == C - 1)
                        last.then_inc(kp_ready, 1)
                    for j in range(VJ):
                        if j >= 4:
                            pe.wait_ge(v_copied, VJ * (u + 1) + j - 3)
                        for t in range(2 * j, min(2 * j + 2, UT)):
                            for k in range(C):
                                last = pe.matmul(psum[:, 4 + j % 4, (t % 2) * D:(t % 2 + 1) * D],
                                                 ct[:, h, k, t * P:(t + 1) * P], xwv[:, k, :],
                                                 start=k == 0, stop=k == C - 1)
                        last.then_inc(vp_ready, 1)
                    pe.wait_ge(k_copied, KJ * (u + 1))
                    pe.wait_ge(v_copied, VJ * (u + 2))

            def first_units_act(act):
                act.wait_ge(neg_bk_ready, 1)
                act.wait_ge(blended_ready, B)
                for u in range(FIRST_UNITS):
                    it, h = divmod(u, 2)

                    def middle(j):
                        act.wait_ge(k_rest_ready, KJ * u + j + 1)
                        act.activation(k_out[:, j % K_BUFS, 1], k_rest[j % K_BUFS], ACT.Copy) \
                            .then_inc(k_mid, 1)

                    for j in range(KJ):
                        kb = j % K_BUFS
                        act.wait_ge(k_split, KJ * u + j - K_BUFS + 1 + K_BUFS)
                        act.wait_ge(kp_ready, KJ * u + j + 1)
                        act.activation(k_f[kb], psum[:, j % 4, 0:KC], ACT.Identity,
                                       bias=neg_bk[:, j // 2:j // 2 + 1], scale=-SCALE).then_inc(k_copied, 1)
                        wait(act, k_stored[kb], 16 * (KJ // K_BUFS * u + j // K_BUFS))
                        act.wait_ge(k_copied, KJ * u + j + 1)
                        act.activation(k_out[:, kb, 0], k_f[kb], ACT.Copy).then_inc(k_hi, 1)
                        if j:
                            middle(j - 1)
                    middle(KJ - 1)

            def first_units_pool(pool):
                for u in range(FIRST_UNITS):
                    it, h = divmod(u, 2)
                    for j in range(KJ):
                        kb = j % K_BUFS
                        pool.wait_ge(k_mid, KJ * u + j + 1)
                        pool.tensor_tensor(k_out[:, kb, 2], k_rest[kb], k_out[:, kb, 1],
                                           ALU.subtract).then_inc(k_split, 1)
                        wait_alone(pool, (k_split, KJ * u + j + 1 + K_BUFS))
                        co, s0 = j // 2, (j % 2) * KC
                        pool.dma_start(
                            k_parts[:, u, co * P:(co + 1) * P, s0:s0 + KC].rearrange("n p s -> p n s"),
                            k_out[:, kb]).then_inc(k_stored[kb], 16)
                    wait_alone(pool, (v_copied, VJ * (u + 2)))
                    pool.dma_start(v_all[u].rearrange("g p f -> p g f"),
                                   v_out[:].rearrange("p g t f -> p g (t f)")).then_inc(v_stored, 16)
                for i in range(K_BUFS):
                    pool.wait_ge(k_stored[i], 16 * FIRST_UNITS * KJ // K_BUFS)
                pool.wait_ge(v_stored, 16 * FIRST_UNITS)

            def first_units_v(v):
                v.tensor_scalar(neg_bk[:], cols[:, XBK:XBK + C], -SCALE, None, ALU.mult).then_inc(neg_bk_ready, 1)
                v.sem_inc(v_copied, VJ)
                v.sem_inc(k_split, K_BUFS)
                for u in range(FIRST_UNITS):
                    it, h = divmod(u, 2)
                    for j in range(KJ):
                        v.wait_ge(k_hi, KJ * u + j + 1)
                        kb = j % K_BUFS
                        v.tensor_tensor(k_rest[kb], k_f[kb], k_out[:, kb, 0], ALU.subtract) \
                            .then_inc(k_rest_ready, 1)
                    wait(v, v_stored, 16 * u)
                    for j in range(VJ):
                        v.wait_ge(vp_ready, VJ * u + j + 1)
                        n = min(2, UT - 2 * j)
                        for i in range(n):
                            last = v.tensor_tensor(
                                v_out[:, :, 2 * j + i, :],
                                psum[:, 4 + j % 4, i * D:(i + 1) * D].rearrange("p (g f) -> p g f", g=G),
                                rows[:, XBV, :].rearrange("p (g f) -> p g f", g=G), ALU.add)
                        last.then_inc(v_copied, 1)

            DVE_FRONT, DVE_END = 29, 4

            def pipeline(eng, step):
                for c in range(2):
                    step(c, c // 2, c % 2, True, c >= 1, False)
                with eng.Fori(1, B // 2) as it:
                    for h in range(2):
                        step(2 * it + h, it, h, True, True, True)
                for c in range(B, B + 2):
                    step(c, c // 2, c % 2, False, c == B, True)

            with nc.Block() as block:
                @block.sync
                def _(sp):
                    for tile, src in consts:
                        sp.dma_start(tile, src).then_inc(consts_loaded, 16)

                    def load(b, h):
                        for c in range(C):
                            sp.dma_start(xt[:, h, c, 1:L + 1], a["xT"][b, c]).then_inc(xt_loaded[h], 16)
                        sp.dma_start(xin[:, h], a["x"][b].rearrange("(t p) d -> p t d", p=P)).then_inc(xt_loaded[h], 16)

                    for h in range(2):
                        load(h, h)
                    with sp.Fori(1, B // 2) as it:
                        for h in range(2):
                            b = 2 * it + h
                            sp.wait_ge(kv_ready, b - 1)
                            sp.wait_ge(x2bo_ready, b - 1)
                            load(b, h)
                    first_units_sp(sp)

                @block.gpsimd
                def _(pool):
                    pool.memset(ident[:], 0.0).then_inc(ident_zeroed, 1)
                    pool.memset(mean_w[:], 1.0 / D)
                    pool.memset(ones[:], 1.0)
                    pool.memset(eps_col[:], EPS)
                    pool.memset(half_pi[:], math.pi / 2)
                    pool.memset(xt[:, :, :, 0:1], 0.0)
                    pool.memset(key_cos[:, :, 0:1], 0.0)
                    pool.memset(key_sin[:, :, 0:1], 0.0)
                    for e in range(E):
                        pool.memset(iota8[:, e:e + 1], float(e))
                    pool.wait_ge(ident_zeroed, 1)
                    pool.affine_select(out=ident[:], in_=ident[:], compare_op=ALU.not_equal, fill=1.0, base=0,
                                       pattern=[[-1, P]], channel_multiplier=1).then_inc(consts_made, 1)
                    pool.wait_ge(consts_loaded, N_CONSTS)

                    def step(c, it, h, front, mid, end):
                        if mid:
                            m, hm = c - 1, 1 - h
                            wait_alone(pool, (y_ready, m), (xt_loaded[hm], 48 * (it + h)))
                            pool.tensor_tensor(x2bo[:], xin[:, hm], rows[:, BO:BO + 1, :].to_broadcast([P, TT, D]),
                                               ALU.add).then_inc(x_bo_ready, 1)
                            pool.wait_ge(x_bo_ready, m + 1)
                            pool.tensor_tensor(x2bo[:], x2bo[:], xin[:, hm], ALU.add).then_inc(x2bo_ready, 1)
                        if end:
                            e = c - 2
                            wait_alone(pool, (x1_ready, e + 1))
                            pool.dma_start(x1_all[e].rearrange("(t p) d -> p t d", p=P), x1[:]).then_inc(x1_stored, 16)
                            wait_alone(pool, (q_stored, 16 * PARTS * e), (q_copied, e + 1 + OPEN))
                            pool.tensor_scalar(q_out[:, 0], q_f[:], 1.0, None, ALU.mult).then_inc(pool_split, 1)
                            pool.wait_ge(pool_split, 3 * e + 1)
                            pool.tensor_tensor(q_rest[:], q_f[:], q_out[:, 0], ALU.subtract).then_inc(pool_split, 1)
                            wait_alone(pool, (pool_split, 3 * e + 2))
                            pool.tensor_scalar(q_out[:, 1], q_rest[:], 1.0, None, ALU.mult).then_inc(pool_split, 1)
                            pool.wait_ge(pool_split, 3 * e + 3)
                            pool.tensor_tensor(q_out[:, 2], q_rest[:], q_out[:, 1], ALU.subtract).then_inc(q_split, 1)
                            wait_alone(pool, (q_split, e + 1 + OPEN))
                            for part in range(PARTS):
                                pool.dma_start(q_parts[part, e].rearrange("(c p) l -> p c l", p=P),
                                               q_out[:, part]).then_inc(q_stored, 16)

                    opened(pool, q_split)
                    pipeline(pool, step)
                    first_units_pool(pool)
                    pool.wait_ge(q_stored, 16 * PARTS * B)
                    pool.wait_ge(x1_stored, 16 * B)

                @block.tensor
                def _(pe):
                    def project(bank, weights, rhs, chunks):
                        for co in range(C):
                            for k in range(chunks):
                                last = pe.matmul(psum[:, bank + co, :], weights[:, k, co * P:(co + 1) * P],
                                                 rhs(k), start=k == 0, stop=k == chunks - 1)
                        return last

                    def step(c, it, h, front, mid, end):
                        b, m, e = c, c - 1, c - 2
                        now = lambda k: xt[:, h, k % C, 1 - k // C:L + 1 - k // C]
                        if front:
                            pe.wait_ge(xt_loaded[h], 48 * (it + 1))
                            wait(pe, phase_ready, b)
                            project(0, wk, now, C).then_inc(kz_ready, 1)
                            wait(pe, kv_used, b)
                            project(2, wg1, now, 2 * C).then_inc(gh_ready, 1)
                            wait(pe, below_max_ready, b)
                            for k in range(C):
                                last = pe.matmul(psum[:, 4, :], wb1[:, k, :], now(k), start=k == 0, stop=k == C - 1)
                            last.then_inc(bh_ready, 1)
                        if end:
                            if front:
                                pe.wait_ge(pv_used, b)
                            wait(pe, q_copied, e + OPEN)
                            pe.wait_ge(ln_ready, e + 1)
                            for t in range(TT):
                                for k in range(C):
                                    last = pe.matmul(psum[:, 5 + t // 2, (t % 2) * D:(t % 2 + 1) * D],
                                                     ln_t[:, k, t * P:(t + 1) * P], wo[:, k, :],
                                                     start=k == 0, stop=k == C - 1)
                            last.then_inc(mix_out_ready, 1)
                        if front:
                            pe.wait_ge(blend_h_ready, b + 1)
                            pe.wait_ge(gate_h_ready, b + 1)
                            for k in range(C):
                                last = pe.matmul(psum[:, 4, :], wg2_wide[:, k, :], gate_h[:, k, :],
                                                 start=k == 0, stop=k == C - 1)
                            last.then_inc(gate_z_ready, 1)
                            wait(pe, pv_used, b)
                            wait(pe, y_ready, e + 1)
                            project(5, wpv, now, C).then_inc(pv_ready, 1)
                            pe.wait_ge(gate_t_ready, b + 1)
                            pe.matmul(psum[:, 4, :], wb2_wide[:], blend_h[:], start=True, stop=True) \
                                .then_inc(bw_z_ready, 1)
                        if mid:
                            wait(pe, rstd_b_ready, m)
                            pe.wait_ge(blended_ready, m + 1)
                            for k in range(C):
                                last = pe.matmul(psum[:, 7, :], mean_w[:], blended[:, k, :], start=k == 0, stop=k == C - 1)
                            last.then_inc(mean_ready, 1)
                        if front:
                            project(2, wkv, now, C).then_inc(kv_ready, 1)
                        if mid:
                            pe.wait_ge(squares_ready, m + 1)
                            for k in range(C):
                                last = pe.matmul(psum[:, 7, :], mean_w[:], squares[:, k, :], start=k == 0, stop=k == C - 1)
                            last.then_inc(var_ready, 1)
                        if end:
                            if front:
                                pe.wait_ge(pv_used, b + 1)
                            pe.wait_ge(x1_ready, e + 1)
                            for k in range(C):
                                for t in range(TT):
                                    last = pe.transpose(psum[:, 5 + k, t * P:(t + 1) * P],
                                                        x1[:, t, k * P:(k + 1) * P], ident[:])
                            last.then_inc(x1t_ready, 1)
                            pe.wait_ge(x1t_copied, e + 1)
                            project(5, wq, lambda k: x1t[:, k, :], C).then_inc(q_ready, 1)

                    pe.wait_ge(consts_loaded, N_CONSTS)
                    pe.wait_ge(consts_made, 1)
                    pe.wait_ge(derived_ready, 1)
                    opened(pe, x1t_ready, q_ready)
                    pipeline(pe, step)
                    pe.wait_ge(q_copied, B + OPEN)
                    pe.wait_ge(rstd_b_ready, B)
                    pe.wait_ge(x1_ready, B)
                    first_units_pe(pe)

                @block.scalar
                def _(act):
                    def step(c, it, h, front, mid, end):
                        b, m, e = c, c - 1, c - 2
                        if front:
                            act.wait_ge(kz_ready, b + 1)
                            for i in range(C):
                                last = act.activation(phase[:, i], psum[:, i], ACT.Tanh, bias=col(BK + i))
                            last.then_inc(phase_ready, 1)
                            act.wait_ge(gh_ready, b + 1)
                            wait(act, gate_z_ready, b)
                            for i in range(C):
                                last = act.activation(gate_h[:, i], psum[:, 2 + i], ACT.Gelu, bias=col(BG1 + i))
                            last.then_inc(gate_h_ready, 1)
                            wait(act, bw_z_ready, b)
                            act.wait_ge(bh_ready, b + 1)
                            act.activation(blend_h[:], psum[:, 4], ACT.Gelu, bias=col(BB1)).then_inc(blend_h_ready, 1)
                            wait(act, gate_sum_ready, b)
                            act.wait_ge(gate_z_ready, b + 1)
                            act.activation(gate_t[:], psum[:, 4], ACT.Tanh, bias=mcols[:, 0:1], scale=0.5) \
                                .then_inc(gate_t_ready, 1)
                            act.wait_ge(phase_ready, b + 1)
                            act.activation(phase_abs[:], phase[:], ACT.Abs).then_inc(act_abs, 1)
                            wait(act, blended_ready, b)
                            act.activation(key_sin[:, :, 1:L + 1], phase[:], ACT.Sin, scale=PI_DOWN)
                            act.wait_ge(act_abs, b + 1)
                            act.activation(key_cos[:, :, 1:L + 1], phase_abs[:], ACT.Sin, bias=half_pi[:],
                                           scale=-PI_DOWN).then_inc(key_trig_ready, 1)
                        if end:
                            act.wait_ge(moments_ready, e + 1)
                            act.activation(rstd_ln[:], moments[:, :, 1], ACT.Ln, bias=eps_col[:]).then_inc(end_ln, 1)
                        if front:
                            act.wait_ge(gate_sum_ready, b + 1)
                            act.activation(gate_ln[:], gate_sum[:], ACT.Ln).then_inc(gate_ln_ready, 1)
                        if end:
                            act.wait_ge(end_ln, e + 1)
                            act.activation(rstd[:], rstd_ln[:], ACT.Exp, scale=-0.5).then_inc(rstd_ready, 1)
                        if front:
                            act.wait_ge(gate_ln_ready, b + 1)
                            act.activation(gate_rs[:], gate_ln[:], ACT.Exp, scale=-0.5).then_inc(gate_rs_ready, 1)
                            act.wait_ge(below_max_ready, b + 1)
                            act.activation(bexp[:, 0], below_max[:, 0], ACT.Exp)
                            act.activation(bexp[:, 1], below_max[:, 1], ACT.Exp, scale=-1.0).then_inc(bexp_ready, 1)
                        if mid:
                            wait(act, var_ready, m)
                            act.wait_ge(centred_ready, m + 1)
                            act.activation(squares[:], centred[:], ACT.Square).then_inc(squares_ready, 1)
                        if end:
                            wait(act, q_ready, e + OPEN)
                            act.wait_ge(x1t_ready, e + 1 + OPEN)
                            act.activation(x1t[:], psum[:, 5:7], ACT.Copy).then_inc(x1t_copied, 1)
                        if mid:
                            act.wait_ge(var_ready, m + 1)
                            act.activation(var_ln[:], psum[:, 7], ACT.Ln, bias=eps_col[:]).then_inc(mid_ln, 1)
                        if front:
                            act.wait_ge(bsum_ready, b + 1)
                            act.activation(bsum_ln[:], bsum[:], ACT.Ln).then_inc(bsum_ln_ready, 1)
                        if mid:
                            act.wait_ge(mid_ln, m + 1)
                            act.activation(rstd_b[:], var_ln[:], ACT.Exp, scale=-0.5).then_inc(rstd_b_ready, 1)
                        if front:
                            act.wait_ge(bsum_ln_ready, b + 1)
                            act.activation(bsum_r[:], bsum_ln[:], ACT.Exp, scale=-1.0).then_inc(bsum_r_ready, 1)
                        if mid:
                            wait(act, mix_out_ready, m)
                            act.wait_ge(normed_ready, m + 1)
                            for i in range(C):
                                last = act.activation(ln_t[:, i], normed[:, i], ACT.Identity, bias=col(LNB + i),
                                                      scale=col(LNG + i))
                            last.then_inc(ln_ready, 1)
                        if end:
                            wait(act, q_split, e + OPEN)
                            act.wait_ge(q_ready, e + 1 + OPEN)
                            for i in range(C):
                                last = act.activation(q_f[:, i], psum[:, 5 + i], ACT.Identity, bias=col(BQ + i))
                            last.then_inc(q_copied, 1)

                    act.wait_ge(consts_loaded, N_CONSTS)
                    act.wait_ge(consts_made, 1)
                    act.wait_ge(pos_ready, 1)
                    act.activation(pos_sin[:], pos[:], ACT.Sin)
                    act.activation(pos_cos[:], turns[:], ACT.Sin, bias=half_pi[:], scale=-1.0).then_inc(trig_ready, 1)
                    opened(act, q_copied)
                    pipeline(act, step)
                    first_units_act(act)

                @block.vector
                def _(v):
                    v.wait_ge(consts_loaded, N_CONSTS)
                    v.tensor_tensor(mcols[:, 1:2], col(WB2), col(WB2 + 1), ALU.subtract).then_inc(dve_pos, 1)
                    v.tensor_tensor(mcols[:, 2:3], col(BW_A), col(BW_B), ALU.subtract)
                    v.tensor_scalar(mcols[:, 0:1], col(BG2), 0.5, None, ALU.mult)
                    for k in range(C):
                        v.tensor_copy(wg2_wide[:, k, :], col(WG2 + k).to_broadcast([P, P]))
                    v.wait_ge(dve_pos, 1)
                    v.tensor_copy(wb2_wide[:], mcols[:, 1:2].to_broadcast([P, P])).then_inc(derived_ready, 1)
                    v.tensor_scalar(turns[:], pos[:], 1.0 / TWO_PI, ROUND, ALU.mult, ALU.add).then_inc(dve_pos, 1)
                    v.wait_ge(dve_pos, 2)
                    v.tensor_scalar(turns[:], turns[:], -ROUND, None, ALU.add).then_inc(dve_pos, 1)
                    v.wait_ge(dve_pos, 3)
                    v.scalar_tensor_tensor(pos[:], turns[:], -TWO_PI_HI, pos[:], ALU.mult, ALU.add).then_inc(dve_pos, 1)
                    v.wait_ge(dve_pos, 4)
                    v.scalar_tensor_tensor(pos[:], turns[:], TWO_PI_HI - TWO_PI, pos[:], ALU.mult, ALU.add) \
                        .then_inc(dve_pos, 1)
                    v.wait_ge(dve_pos, 5)
                    v.tensor_scalar(pos[:], pos[:], -PI_DOWN, PI_DOWN, ALU.max, ALU.min).then_inc(dve_pos, 1)
                    v.wait_ge(dve_pos, 6)
                    v.scalar_tensor_tensor(turns[:], pos[:], -1.0, pos[:], ALU.mult, ALU.max).then_inc(pos_ready, 1)
                    v.wait_ge(trig_ready, 1)

                    def step(c, it, h, front, mid, end):
                        b, m, e = c, c - 1, c - 2
                        steps = Steps(DVE_FRONT * b)
                        ends = Steps(DVE_END * e)

                        def scan(mem):
                            for i in range(C):
                                v.tensor_tensor_scan(mem[:, i], mem[:, i], mem[:, i], 0.0, ALU.add, ALU.bypass) \
                                    .then_inc(dve_front, 1)
                                s = steps.next()
                            return s

                        def times(out_t, in0, in1, op=ALU.mult):
                            v.tensor_tensor(out_t, in0, in1, op).then_inc(dve_front, 1)
                            return steps.next()

                        if end:
                            v.wait_ge(x2bo_ready, e + 1)
                            v.wait_ge(mix_out_ready, e + 1)
                            v.tensor_tensor(y[:].rearrange("p t d -> p (t d)").rearrange("p (n f) -> p n f", n=2),
                                            psum[:, 5:7],
                                            x2bo[:].rearrange("p t d -> p (t d)").rearrange("p (n f) -> p n f", n=2),
                                            ALU.add).then_inc(y_ready, 1)
                        if front:
                            v.wait_ge(gate_t_ready, b + 1)
                            v.tensor_scalar(gate[:], gate_t[:], 0.5, 0.5, ALU.mult, ALU.add).then_inc(dve_front, 1)
                            s = steps.next()
                            wait(v, gate_rs_ready, b)
                            v.wait_ge(dve_front, s)
                            v.tensor_tensor_scan(gate_sum[:], gate[:], gate[:], 0.0, ALU.add, ALU.bypass) \
                                .then_inc(dve_front, 1)
                            s = steps.next()
                            v.wait_ge(dve_front, s)
                            v.tensor_scalar(gate_sum[:], gate_sum[:], 1.0, None, ALU.max).then_inc(gate_sum_ready, 1)
                        if end:
                            v.wait_ge(y_ready, e + 1)
                            for t in range(TT):
                                v.bn_stats(stats[:, t], y[:, t]).then_inc(dve_end, 1)
                                s = ends.next()
                            wait_alone(v, (dve_end, s))
                            for t in range(TT):
                                last = v.bn_aggr(moments[:, t], stats[:, t])
                            last.then_inc(moments_ready, 1)
                        if front:
                            v.wait_ge(pv_ready, b + 1)
                            for i in range(C):
                                v.scalar_tensor_tensor(mem_c[:, i], psum[:, 5 + i], col(BPV + i), pos_cos[:, i], ALU.add,
                                                       ALU.mult).then_inc(dve_front, 1)
                                steps.next()
                            for i in range(C):
                                last = v.scalar_tensor_tensor(mem_s[:, i], psum[:, 5 + i], col(BPV + i), pos_sin[:, i],
                                                              ALU.add, ALU.mult)
                                last.then_inc(pv_used if i else dve_front, 1)
                            s_pos = steps.next()
                            wait(v, bexp_ready, b)
                            v.wait_ge(bw_z_ready, b + 1)
                            v.tensor_scalar(below_max[:, 0], psum[:, 4], mcols[:, 2:3], 0.0, ALU.add, ALU.min)
                            v.tensor_scalar(below_max[:, 1], psum[:, 4], mcols[:, 2:3], 0.0, ALU.add, ALU.max) \
                                .then_inc(below_max_ready, 1)
                        if mid:
                            v.wait_ge(blended_ready, m + 1)
                            wait(v, squares_ready, m)
                            wait(v, ln_ready, m)
                            v.wait_ge(mean_ready, m + 1)
                            for i in range(C):
                                last = v.tensor_tensor(centred[:, i], blended[:, i], psum[:, 7], ALU.subtract)
                            last.then_inc(centred_ready, 1)
                        if end:
                            wait(v, x1_stored, 16 * e)
                            wait(v, x1t_ready, e + OPEN)
                            v.wait_ge(moments_ready, e + 1)
                            v.wait_ge(rstd_ready, e + 1)
                            for t in range(TT):
                                last = v.tensor_scalar(x1[:, t], y[:, t], moments[:, t, 0:1], rstd[:, t:t + 1],
                                                       ALU.subtract, ALU.mult)
                            last.then_inc(x1_ready, 1)
                        if front:
                            v.wait_ge(dve_front, s_pos)
                            v.wait_ge(pv_used, b + 1)
                            scan(mem_c)
                            s = scan(mem_s)
                            v.wait_ge(bexp_ready, b + 1)
                            wait(v, bsum_r_ready, b)
                            v.tensor_tensor(bsum[:], bexp[:, 0], bexp[:, 1], ALU.add).then_inc(bsum_ready, 1)
                            v.wait_ge(dve_front, s - 2)
                            times(mem_c[:], mem_c[:], pos_cos[:])
                            v.wait_ge(dve_front, s)
                            s = times(mem_s[:], mem_s[:], pos_sin[:])
                            v.wait_ge(dve_front, s)
                            times(pos_ret[:], mem_c[:], mem_s[:], ALU.add)
                            v.wait_ge(kv_ready, b + 1)
                            for i in range(C):
                                v.scalar_tensor_tensor(kvg[:, i], psum[:, 2 + i], col(BKV + i), gate[:], ALU.add,
                                                       ALU.mult).then_inc(kv_used if i else dve_front, 1)
                            s = steps.next()
                            v.wait_ge(dve_front, s)
                            v.wait_ge(kv_used, b + 1)
                            v.wait_ge(key_trig_ready, b + 1)
                            times(mem_c[:], kvg[:], key_cos[:, :, 0:L])
                            s = times(mem_s[:], kvg[:], key_sin[:, :, 0:L])
                        if mid:
                            v.wait_ge(centred_ready, m + 1)
                            v.wait_ge(rstd_b_ready, m + 1)
                            for i in range(C):
                                last = v.tensor_tensor(normed[:, i], centred[:, i], rstd_b[:], ALU.mult)
                            last.then_inc(normed_ready, 1)
                        if front:
                            v.wait_ge(dve_front, s - 1)
                            scan(mem_c)
                            v.wait_ge(dve_front, s)
                            s = scan(mem_s)
                            v.wait_ge(dve_front, s - 2)
                            times(mem_c[:], mem_c[:], key_cos[:, :, 1:L + 1])
                            v.wait_ge(dve_front, s)
                            s = times(mem_s[:], mem_s[:], key_sin[:, :, 1:L + 1])
                            v.wait_ge(dve_front, s)
                            times(mem_c[:], mem_c[:], mem_s[:], ALU.add)
                            v.wait_ge(bsum_r_ready, b + 1)
                            v.wait_ge(gate_rs_ready, b + 1)
                            for i in range(2):
                                v.scalar_tensor_tensor(bw[:, i], bexp[:, i], 1.0 / ROOT_D, bsum_r[:], ALU.mult, ALU.mult) \
                                    .then_inc(dve_front, 1)
                                s = steps.next()
                            v.wait_ge(dve_front, s)
                            s = times(kv_w[:], bw[:, 1], gate_rs[:])
                            for i in range(C):
                                times(pos_ret[:, i], pos_ret[:, i], bw[:, 0])
                            v.wait_ge(dve_front, s)
                            for i in range(C):
                                s = times(mem_c[:, i], mem_c[:, i], kv_w[:])
                            v.wait_ge(dve_front, s)
                            v.tensor_tensor(blended[:], pos_ret[:], mem_c[:], ALU.add).then_inc(blended_ready, 1)
                            assert steps.n == DVE_FRONT, steps.n
                        if end:
                            assert ends.n == DVE_END, ends.n

                    pipeline(v, step)
                    first_units_v(v)

        sb = tensors(top)
        w1_all = sb("w1_all", [P, E, C, HID])
        ffn_loaded = sem("ffn_loaded")
        with ExitStack() as ctx:
            sb = tensors(ctx)
            SUBS = 2 * ST
            SCORE_BUFS, P_BUFS = 3, 6
            N_SUB, N_TILE = 2 * SUBS, 2 * ST
            LAG = 3
            ct1 = sb("ct1", [P, C, SU])
            k1_f, k1_rest = sb("k1_f", [P, KC]), sb("k1_rest", [P, KC])
            k1_out = sb("k1_out", [P, 2, PARTS, KC], BF16)
            v1_out = sb("v1_out", [P, G, UT, GH * DH])
            ct1_loaded, items_ready, items_read, unit_steps, v1_stored = (sem(n) for n in (
                "ct1_loaded", "items_ready", "items_read", "unit_steps", "v1_stored"))
            k1_stored = (sem("k1_stored0"), sem("k1_stored1"))
            ITEMS = 8
            FILL_AT = [1 + 6 * p for p in range(4)]
            AHEAD = 2
            FILLED = UNITS - FIRST_UNITS
            qst = sb("qst", [STACK, 2, GH, L], BF16)
            kst = sb("kst", [STACK, 2, GH, 2 * SU], BF16)
            vst = sb("vst", [P, 2, 2 * UT, GH * DH])
            neg_max = sb("neg_max", [P, SCORE_BUFS, 2])
            probs = sb("probs", [P, P_BUFS, GH, L])
            sums = sb("sums", [P, P_BUFS, GH])
            inv = sb("inv", [P, P_BUFS, GH])
            v_scaled = sb("v_scaled", [P, P_BUFS, GH, PAD])
            attn = sb("attn", [P, 2, L])
            heads_loaded = (sem("heads_loaded0"), sem("heads_loaded1"))
            (pads_zeroed, scores_ready, max_ready, exp_done, inv_ready, v_scaled_ready, pv_done,
             attn_copied) = (sem(n) for n in (
                 "pads_zeroed", "scores_ready", "max_ready", "exp_done", "inv_ready", "v_scaled_ready", "pv_done",
                 "attn_copied"))
            attn_stored = (sem("attn_stored0"), sem("attn_stored1"))
            score_buf = [k % SCORE_BUFS for k in range(N_SUB - 1)] + [1]
            full_turns = N_TILE % (P_BUFS - 1)
            prob_buf = full_turns * list(range(P_BUFS)) + \
                (N_TILE - full_turns * P_BUFS) // (P_BUFS - 1) * list(range(P_BUFS - 1))
            assert len(prob_buf) == N_TILE
            CREDIT = N_TILE

            def free(k, buffer_of, it):
                rounds, k = divmod(k, len(buffer_of))
                round_, p = last_user(k, buffer_of)
                return len(buffer_of) * it + len(buffer_of) * (rounds + round_) + p + 1 + CREDIT

            def rounds(eng, tile_step):
                for tile in range(LAG):
                    tile_step(tile, 0, False)
                for first, end, fill in ((0, FILLED, True), (FILLED, NG // 2 - 1, False)):
                    with eng.Fori(first, end) as it:
                        for tile in range(LAG, N_TILE + LAG):
                            tile_step(tile, it, fill)
                for tile in range(LAG, N_TILE + LAG):
                    tile_step(tile, NG // 2 - 1, False)

            def is_over(tile, it):
                return isinstance(it, int) and tile >= N_TILE and it == NG // 2 - 1

            with nc.Block() as block:
                @block.sync
                def _(sp):
                    def load(b, g):
                        h = g % 2
                        for slot in range(len(Q_SLOTS)):
                            at = slice(slot * DH, (slot + 1) * DH)
                            qd = q_parts[Q_SLOTS[slot]].rearrange("b (g j d) l -> b g d j l", g=G, j=GH)[b, g]
                            sp.dma_start(qst[at, h], qd).then_inc(heads_loaded[h], 16)
                            for r in range(2):
                                kd = k_parts[K_SLOTS[slot]] \
                                    .rearrange("(b r) (g j d) s -> r g b d j s", r=2, g=G, j=GH)[r, g, b]
                                sp.dma_start(kst[at, h, :, r * SU:(r + 1) * SU], kd).then_inc(heads_loaded[h], 16)
                        for r in range(2):
                            sp.dma_start(vst[:, h, r * UT:(r + 1) * UT].rearrange("p t f -> p (t f)"),
                                         v_all.rearrange("(b r) g p f -> r g b p f", r=2)[r, g, b]) \
                                .then_inc(heads_loaded[h], 16)

                    def load_context(u):
                        sp.dma_start(ct1[:], a["ctxT"][u].rearrange("c p s -> p c s")).then_inc(ct1_loaded, 16)

                    def two_rounds(b, fill):
                        for r in range(2):
                            for h in range(2):
                                n = G * b + 2 * r + h
                                sp.wait_ge(attn_copied, n + 2)
                                sp.dma_start(attn_all[n], attn[:, h]).then_inc(attn_stored[h], 16)
                                if r == 0:
                                    load(b, 2 + h)
                                elif not (isinstance(b, int) and b == B - 1):
                                    if h == 0:
                                        made = 2 * b + 4 - FIRST_UNITS
                                        wait_alone(sp, (k1_stored[0], 32 * made), (k1_stored[1], 32 * made),
                                                   (v1_stored, 16 * made))
                                    load(b + 1, h)
                                if h == 0 and fill:
                                    sp.wait_ge(items_ready, ITEMS * (2 * b + r + 1))
                                    load_context(2 * b + r + 1 + FIRST_UNITS)

                    def load_weights(e):
                        sp.dma_start(w1_all[:, bass.ds(e, 1)].rearrange("p o c h -> p (o c) h"),
                                     a["W1"][e].rearrange("(c p) h -> p c h", p=P)).then_inc(ffn_loaded, 16)

                    opened(sp, *attn_stored)
                    load(0, 0)
                    load(0, 1)
                    load_context(FIRST_UNITS)
                    with sp.Fori(0, B - 2) as b:
                        two_rounds(b, True)
                        load_weights(b)
                    for b in range(B - 2, B):
                        two_rounds(b, False)
                        load_weights(b)
                    for h in range(2):
                        sp.wait_ge(attn_stored[h], 16 * NG // 2 + OPEN)

                LOADS = 16 * (3 * len(Q_SLOTS) + 2)

                def rows_of(t):
                    return P if t < ST - 1 else TAIL

                @block.tensor
                def _(pe):
                    def pv(tile, it):
                        h, t = divmod(tile, ST)
                        if t == 0:
                            pe.wait_ge(attn_copied, 2 * it + h + 1)
                        pe.wait_ge(v_scaled_ready, N_TILE * it + tile + 1)
                        r, pb = rows_of(t), prob_buf[tile]
                        for j in range(GH):
                            last = pe.matmul(psum[j * PAD:(j + 1) * PAD, 6, :], v_scaled[0:r, pb, j, :],
                                             probs[0:r, pb, j, :], start=t == 0, stop=t == ST - 1)
                        last.then_inc(pv_done, 1)

                    def make_item(item, part, it):
                        p, of_values = divmod(item, 2)
                        if item == 0:
                            pe.wait_ge(ct1_loaded, 16 * (it + 1))
                        if part == 0:
                            pe.wait_ge(items_read, ITEMS * it + item + 1)
                        if of_values:
                            for t in range(2 * p + part, min(2 * p + part + 1, UT)):
                                for k in range(C):
                                    last = pe.matmul(psum[:, 7, (t % 2) * D:(t % 2 + 1) * D],
                                                     ct1[:, k, t * P:(t + 1) * P], xwv[:, k, :],
                                                     start=k == 0, stop=k == C - 1)
                        else:
                            co, s0 = p // 2, (p % 2) * KC
                            last = pe.matmul(psum[:, 7, 0:KC], xwk[:, part, co * P:(co + 1) * P],
                                             ct1[:, part, s0:s0 + KC], start=part == 0, stop=part == 1)
                        if part == 1 or of_values and 2 * p + 1 == UT:
                            last.then_inc(items_ready, 1)

                    def tile_step(tile, it, fill):
                        if not is_over(tile, it):
                            rounds_on, here = divmod(tile, N_TILE)
                            h, t = divmod(here, ST)
                            if t == 0:
                                pe.wait_ge(heads_loaded[h], LOADS * (it + rounds_on + 1))
                            r = rows_of(t)
                            for sub in range(2):
                                k = 2 * tile + sub
                                sbuf = score_buf[k % N_SUB]
                                pe.wait_ge(exp_done, free(k, score_buf, it))
                                for i in range(2):
                                    j = 2 * sub + i
                                    last = pe.matmul(psum[0:r, 2 * sbuf + i, :], kst[:, h, j, t * P:t * P + r],
                                                     qst[:, h, j, :], start=True, stop=True)
                                last.then_inc(scores_ready, 1)
                        if fill:
                            for p in range(4):
                                for i in range(2):
                                    part = tile - (FILL_AT[p] + 3 * i + AHEAD)
                                    if part in (0, 1) and not (i and 2 * p + part == UT):
                                        make_item(2 * p + i, part, it)
                        if tile >= LAG:
                            pv(tile - LAG, it)

                    pe.wait_ge(pads_zeroed, 1)
                    pe.sem_inc(pv_done, CREDIT)
                    rounds(pe, tile_step)

                @block.vector
                def _(v):
                    def inverse(tile, it):
                        v.wait_ge(exp_done, N_SUB * it + 2 * tile + 2 + CREDIT)
                        t = tile % N_TILE
                        r = rows_of(t % ST)
                        v.reciprocal(inv[0:r, prob_buf[t]], sums[0:r, prob_buf[t]]).then_inc(inv_ready, 1)

                    def read_item(item, it):
                        p, of_values = divmod(item, 2)
                        if of_values:
                            if p == 0:
                                v.wait_ge(v1_stored, 16 * it)
                            v.wait_ge(items_ready, ITEMS * it + item + 1)
                            n = min(2, UT - 2 * p)
                            for i in range(n):
                                last = v.tensor_tensor(
                                    v1_out[:, :, 2 * p + i, :],
                                    psum[:, 7, i * D:(i + 1) * D].rearrange("p (g f) -> p g f", g=G),
                                    rows[:, XBV, :].rearrange("p (g f) -> p g f", g=G), ALU.add)
                        else:
                            v.wait_ge(unit_steps, 16 * it + 4 * p + 1)
                            v.wait_ge(items_ready, ITEMS * it + item + 1)
                            last = v.tensor_scalar(k1_f[:], psum[:, 7, 0:KC], -SCALE, neg_bk[:, p // 2:p // 2 + 1],
                                                   ALU.mult, ALU.add)
                        last.then_inc(items_read, 1)

                    def tile_step(tile, it, fill):
                        if not is_over(tile, it):
                            r = rows_of(tile % N_TILE % ST)
                            for sub in range(2):
                                k = 2 * tile + sub
                                sbuf = score_buf[k % N_SUB]
                                v.wait_ge(scores_ready, N_SUB * it + k + 1)
                                v.tensor_reduce(neg_max[0:r, sbuf], psum[0:r, 2 * sbuf:2 * sbuf + 2], AX_X, ALU.min) \
                                    .then_inc(max_ready, 1)
                        if tile >= 1 and not is_over(tile - 1, it):
                            inverse(tile - 1, it)
                        if fill:
                            for p in range(4):
                                for i in range(2):
                                    if tile == FILL_AT[p] + 3 * i + AHEAD + 1:
                                        read_item(2 * p + i, it)
                        for h in range(2):
                            if tile == ST * (h + 1) + LAG - 1:
                                v.wait_ge(pv_done, N_TILE * it + ST * (h + 1) + CREDIT)
                                v.wait_ge(attn_stored[h], 16 * it + OPEN)
                                v.tensor_copy(attn[:, h], psum[:, 6]).then_inc(attn_copied, 1)

                    v.memset(v_scaled[:], 0.0).then_inc(pads_zeroed, 1)
                    v.sem_inc(attn_copied, 1)
                    rounds(v, tile_step)

                @block.gpsimd
                def _(pool):
                    def unit_step(p, at, it):
                        u = it + FIRST_UNITS
                        kb = p % 2
                        before = STEPS_OF_PAIR * (4 * it + p)
                        co, s0 = p // 2, (p % 2) * KC
                        if at == 0:
                            wait_alone(pool, (k1_stored[kb], 16 * (2 * it + p // 2)), (items_read, ITEMS * it + 2 * p + 2))
                            pool.tensor_scalar(k1_out[:, kb, 0], k1_f[:], 1.0, None, ALU.mult).then_inc(unit_steps, 1)
                        elif at == 1:
                            pool.wait_ge(unit_steps, before + 2)
                            pool.tensor_tensor(k1_rest[:], k1_f[:], k1_out[:, kb, 0], ALU.subtract) \
                                .then_inc(unit_steps, 1)
                        elif at == 2:
                            wait_alone(pool, (unit_steps, before + 3))
                            pool.tensor_scalar(k1_out[:, kb, 1], k1_rest[:], 1.0, None, ALU.mult).then_inc(unit_steps, 1)
                        elif at == 3:
                            pool.wait_ge(unit_steps, before + 4)
                            pool.tensor_tensor(k1_out[:, kb, 2], k1_rest[:], k1_out[:, kb, 1], ALU.subtract) \
                                .then_inc(unit_steps, 1)
                            wait_alone(pool, (unit_steps, before + 5))
                            pool.dma_start(k_parts[:, u, co * P:(co + 1) * P, s0:s0 + KC].rearrange("n p s -> p n s"),
                                           k1_out[:, kb]).then_inc(k1_stored[kb], 16)
                        elif p == 3:
                            wait_alone(pool, (items_read, ITEMS * (it + 1) + 1))
                            pool.dma_start(v_all[u].rearrange("g p f -> p g f"),
                                           v1_out[:].rearrange("p g t f -> p g (t f)")).then_inc(v1_stored, 16)

                    STEPS_OF_PAIR = 4
                    pool.wait_ge(pads_zeroed, 1)
                    pool.sem_inc(unit_steps, 1)
                    pool.sem_inc(items_read, 1)
                    for first, end, fill in ((0, FILLED, True), (FILLED, NG // 2, False)):
                        with pool.Fori(first, end) as it:
                            for tile in range(N_TILE):
                                h, t = divmod(tile, ST)
                                r, pb = rows_of(t), prob_buf[tile]
                                pool.wait_ge(pv_done, free(tile, prob_buf, it))
                                pool.wait_ge(inv_ready, N_TILE * it + tile + 1)
                                pool.tensor_tensor(
                                    v_scaled[0:r, pb, :, 0:DH], vst[0:r, h, t, :].rearrange("p (j d) -> p j d", j=GH),
                                    inv[0:r, pb].rearrange("p (j o) -> p j o", o=1).to_broadcast([r, GH, DH]), ALU.mult) \
                                    .then_inc(v_scaled_ready, 1)
                                if fill:
                                    for p in range(4):
                                        if 2 <= tile - FILL_AT[p] < 7:
                                            unit_step(p, tile - FILL_AT[p] - 2, it)
                    for i in range(2):
                        pool.wait_ge(k1_stored[i], 32 * FILLED)
                    pool.wait_ge(v1_stored, 16 * FILLED)

                @block.scalar
                def _(act):
                    act.wait_ge(pads_zeroed, 1)
                    act.sem_inc(exp_done, CREDIT)
                    with act.Fori(0, NG // 2) as it:
                        for tile in range(N_TILE):
                            h, t = divmod(tile, ST)
                            r, pb = rows_of(t), prob_buf[tile]
                            act.wait_ge(pv_done, free(tile, prob_buf, it))
                            for sub in range(2):
                                k = 2 * tile + sub
                                sbuf = score_buf[k]
                                act.wait_ge(max_ready, N_SUB * it + k + 1)
                                for i in range(2):
                                    j = 2 * sub + i
                                    last = act.activation(probs[0:r, pb, j, :], psum[0:r, 2 * sbuf + i, :], ACT.Exp,
                                                          bias=neg_max[0:r, sbuf, i:i + 1], scale=-1.0,
                                                          accum_out=sums[0:r, pb, j:j + 1])
                                last.then_inc(exp_done, 1)

        sb = tensors(top)
        w2_all = sb("w2_all", [P, E, HC, D])
        tile_row = sb("tile_row", [1, TILES + 1], I32)
        tile_expert = sb("tile_expert", [1, TILES + 1], I32)

        with ExitStack() as ctx:
            sb = tensors(ctx)
            xwo = sb("xwo", [P, G, D])
            at_in = sb("at_in", [P, 2, G, L])
            x1_in = sb("x1_in", [P, 2, TT, D])
            y2 = sb("y2", [P, TT, D])
            stats2 = sb("stats2", [P, TT, 6])
            moments2 = sb("moments2", [P, TT, 2])
            rstd2_ln = sb("rstd2_ln", [P, TT])
            rstd2 = sb("rstd2", [P, TT])
            x2 = sb("x2", [P, 2, TT, D])
            rows_out = sb("rows_out", [P, 2, 2, TT, ROW])
            x2t = sb("x2t", [P, C, L])
            x2b = sb("x2b", [P, TT, D])
            mask = sb("mask", [P, TT, E])
            slot_at = sb("slot_at", [P, TT + 1, E])
            slot_of = sb("slot_of", [P, TT, E])
            slot_f = sb("slot_f", [P, 2 * TT])
            slot_u = sb("slot_u", [P, 2, 2 * TT], U32)
            pad_row = sb("pad_row", [P, ROW])
            pad_f = sb("pad_f", [P, E])
            pad_u = sb("pad_u", [P, E], U32)
            n_rows = sb("n_rows", [1, E])
            n_tiles = sb("n_tiles", [1, E])
            ends = sb("ends", [1, E])
            skip = sb("skip", [1, E])
            row_g = sb("row_g", [1, TILES + 1])

            def table(t, at, width):
                return t[0:1].rearrange("p a b -> p (a b)")[:, at:at + (TILES + 1) * width]

            past, past_skip = (table(t, 0, E).rearrange("p (j e) -> p j e", e=E) for t in (y2, x2t))
            expert_f, row_f = table(y2, (TILES + 1) * E, 1), table(x2t, (TILES + 1) * E, 1)
            logits = sb("logits", [P, TT, E])
            top8 = sb("top8", [P, TT, E])
            top8_at = sb("top8_at", [P, TT, E], U32)
            chosen = sb("chosen", [P, TT, 2])
            N_HOT = 2 * TT * E
            onehot, weighted, slot_own = (
                xwv[:, 0, i * N_HOT:(i + 1) * N_HOT].rearrange("p (i t e) -> p i t e", i=2, t=TT) for i in range(3))
            gap = sb("gap", [P, TT])
            egap = sb("egap", [P, TT])
            den = sb("den", [P, TT])
            w01 = sb("w01", [P, 2, TT])
            wts = sb("wts", [P, TT, E])
            wts_t = xwk[0:E].rearrange("p c d -> p (c d)")
            xwo_loaded = sem("xwo_loaded")
            route_loaded = (sem("route_loaded0"), sem("route_loaded1"))
            (x1bo_ready, proj_ready, y2_ready, dve_route, moments2_ready, act_ln2, rstd2_ready, x2_ready, x2t_ready,
             x2t_copied, twin_ready, logits_z_ready, logits_ready, gap_ready, egap_ready, wts_ready, wts_t_ready,
             wts_t_copied, b2_ready, acc_ready) = (sem(n) for n in (
                 "x1bo_ready", "proj_ready", "y2_ready", "dve_route", "moments2_ready", "act_ln2", "rstd2_ready",
                 "x2_ready", "x2t_ready", "x2t_copied", "twin_ready", "logits_z_ready", "logits_ready", "gap_ready",
                 "egap_ready", "wts_ready", "wts_t_ready", "wts_t_copied", "b2_ready", "acc_ready"))
            NORM_STEPS, ROUTE_STEPS = 4, 24

            def pipeline(eng, step):
                for c in range(2):
                    step(c, 0, c, True, c == 1)
                with eng.Fori(1, B // 2) as it:
                    for h in range(2):
                        step(2 * it + h, it, h, True, True)
                step(B, B // 2, 0, False, True)

            def pipeline_ahead(eng, step):
                step(0, 0, 0, True, False)
                with eng.Fori(0, B // 2 - 1) as it:
                    step(2 * it + 1, it, 1, True, True)
                    step(2 * it + 2, it + 1, 0, True, True)
                step(B - 1, B // 2 - 1, 1, False, True)
                step(B, B // 2, 0, False, True)

            mask_ready, ranks_ready, slots_ready, numbered, pads_made, pads_ready, plan = (sem(n) for n in (
                "mask_ready", "ranks_ready", "slots_ready", "numbered", "pads_made", "pads_ready", "plan"))
            scattered = (sem("scattered0"), sem("scattered1"))
            pads_stored = sem("pads_stored")
            x2b_stored, dve_norm = sem("x2b_stored"), sem("dve_norm")

            with nc.Block() as block:
                @block.sync
                def _(sp):
                    def load(b, h):
                        sp.dma_start(at_in[:, h], attn_all.rearrange("(b g) p l -> b p g l", g=G)[b]) \
                            .then_inc(route_loaded[h], 16)
                        sp.dma_start(x1_in[:, h], x1_all[b].rearrange("(t p) d -> p t d", p=P)) \
                            .then_inc(route_loaded[h], 16)

                    sp.dma_start(xwo[:], a["xWo"].rearrange("g p d -> p g d")).then_inc(xwo_loaded, 16)
                    def load_weights(e):
                        sp.dma_start(w2_all[:, bass.ds(e, 1)].rearrange("p o c d -> p (o c) d"),
                                     a["W2"][e].rearrange("(c p) d -> p c d", p=P)).then_inc(ffn_loaded, 16)

                    for h in range(2):
                        load(h, h)
                    for e in range(2):
                        load_weights(e)
                    with sp.Fori(1, B // 2) as it:
                        for h in range(2):
                            sp.wait_ge(y2_ready, 2 * it + h - 1)
                            load(2 * it + h, h)
                            load_weights(2 * it + h)

                @block.gpsimd
                def _(pool):
                    def residual(it, h):
                        pool.wait_ge(route_loaded[h], 32 * (it + 1))
                        pool.tensor_tensor(x1_in[:, h], x1_in[:, h], rows[:, XBO:XBO + 1, :].to_broadcast([P, TT, D]),
                                           ALU.add).then_inc(x1bo_ready, 1)

                    def step(c, it, h, ahead, back):
                        if ahead:
                            residual(it + h, 1 - h)
                        if back:
                            e, he = c - 1, 1 - h
                            wait(pool, scattered[he], 16 * 2 * TT * (it - he))
                            pool.tensor_copy(rows_out[:, he, :, :, AT_DEST],
                                             dest_ids[:, :, bass.ds(e * TT, TT)]).then_inc(numbered, 1)
                            wait_alone(pool, (numbered, e + 1), (twin_ready, e + 1), (slots_ready, e + 1))
                            for i in range(2):
                                for t in range(TT):
                                    at = i * TT + t
                                    pool.indirect_dma_start(
                                        xs, bass.IndirectOffsetOnAxis(slot_u[:, he, at:at + 1], 0),
                                        rows_out[:, he, i, t, :], None).then_inc(scattered[he], 16)
                            wait_alone(pool, (acc_ready, e + 1))
                            pool.dma_start(x2_all[e].rearrange("(t p) d -> p t d", p=P), x2b[:]).then_inc(x2b_stored, 16)

                    residual(0, 0)
                    pipeline_ahead(pool, step)
                    pool.wait_ge(pads_ready, 1)
                    for e in range(E):
                        pool.indirect_dma_start(xs, bass.IndirectOffsetOnAxis(pad_u[:, e:e + 1], 0), pad_row[:], None) \
                            .then_inc(pads_stored, 16)
                    pool.dma_start(xs[NO_TILE:NO_TILE + P], pad_row[:]).then_inc(pads_stored, 16)
                    pool.wait_ge(pads_stored, 16 * (E + 1))
                    pool.wait_ge(x2b_stored, 16 * B)
                    for h in range(2):
                        pool.wait_ge(scattered[h], 16 * TT * B)

                @block.tensor
                def _(pe):
                    def project(b, it, h):
                        wait(pe, y2_ready, b)
                        pe.wait_ge(route_loaded[h], 32 * (it + 1))
                        for t in range(TT):
                            for g in range(G):
                                last = pe.matmul(psum[:, t // 2, (t % 2) * D:(t % 2 + 1) * D],
                                                 at_in[:, h, g, t * P:(t + 1) * P], xwo[:, g, :],
                                                 start=g == 0, stop=g == G - 1)
                        last.then_inc(proj_ready, 1)

                    def step(c, it, h, ahead, back):
                        e, he = c - 1, 1 - h
                        if back:
                            wait(pe, x2t_copied, e)
                            pe.wait_ge(x2_ready, e + 1)
                            for k in range(C):
                                for t in range(TT):
                                    last = pe.transpose(psum[:, 2 + k, t * P:(t + 1) * P],
                                                        x2[:, he, t, k * P:(k + 1) * P], ident[:])
                            last.then_inc(x2t_ready, 1)
                            wait(pe, slots_ready, e)
                            pe.wait_ge(x2t_copied, e + 1)
                            for t in range(TT):
                                for k in range(C):
                                    last = pe.matmul(psum[:, 4, t * E:(t + 1) * E], x2t[:, k, t * P:(t + 1) * P],
                                                     router_w[:, k, :], start=k == 0, stop=k == C - 1)
                            last.then_inc(logits_z_ready, 1)
                        if ahead:
                            project(c + 1, it + h, 1 - h)
                        if back:
                            pe.wait_ge(mask_ready, e + 1)
                            pe.matmul(psum[:, 4, 64:64 + TT * E], before[:], mask[:].rearrange("p t e -> p (t e)"),
                                      start=True, stop=True)
                            pe.matmul(psum[:, 4, 128:128 + TT * E], ones[:], mask[:].rearrange("p t e -> p (t e)"),
                                      start=True, stop=True).then_inc(ranks_ready, 1)
                            wait(pe, wts_t_copied, e)
                            pe.wait_ge(wts_ready, e + 1)
                            for t in range(TT):
                                last = pe.transpose(psum[0:E, 5, t * P:(t + 1) * P], wts[:, t, :], ident[:])
                            last.then_inc(wts_t_ready, 1)
                            wait(pe, acc_ready, e)
                            pe.wait_ge(wts_t_copied, e + 1)
                            for t in range(TT):
                                last = pe.matmul(psum[:, 6 + t // 2, (t % 2) * D:(t % 2 + 1) * D],
                                                 wts_t[:, t * P:(t + 1) * P], b2_rows[:], start=True, stop=True)
                            last.then_inc(b2_ready, 1)

                    pe.wait_ge(xwo_loaded, 16)
                    project(0, 0, 0)
                    pipeline_ahead(pe, step)

                @block.scalar
                def _(act):
                    def step(c, it, h, front, back):
                        b, e, he = c, c - 1, 1 - h
                        if back:
                            wait(act, logits_z_ready, e)
                            act.wait_ge(x2t_ready, e + 1)
                            act.activation(x2t[:], psum[:, 2:4], ACT.Copy).then_inc(x2t_copied, 1)
                        if front:
                            act.wait_ge(moments2_ready, b + 1)
                            act.activation(rstd2_ln[:], moments2[:, :, 1], ACT.Ln, bias=eps_col[:]).then_inc(act_ln2, 1)
                            act.wait_ge(act_ln2, b + 1)
                            act.activation(rstd2[:], rstd2_ln[:], ACT.Exp, scale=-0.5).then_inc(rstd2_ready, 1)
                        if back:
                            act.wait_ge(gap_ready, e + 1)
                            act.activation(egap[:], gap[:], ACT.Exp).then_inc(egap_ready, 1)
                        if front:
                            wait(act, scattered[h], 16 * 2 * TT * it)
                            act.wait_ge(x2_ready, b + 1)
                            for i in range(2):
                                last = act.activation(rows_out[:, h, i, :, 0:D], x2[:, h], ACT.Copy)
                            last.then_inc(twin_ready, 1)
                        if back:
                            wait(act, b2_ready, e)
                            act.wait_ge(wts_t_ready, e + 1)
                            act.activation(wts_t[:], psum[0:E, 5], ACT.Copy).then_inc(wts_t_copied, 1)

                    pipeline(act, step)

                @block.vector
                def _(v):
                    def wide(t):
                        return t.rearrange("p t d -> p (t d)").rearrange("p (n f) -> p n f", n=2)

                    def step(c, it, h, front, back):
                        b, e, he = c, c - 1, 1 - h
                        norms = Steps(NORM_STEPS * b)
                        steps = Steps(ROUTE_STEPS * e)
                        if front:
                            wait(v, x2_ready, b)
                            v.wait_ge(x1bo_ready, b + 1)
                            v.wait_ge(proj_ready, b + 1)
                            v.tensor_tensor(wide(y2[:]), psum[:, 0:2], wide(x1_in[:, h]), ALU.add).then_inc(y2_ready, 1)
                            v.wait_ge(y2_ready, b + 1)
                            for t in range(TT):
                                v.bn_stats(stats2[:, t], y2[:, t]).then_inc(dve_norm, 1)
                                s = norms.next()
                            wait_alone(v, (dve_norm, s))
                            for t in range(TT):
                                last = v.bn_aggr(moments2[:, t], stats2[:, t])
                            last.then_inc(moments2_ready, 1)
                        if back:
                            v.wait_ge(logits_z_ready, e + 1)
                            v.tensor_tensor(logits[:], psum[:, 4, 0:TT * E].rearrange("p (t e) -> p t e", t=TT),
                                            router_b[:].rearrange("p (o e) -> p o e", o=1).to_broadcast([P, TT, E]),
                                            ALU.add).then_inc(logits_ready, 1)
                            wait_alone(v, (logits_ready, e + 1))
                            for t in range(TT):
                                v.max(top8[:, t], logits[:, t]).then_inc(dve_route, 1)
                                s = steps.next()
                            wait_alone(v, (dve_route, s))
                            for t in range(TT):
                                v.max_index(top8_at[:, t], top8[:, t], logits[:, t]).then_inc(dve_route, 1)
                                s_at = steps.next()
                            v.tensor_tensor(gap[:], top8[:, :, 1], top8[:, :, 0], ALU.subtract).then_inc(gap_ready, 1)
                        if front:
                            wait(v, twin_ready, b - 1)
                            v.wait_ge(moments2_ready, b + 1)
                            v.wait_ge(rstd2_ready, b + 1)
                            for t in range(TT):
                                last = v.tensor_scalar(x2[:, h, t], y2[:, t], moments2[:, t, 0:1],
                                                       rstd2[:, t:t + 1], ALU.subtract, ALU.mult)
                            last.then_inc(x2_ready, 1)
                        if back:
                            v.wait_ge(dve_route, s_at)
                            v.tensor_copy(chosen[:], top8_at[:, :, 0:2]).then_inc(dve_route, 1)
                            s = steps.next()
                            v.wait_ge(egap_ready, e + 1)
                            v.tensor_scalar(den[:], egap[:], 1.0, None, ALU.add).then_inc(dve_route, 1)
                            s1 = steps.next()
                            v.wait_ge(dve_route, s)
                            for i in range(2):
                                v.tensor_tensor(onehot[:, i],
                                                iota8[:].rearrange("p (o e) -> p o e", o=1).to_broadcast([P, TT, E]),
                                                chosen[:, :, i:i + 1].to_broadcast([P, TT, E]), ALU.is_equal) \
                                    .then_inc(dve_route, 1)
                                s2 = steps.next()
                            v.wait_ge(dve_route, s2)
                            v.tensor_tensor(mask[:], onehot[:, 0], onehot[:, 1], ALU.add).then_inc(mask_ready, 1)
                            v.wait_ge(dve_route, s1)
                            v.reciprocal(w01[:, 0], den[:]).then_inc(dve_route, 1)
                            s = steps.next()
                            v.wait_ge(dve_route, s)
                            v.tensor_tensor(w01[:, 1], w01[:, 0], egap[:], ALU.mult).then_inc(dve_route, 1)
                            s = steps.next()
                            v.wait_ge(dve_route, s)
                            wait(v, scattered[he], 16 * 2 * TT * (it - he))
                            v.tensor_copy(rows_out[:, he, :, :, AT_WEIGHT], w01[:])
                            for i in range(2):
                                v.tensor_tensor(weighted[:, i], onehot[:, i],
                                                w01[:, i].rearrange("p (t o) -> p t o", o=1).to_broadcast([P, TT, E]),
                                                ALU.mult).then_inc(dve_route, 1)
                                s = steps.next()
                            v.wait_ge(dve_route, s)
                            v.tensor_tensor(wts[:], weighted[:, 0], weighted[:, 1], ALU.add).then_inc(wts_ready, 1)
                            v.wait_ge(ranks_ready, e + 1)
                            for t in range(TT):
                                v.tensor_tensor(slot_at[:, t + 1], slot_at[:, t],
                                                psum[:, 4, 128 + t * E:128 + (t + 1) * E], ALU.add).then_inc(dve_route, 1)
                                s = steps.next()
                                v.wait_ge(dve_route, s)
                            v.tensor_tensor(slot_of[:], slot_at[:, 0:TT],
                                            psum[:, 4, 64:64 + TT * E].rearrange("p (t e) -> p t e", t=TT), ALU.add) \
                                .then_inc(dve_route, 1)
                            s = steps.next()
                            v.wait_ge(dve_route, s)
                            v.tensor_copy(slot_at[:, 0], slot_at[:, TT]).then_inc(dve_route, 1)
                            steps.next()
                            for i in range(2):
                                last = v.tensor_tensor(slot_own[:, i], onehot[:, i], slot_of[:], ALU.mult)
                            last.then_inc(dve_route, 1)
                            s = steps.next()
                            v.wait_ge(dve_route, s)
                            v.tensor_reduce(slot_f[:], slot_own[:].rearrange("p i t e -> p (i t) e"), AX_X, ALU.add) \
                                .then_inc(dve_route, 1)
                            s = steps.next()
                            v.wait_ge(dve_route, s)
                            v.tensor_copy(slot_u[:, he], slot_f[:]).then_inc(slots_ready, 1)
                            v.wait_ge(b2_ready, e + 1)
                            wait(v, x2b_stored, 16 * e)
                            v.tensor_tensor(x2b[:], psum[:, 6:8].rearrange("p n (t d) -> p (n t) d", t=2),
                                            x2[:, he], ALU.add).then_inc(acc_ready, 1)
                            assert steps.n == ROUTE_STEPS, steps.n

                    v.memset(pad_row[:], 0.0).then_inc(pads_made, 1)
                    v.tensor_copy(slot_at[:, 0], region_at[:])
                    v.wait_ge(pads_made, 1)
                    v.memset(pad_row[:, AT_DEST:AT_DEST + 1], float(NO_DEST)).then_inc(pads_made, 1)
                    pipeline(v, step)

                    plans = Steps(0)

                    def planned(last):
                        last.then_inc(plan, 1)
                        v.wait_ge(plan, plans.next())

                    planned(v.tensor_tensor(pad_f[:], slot_at[:, 0], own_row[:].to_broadcast([P, E]), ALU.add))
                    v.tensor_copy(pad_u[:], pad_f[:]).then_inc(pads_ready, 1)
                    planned(v.tensor_tensor(n_rows[:], slot_at[0:1, 0], region_at[0:1], ALU.subtract))
                    planned(v.tensor_scalar(n_rows[:], n_rows[:], (P - 1) / 2, 1.0 / P, ALU.add, ALU.mult))
                    planned(v.tensor_scalar(n_rows[:], n_rows[:], ROUND, None, ALU.add))
                    planned(v.tensor_scalar(n_tiles[:], n_rows[:], -ROUND, None, ALU.add))
                    planned(v.tensor_tensor_scan(ends[:], n_tiles[:], n_tiles[:], 0.0, ALU.add, ALU.bypass))
                    planned(v.tensor_scalar(skip[:], n_tiles[:], -float(P), float(REGION), ALU.mult, ALU.add))
                    each = [1, TILES + 1, E]
                    planned(v.tensor_tensor(past[:], ends[:].rearrange("p (o e) -> p o e", o=1).to_broadcast(each),
                                            tile_no[:].rearrange("p (j o) -> p j o", o=1).to_broadcast(each), ALU.is_le))
                    planned(v.tensor_tensor(past_skip[:], past[:],
                                            skip[:].rearrange("p (o e) -> p o e", o=1).to_broadcast(each), ALU.mult))
                    v.tensor_reduce(expert_f[:], past[:], AX_X, ALU.add)
                    planned(v.tensor_reduce(row_f[:], past_skip[:], AX_X, ALU.add))
                    planned(v.scalar_tensor_tensor(row_g[:], tile_no[:], float(P), row_f[:], ALU.mult, ALU.add))
                    v.tensor_scalar(tile_row[:], row_g[:], float(NO_TILE), None, ALU.min)
                    v.tensor_scalar(tile_expert[:], expert_f[:], float(E - 1), None, ALU.min)

        with ExitStack() as ctx:
            sb = tensors(ctx)
            rows_in = sb("rows_in", [P, 2, ROW])
            xst = sb("xst", [P, 2, C, P])
            dest = sb("dest", [P, 2, 1], U32)
            weight = sb("weight", [P, 2, 1])
            w1 = sb("w1", [P, 2, C, HID])
            w2 = sb("w2", [P, 2, HC, D])
            b1 = sb("b1", [P, 2, HC])
            hid = sb("hid", [P, 2, HC, P])
            y_out = sb("y_out", [P, 2, D])
            rows_loaded = (sem("rows_loaded0"), sem("rows_loaded1"))
            y_scattered = (sem("y_scattered0"), sem("y_scattered1"))
            xs_t_ready, xst_copied, w1_ready, w2_ready, mm1_done, h_ready, mm2_done, y_scaled = (sem(n) for n in (
                "xs_t_ready", "xst_copied", "w1_ready", "w2_ready", "mm1_done", "h_ready", "mm2_done", "y_scaled"))

            with nc.Block() as block:
                @block.sync
                def _(sp):
                    def load(j, n, h):
                        row = sp.value_load(tile_row[0:1, j], min_val=0, max_val=NO_TILE)
                        sp.dma_start(rows_in[:, h], xs[bass.ds(row, P)]).then_inc(rows_loaded[h], 16)

                    load(slice(0, 1), 0, 0)
                    with sp.Fori(0, TILES // 2) as it:
                        for h in range(2):
                            n = 2 * it + h + 1
                            sp.wait_ge(xst_copied, n)
                            load(bass.ds(n, 1), n, 1 - h)

                @block.tensor
                def _(pe):
                    def turn(half, count):
                        pe.wait_ge(rows_loaded[half], count)
                        for k in range(C):
                            last = pe.transpose(psum[:, half, k * P:(k + 1) * P],
                                                rows_in[:, half, k * P:(k + 1) * P], ident[:])
                        last.then_inc(xs_t_ready, 1)

                    opened(pe, mm1_done, mm2_done)
                    turn(0, 16)
                    with pe.Fori(0, TILES // 2) as it:
                        for h in range(2):
                            n = 2 * it + h
                            pe.wait_ge(xst_copied, n + 2)
                            turn(1 - h, 16 * (it + 1 + h))
                            pe.wait_ge(w1_ready, n + 1)
                            for c in range(HC):
                                for k in range(C):
                                    last = pe.matmul(psum[:, 2 + 2 * h + c // 4, (c % 4) * P:(c % 4 + 1) * P],
                                                     w1[:, h, k, c * P:(c + 1) * P], xst[:, h, k, :],
                                                     start=k == 0, stop=k == C - 1)
                                if c % 4 == 3:
                                    last.then_inc(mm1_done, 1)
                            pe.wait_ge(w2_ready, n + 1)
                            pe.wait_ge(y_scaled, n + OPEN)
                            for c in range(HC):
                                pe.wait_ge(h_ready, HC * n + c + 1)
                                last = pe.matmul(psum[:, 6 + h, 0:D], hid[:, h, c, :], w2[:, h, c, :],
                                                 start=c == 0, stop=c == HC - 1)
                            last.then_inc(mm2_done, 1)

                @block.scalar
                def _(act):
                    with act.Fori(0, TILES // 2) as it:
                        for h in range(2):
                            n = 2 * it + h
                            if h:
                                act.wait_ge(mm2_done, n - 1 + OPEN)
                            else:
                                act.wait_ge(mm2_done, n + OPEN)
                            for c in range(HC):
                                act.wait_ge(mm1_done, HC // 4 * n + c // 4 + 1 + OPEN)
                                act.activation(hid[:, h, c], psum[:, 2 + 2 * h + c // 4, (c % 4) * P:(c % 4 + 1) * P],
                                               ACT.Relu, bias=b1[:, h, c:c + 1]).then_inc(h_ready, 1)

                @block.gpsimd
                def _(pool):
                    with pool.Fori(0, TILES // 2) as it:
                        for h in range(2):
                            n = 2 * it + h
                            wait_alone(pool, (y_scaled, n + 2 + OPEN))
                            pool.indirect_dma_start(y_all, bass.IndirectOffsetOnAxis(dest[:, h, :], 0), y_out[:, h], None,
                                                    bounds_check=2 * TOKENS - 1, oob_is_err=False) \
                                .then_inc(y_scattered[h], 16)
                    for h in range(2):
                        pool.wait_ge(y_scattered[h], 16 * TILES // 2)

                @block.vector
                def _(v):
                    def weights(j, half):
                        e = v.value_load(tile_expert[0:1, j], min_val=0, max_val=E - 1)
                        at = bass.ds(e, 1)
                        v.tensor_copy(b1[:, half], b1_cols[:, at, :].rearrange("p o c -> p (o c)"))
                        v.tensor_copy(w1[:, half], w1_all[:, at].rearrange("p o c h -> p (o c) h")).then_inc(w1_ready, 1)
                        v.tensor_copy(w2[:, half], w2_all[:, at].rearrange("p o c d -> p (o c) d")).then_inc(w2_ready, 1)

                    def take_rows(half):
                        v.tensor_copy(dest[:, half], rows_in[:, half, AT_DEST:AT_DEST + 1])
                        v.tensor_copy(weight[:, half], rows_in[:, half, AT_WEIGHT:AT_WEIGHT + 1])
                        v.tensor_copy(xst[:, half].rearrange("p c t -> p (c t)"), psum[:, half, 0:C * P]) \
                            .then_inc(xst_copied, 1)

                    v.wait_ge(ffn_loaded, 32 * E)
                    opened(v, y_scaled)
                    v.sem_inc(y_scaled, 1)
                    v.sem_inc(xst_copied, 1)
                    v.wait_ge(xs_t_ready, 1)
                    take_rows(0)
                    weights(slice(0, 1), 0)
                    with v.Fori(0, TILES // 2) as it:
                        for h in range(2):
                            n = 2 * it + h
                            v.wait_ge(y_scattered[1 - h], 16 * (it + h))
                            v.wait_ge(mm1_done, HC // 4 * n + OPEN)
                            v.wait_ge(xs_t_ready, n + 2)
                            take_rows(1 - h)
                            v.wait_ge(mm2_done, n + OPEN)
                            weights(bass.ds(n + 1, 1), 1 - h)
                            v.wait_ge(y_scattered[h], 16 * it)
                            v.wait_ge(mm2_done, n + 1 + OPEN)
                            v.tensor_scalar(y_out[:, h], psum[:, 6 + h, 0:D], weight[:, h], None, ALU.mult) \
                                .then_inc(y_scaled, 1)

        with ExitStack() as ctx:
            sb = tensors(ctx)
            y_in = sb("y_in", [P, 2, 2, TT, D])
            x2_in = sb("x2_in", [P, 2, TT, D])
            y_pair = sb("y_pair", [P, TT, D])
            y3 = sb("y3", [P, 2, TT, D])
            x3 = sb("x3", [P, 2, TT, D])
            stats3 = sb("stats3", [P, TT, 6])
            moments3 = sb("moments3", [P, 2, TT, 2])
            rstd3_ln = sb("rstd3_ln", [P, 2, TT])
            rstd3 = sb("rstd3", [P, 2, TT])
            y_loaded = (sem("y_loaded0"), sem("y_loaded1"))
            out_stored = (sem("out_stored0"), sem("out_stored1"))
            pair_ready, y3_ready, stats3_ready, moments3_ready, act_ln3, rstd3_ready, out_ready = (sem(n) for n in (
                "pair_ready", "y3_ready", "stats3_ready", "moments3_ready", "act_ln3", "rstd3_ready", "out_ready"))
            with nc.Block() as block:
                @block.sync
                def _(sp):
                    def load(b, h):
                        for i in range(2):
                            sp.dma_start(y_in[:, h, i],
                                         y_all.rearrange("(i b t p) d -> i b p t d", i=2, b=B, p=P)[i, b]) \
                                .then_inc(y_loaded[h], 16)
                        sp.dma_start(x2_in[:, h], x2_all[b].rearrange("(t p) d -> p t d", p=P)) \
                            .then_inc(y_loaded[h], 16)

                    def store(b, h):
                        sp.wait_ge(out_ready, b + 1)
                        sp.dma_start(out[b].rearrange("(t p) d -> p t d", p=P), x3[:, h]).then_inc(out_stored[h], 16)

                    opened(sp, *out_stored)
                    for h in range(2):
                        load(h, h)
                    with sp.Fori(1, B // 2) as it:
                        for h in range(2):
                            b = 2 * it + h
                            sp.wait_ge(pair_ready, b - 1 + OPEN)
                            sp.wait_ge(y3_ready, b - 1 + OPEN)
                            load(b, h)
                            store(b - 2, h)
                    for h in range(2):
                        store(B - 2 + h, h)
                    for h in range(2):
                        sp.wait_ge(out_stored[h], 16 * B // 2 + OPEN)

                @block.gpsimd
                def _(pool):
                    opened(pool, pair_ready)
                    with pool.Fori(0, B // 2) as it:
                        for h in range(2):
                            b = 2 * it + h
                            pool.wait_ge(y3_ready, b + OPEN)
                            pool.wait_ge(y_loaded[h], 48 * (it + 1))
                            pool.tensor_tensor(y_pair[:], y_in[:, h, 0], y_in[:, h, 1], ALU.add).then_inc(pair_ready, 1)

                @block.vector
                def _(v):
                    opened(v, y3_ready)

                    def sums(b, it, h):
                        if it is not None:
                            v.wait_ge(out_ready, b - 1)
                        v.wait_ge(pair_ready, b + 1 + OPEN)
                        v.tensor_tensor(y3[:, h], x2_in[:, h], y_pair[:], ALU.add).then_inc(y3_ready, 1)
                        wait_alone(v, (y3_ready, b + 1 + OPEN))
                        for t in range(TT):
                            last = v.bn_stats(stats3[:, t], y3[:, h, t])
                        last.then_inc(stats3_ready, 1)
                        wait_alone(v, (stats3_ready, b + 1))
                        for t in range(TT):
                            last = v.bn_aggr(moments3[:, h, t], stats3[:, t])
                        last.then_inc(moments3_ready, 1)

                    def norm(b, it, h):
                        v.wait_ge(out_stored[h], 16 * it + OPEN)
                        v.wait_ge(moments3_ready, b + 1)
                        v.wait_ge(rstd3_ready, b + 1)
                        for t in range(TT):
                            last = v.tensor_scalar(x3[:, h, t], y3[:, h, t], moments3[:, h, t, 0:1],
                                                   rstd3[:, h, t:t + 1], ALU.subtract, ALU.mult)
                        last.then_inc(out_ready, 1)

                    sums(0, None, 0)
                    sums(1, None, 1)
                    norm(0, 0, 0)
                    with v.Fori(1, B // 2) as it:
                        for h in range(2):
                            sums(2 * it + h, it, h)
                            norm(2 * it + h - 1, it - 1 + h, 1 - h)
                    norm(B - 1, B // 2 - 1, 1)

                @block.scalar
                def _(act):
                    with act.Fori(0, B // 2) as it:
                        for h in range(2):
                            b = 2 * it + h
                            act.wait_ge(moments3_ready, b + 1)
                            act.activation(rstd3_ln[:, h], moments3[:, h, :, 1], ACT.Ln, bias=eps_col[:]).then_inc(act_ln3, 1)
                            act.wait_ge(act_ln3, b + 1)
                            act.activation(rstd3[:, h], rstd3_ln[:, h], ACT.Exp, scale=-0.5).then_inc(rstd3_ready, 1)


def _columns(*vectors):
    import numpy as np
    return np.ascontiguousarray(np.concatenate([v.reshape(-1, P).T for v in vectors], axis=1))


def kernel(**inputs):
    import numpy as np
    import concourse.bacc as bacc
    from concourse.bass_utils import run_bass_kernel_spmd

    w = {k: np.asarray(v) for k, v in inputs.items()}
    x, ctx = w["x"], w["ctx_1024"]
    B, L, D = x.shape
    S = ctx.shape[1]
    half = -(-S // (2 * P)) * P
    m, t, f = "L0_attn_", "L0_xattn_", "L0_ffn_"
    one = lambda v, i=0: np.repeat(v[i:i + 1], P)
    ctx_p = np.zeros((B, 2 * half, D), ctx.dtype)
    ctx_p[:, :S] = ctx
    wo = w[t + "Wo"].reshape(4, 4, D // 16, D)
    wo_p = np.zeros((4, 4, 32, D), wo.dtype)
    wo_p[:, :, :D // 16] = wo
    E, TT = w[f + "W1"].shape[0], L // P
    tokens = np.arange(B * L, dtype=np.float32).reshape(B * TT, P).T
    arrays = {
        "before": np.triu(np.ones((P, P), np.float32), 1),
        "dest_ids": np.stack([tokens, tokens + B * L], axis=1),
        "region_at": np.tile(np.arange(E, dtype=np.float32) * (B * L + P), (P, 1)),
        "own_row": np.arange(P, dtype=np.float32)[:, None],
        "tile_no": np.arange(2 * B * TT + E + 1, dtype=np.float32)[None],
        "x": x,
        "xT": x.transpose(0, 2, 1).reshape(B, D // P, P, L),
        "ctxT": ctx_p.reshape(2 * B, half, D).transpose(0, 2, 1).reshape(2 * B, D // P, P, half),
        "posT": w[m + "pos_phases"][:L].T,
        "cols": _columns(w[m + "bpv"], w[m + "bk"], w[m + "bkv"], w[m + "bg1"], w[m + "ln_g"], w[m + "ln_b"],
                         w[t + "bq"], w[t + "bk"], w[m + "bb1"], one(w[m + "bg2"]), one(w[m + "bb2"], 0),
                         one(w[m + "bb2"], 1), w[m + "Wg2"], w[m + "Wb2"].T),
        "rows": np.stack([w[m + "bo"], w[t + "bo"], w[t + "bv"], w[t + "bv"]]),
        "Wpv": w[m + "Wpv"], "Wk": w[m + "Wk"], "Wkv": w[m + "Wkv"], "Wg1": w[m + "Wg1"],
        "Wb1": w[m + "Wb1"], "Wo": w[m + "Wo"],
        "xWq": w[t + "Wq"], "xWk": w[t + "Wk"], "xWv": w[t + "Wv"], "xWo": wo_p.reshape(4, P, D),
        "Wr": w[f + "Wr"], "br": w[f + "br"], "W1": w[f + "W1"], "W2": w[f + "W2"],
        "b1T": w[f + "b1"].reshape(w[f + "b1"].shape[0], -1, P).transpose(2, 0, 1), "b2": w[f + "b2"],
    }
    arrays = {f"in_{n}": np.ascontiguousarray(v) for n, v in arrays.items()}
    nc = bacc.Bacc("TRN2", target_bir_lowering=False, num_devices=1)
    a = {n[3:]: nc.dram_tensor(n, v.shape, mybir.dt.from_np(v.dtype), kind="ExternalInput").ap()
         for n, v in arrays.items()}
    a["S_REAL"] = S
    out = nc.dram_tensor("out", [B, L, D], F32, kind="ExternalOutput").ap()
    decoder_layer(nc, a, out)
    r = run_bass_kernel_spmd(nc, [arrays], core_ids=[0])
    return r.results[0]["out"]
```
